# Optimizing a Trainium2 kernel written in Bass

```python
import numpy as np
import jax
import jax.numpy as jnp

def _softmax(x, axis=-1):
    return jax.nn.softmax(x, axis=axis)

def _gelu(x):
    return jax.nn.gelu(x, approximate=True)

def _silu(x):
    return jax.nn.silu(x)

def _sigmoid(x):
    return jax.nn.sigmoid(x)

def _layernorm(x, axis=-1, eps=1e-05):
    m = jnp.mean(x, axis=axis, keepdims=True)
    v = jnp.var(x, axis=axis, keepdims=True)
    return (x - m) / jnp.sqrt(v + eps)

def _scatter_add(tgt, idx, src, axis=0):
    return tgt.at[idx].add(src)

def _segment_sum(src, seg, n):
    return jax.ops.segment_sum(src, seg, n)
kernel_name = 'mk_hybrid_d1_jaxref_r8_85569f'

def setup_inputs(seed: int=0):
    np.random.seed(seed)
    _w = jnp.asarray

    def _L0_attn_a_setup():
        import jax, jax.numpy as jnp
        import numpy as np
        D_MODEL = 512
        D_LATENT = 64
        NUM_HEADS = 32
        HEAD_DIM = D_MODEL // NUM_HEADS
        ROPE_THETA = 10000.0
        BATCH, SEQ = (2, 256)

        def _rotate_half(x):
            x1, x2 = jnp.split(x, 2, axis=-1)
            return jnp.concatenate([-x2, x1], axis=-1)

        def _rope_cos_sin(positions, head_dim, theta, dtype):
            inv_freq = 1.0 / theta ** (jnp.arange(0, head_dim, 2, dtype=jnp.float32) / head_dim)
            freqs = positions.astype(jnp.float32)[..., None] * inv_freq
            emb = jnp.concatenate([freqs, freqs], axis=-1)
            return (jnp.cos(emb)[:, :, None, :].astype(dtype), jnp.sin(emb)[:, :, None, :].astype(dtype))
        key = jax.random.key(seed)
        ks = jax.random.split(key, 6)
        s = 0.02
        return {'hidden_states': jax.random.normal(ks[0], (BATCH, SEQ, D_MODEL), jnp.float32), 'Wq': jax.random.normal(ks[1], (D_MODEL, NUM_HEADS * HEAD_DIM), jnp.float32) * s, 'Wc': jax.random.normal(ks[2], (D_MODEL, D_LATENT), jnp.float32) * s, 'Wk': jax.random.normal(ks[3], (D_LATENT, NUM_HEADS * HEAD_DIM), jnp.float32) * s, 'Wv': jax.random.normal(ks[4], (D_LATENT, NUM_HEADS * HEAD_DIM), jnp.float32) * s, 'Wo': jax.random.normal(ks[5], (NUM_HEADS * HEAD_DIM, D_MODEL), jnp.float32) * s}
    _L0_attn_a_in = _L0_attn_a_setup()

    def _L0_attn_b_setup():
        import jax, jax.numpy as jnp
        import numpy as np
        import math
        HIDDEN = 512
        NUM_HEADS = 32
        HEAD_DIM = HIDDEN // NUM_HEADS
        SCALE = 1.0 / HEAD_DIM

        def _alibi_slopes(n_heads: int) -> np.ndarray:
            cp2 = 2 ** math.floor(math.log2(n_heads))
            base = 2 ** (-2 ** (-(math.log2(cp2) - 3)))
            slopes = base ** np.arange(1, cp2 + 1, dtype=np.float32)
            if cp2 != n_heads:
                extra_base = 2 ** (-2 ** (-(math.log2(2 * cp2) - 3)))
                n_rem = min(cp2, n_heads - cp2)
                extra = extra_base ** np.arange(1, 1 + 2 * n_rem, 2, dtype=np.float32)
                slopes = np.concatenate([slopes, extra])
            return slopes.astype(np.float32)
        key = jax.random.key(seed)
        k1, k2, k3, k4, k5 = jax.random.split(key, 5)
        B, S = (2, 256)
        return {'hidden_states': jax.random.normal(k1, (B, S, HIDDEN), dtype=jnp.float32), 'w_attn': jax.random.normal(k2, (HIDDEN, 3 * HIDDEN), dtype=jnp.float32) * 0.02, 'b_attn': jnp.zeros((3 * HIDDEN,), dtype=jnp.float32), 'w_proj': jax.random.normal(k3, (HIDDEN, HIDDEN), dtype=jnp.float32) * 0.02, 'b_proj': jnp.zeros((HIDDEN,), dtype=jnp.float32)}
    _L0_attn_b_in = _L0_attn_b_setup()

    def _L0_ffn_setup():
        import jax, jax.numpy as jnp
        import numpy as np
        B_, S, D_IN, D_OUT = (4, 256, 512, 512)
        N, RANK, ALPHA = (8, 16, 32)
        SCALE = ALPHA / RANK
        key = jax.random.key(seed)
        kx, ka, kb, kw, kbias = jax.random.split(key, 5)
        x = jax.random.normal(kx, (B_, S, D_IN), dtype=jnp.float32)
        lora_A = jax.random.normal(ka, (N, RANK, D_IN), dtype=jnp.float32) * (1.0 / np.sqrt(D_IN))
        lora_B = jax.random.normal(kb, (N, D_OUT, RANK), dtype=jnp.float32) * (1.0 / np.sqrt(RANK))
        W = jax.random.normal(kw, (D_OUT, D_IN), dtype=jnp.float32) * (1.0 / np.sqrt(D_IN))
        bias = jax.random.normal(kbias, (D_OUT,), dtype=jnp.float32) * 0.01
        lora_weights = jnp.full((N,), 1.0 / N, dtype=jnp.float32)
        return {'x': x, 'lora_A': lora_A, 'lora_B': lora_B, 'W': W, 'bias': bias, 'lora_weights': lora_weights}
    _L0_ffn_in = _L0_ffn_setup()
    _d = {'L0_attn_a_hidden_states': _L0_attn_a_in['hidden_states'], 'L0_attn_a_Wq': _L0_attn_a_in['Wq'], 'L0_attn_a_Wc': _L0_attn_a_in['Wc'], 'L0_attn_a_Wk': _L0_attn_a_in['Wk'], 'L0_attn_a_Wv': _L0_attn_a_in['Wv'], 'L0_attn_a_Wo': _L0_attn_a_in['Wo'], 'L0_attn_b_w_attn': _L0_attn_b_in['w_attn'], 'L0_attn_b_b_attn': _L0_attn_b_in['b_attn'], 'L0_attn_b_w_proj': _L0_attn_b_in['w_proj'], 'L0_attn_b_b_proj': _L0_attn_b_in['b_proj'], 'L0_ffn_lora_A': _L0_ffn_in['lora_A'], 'L0_ffn_lora_B': _L0_ffn_in['lora_B'], 'L0_ffn_W': _L0_ffn_in['W'], 'L0_ffn_bias': _L0_ffn_in['bias'], 'L0_ffn_lora_weights': _L0_ffn_in['lora_weights']}
    _x0 = _d['L0_attn_a_hidden_states']
    _d['L0_attn_a_hidden_states'] = jax.random.normal(jax.random.fold_in(jax.random.key(seed), 1), (2, 1024, 512), dtype=_x0.dtype)
    del _x0
    return _d

def reference(L0_attn_a_hidden_states, L0_attn_a_Wq, L0_attn_a_Wc, L0_attn_a_Wk, L0_attn_a_Wv, L0_attn_a_Wo, L0_attn_b_w_attn, L0_attn_b_b_attn, L0_attn_b_w_proj, L0_attn_b_b_proj, L0_ffn_lora_A, L0_ffn_lora_B, L0_ffn_W, L0_ffn_bias, L0_ffn_lora_weights):

    def _L0_attn_a_ref(hidden_states, Wq, Wc, Wk, Wv, Wo):
        import jax, jax.numpy as jnp
        import numpy as np
        D_MODEL = 512
        D_LATENT = 64
        NUM_HEADS = 32
        HEAD_DIM = D_MODEL // NUM_HEADS
        ROPE_THETA = 10000.0
        BATCH, SEQ = (2, 256)

        def _rotate_half(x):
            x1, x2 = jnp.split(x, 2, axis=-1)
            return jnp.concatenate([-x2, x1], axis=-1)

        def _rope_cos_sin(positions, head_dim, theta, dtype):
            inv_freq = 1.0 / theta ** (jnp.arange(0, head_dim, 2, dtype=jnp.float32) / head_dim)
            freqs = positions.astype(jnp.float32)[..., None] * inv_freq
            emb = jnp.concatenate([freqs, freqs], axis=-1)
            return (jnp.cos(emb)[:, :, None, :].astype(dtype), jnp.sin(emb)[:, :, None, :].astype(dtype))
        B, S, _ = hidden_states.shape
        H, Dh = (NUM_HEADS, HEAD_DIM)
        q = (hidden_states @ Wq).reshape(B, S, H, Dh)
        kv_latent = hidden_states @ Wc
        k = (kv_latent @ Wk).reshape(B, S, H, Dh)
        v = (kv_latent @ Wv).reshape(B, S, H, Dh)
        pos = jnp.broadcast_to(jnp.arange(S)[None, :], (B, S))
        cos, sin = _rope_cos_sin(pos, Dh, ROPE_THETA, q.dtype)
        q = q * cos + _rotate_half(q) * sin
        k = k * cos + _rotate_half(k) * sin
        scale = 1.0 / np.sqrt(Dh)
        scores = jnp.einsum('bqhd,bkhd->bhqk', q, k) * scale
        probs = jax.nn.softmax(scores, axis=-1)
        attn = jnp.einsum('bhqk,bkhd->bqhd', probs, v)
        out = attn.reshape(B, S, H * Dh) @ Wo
        return out

    def _L0_attn_b_ref(hidden_states, w_attn, b_attn, w_proj, b_proj):
        import jax, jax.numpy as jnp
        import numpy as np
        import math
        HIDDEN = 512
        NUM_HEADS = 32
        HEAD_DIM = HIDDEN // NUM_HEADS
        SCALE = 1.0 / HEAD_DIM

        def _alibi_slopes(n_heads: int) -> np.ndarray:
            cp2 = 2 ** math.floor(math.log2(n_heads))
            base = 2 ** (-2 ** (-(math.log2(cp2) - 3)))
            slopes = base ** np.arange(1, cp2 + 1, dtype=np.float32)
            if cp2 != n_heads:
                extra_base = 2 ** (-2 ** (-(math.log2(2 * cp2) - 3)))
                n_rem = min(cp2, n_heads - cp2)
                extra = extra_base ** np.arange(1, 1 + 2 * n_rem, 2, dtype=np.float32)
                slopes = np.concatenate([slopes, extra])
            return slopes.astype(np.float32)
        B, S, _ = hidden_states.shape
        H, D = (NUM_HEADS, HEAD_DIM)
        qkv = hidden_states @ w_attn + b_attn
        q, k, v = jnp.split(qkv, 3, axis=-1)
        q = q.reshape(B, S, H, D)
        k = k.reshape(B, S, H, D)
        v = v.reshape(B, S, H, D)
        scores = jnp.einsum('bqhd,bkhd->bhqk', q, k) * SCALE
        slopes = jnp.asarray(_alibi_slopes(H))
        pos = jnp.arange(S)
        rel = pos[None, :] - pos[:, None]
        bias = slopes[:, None, None] * rel[None, :, :]
        causal = rel <= 0
        scores = jnp.where(causal[None, None], scores + bias[None], -jnp.inf)
        attn = jax.nn.softmax(scores, axis=-1)
        out = jnp.einsum('bhqk,bkhd->bqhd', attn, v).reshape(B, S, HIDDEN)
        return out @ w_proj + b_proj

    def _L0_ffn_ref(x, lora_A, lora_B, W, bias, lora_weights):
        import jax, jax.numpy as jnp
        import numpy as np
        B_, S, D_IN, D_OUT = (4, 256, 512, 512)
        N, RANK, ALPHA = (8, 16, 32)
        SCALE = ALPHA / RANK
        h = jnp.einsum('bsd,nrd->nbsr', x, lora_A)
        coef = (SCALE * lora_weights)[:, None, None]
        lora_out = jnp.einsum('nbsr,nor->bso', h, lora_B * coef)
        base = jnp.einsum('bsd,od->bso', x, W) + bias
        return base + lora_out
    x = L0_attn_a_hidden_states
    x = x + _L0_attn_a_ref(_layernorm(x, axis=-1), L0_attn_a_Wq, L0_attn_a_Wc, L0_attn_a_Wk, L0_attn_a_Wv, L0_attn_a_Wo)
    x = x + _L0_ffn_ref(_layernorm(x, axis=-1), L0_ffn_lora_A, L0_ffn_lora_B, L0_ffn_W, L0_ffn_bias, L0_ffn_lora_weights)
    x = x + _L0_attn_b_ref(_layernorm(x, axis=-1), L0_attn_b_w_attn, L0_attn_b_b_attn, L0_attn_b_w_proj, L0_attn_b_b_proj)
    x = x + _L0_ffn_ref(_layernorm(x, axis=-1), L0_ffn_lora_A, L0_ffn_lora_B, L0_ffn_W, L0_ffn_bias, L0_ffn_lora_weights)
    return x

_drawn_inputs = setup_inputs


def setup_inputs(seed=0):
    import zlib

    import numpy as np

    out = dict(_drawn_inputs(seed))
    spreads = {'L0_attn_b_b_attn': (0.0, 2.0),
     'L0_attn_b_b_proj': (0.0, 0.8),
     'L0_ffn_lora_weights': (0.125, 0.6)}
    factors = {'L0_attn_a_Wq': 8.0,
     'L0_attn_a_Wc': 8.0,
     'L0_attn_a_Wk': 8.0,
     'L0_attn_a_Wv': 8.0,
     'L0_attn_a_Wo': 8.0,
     'L0_ffn_bias': 47.809,
     'L0_attn_b_w_attn': 8.0,
     'L0_attn_b_w_proj': 5.574}
    for name, (base, spread) in spreads.items():
        noise = np.random.default_rng([zlib.crc32(name.encode()), seed]).standard_normal(out[name].shape)
        drawn = base * np.exp(spread * noise) if base else spread * noise
        out[name] = jnp.asarray(drawn.astype(out[name].dtype))
    for name, factor in factors.items():
        out[name] = (out[name] * factor).astype(out[name].dtype)
    return out
```

```python
from contextlib import ExitStack

import numpy as np

import concourse.bass as bass
from concourse import mybir

ALU = mybir.AluOpType
ACT = mybir.ActivationFunctionType
AX = mybir.AxisListType
BF16 = mybir.dt.bfloat16
F32 = mybir.dt.float32

P = 128
B, S, D = 2, 1024, 512
H, DH = 32, 16
LATENT = 64
RANKS = 128
T = B * S
TILES = T // P
CHUNK = 512
NC = T // CHUNK
TPC = CHUNK // P
KC = D // P
GH = 4
GPB = H // GH
NG = B * GPB
GD = GH * DH
VW = 32
EPS = 1e-5
LORA_SCALE = 2.0
NEG = -1e30
LOWEST = -3e38
BANKS = 8
Q_PARTS = (0, 0, 0, 1, 1, 2)
K_PARTS = (0, 1, 2, 0, 1, 0)
SROWS = DH * len(Q_PARTS)
LEAD = 2
SLOTS = 3
PEELED_FRONT = 1
LOOPED = 12


def wait_past(e, sem, value):
    if not isinstance(value, int) or value > 0:
        e.wait_ge(sem, value)


def attention(nc, tag, causal, scale, consts, q_d, k_d, v_d, o_d, z_d, alibi_d):
    units = [(qh, kt) for qh in range(2) for kt in range((4 * (qh + 1)) if causal else 8)]
    NU = len(units)
    pieces = []
    for h in range(GH):
        for qt in range(8):
            for half in range(2):
                n = min(CHUNK, P * (qt + 1) - CHUNK * half) if causal else CHUNK
                if n > 0:
                    pieces.append((h, qt, half, n))
    NPC = len(pieces)
    PPU = NPC // NU
    al = 3 if causal else 0
    crow = SROWS + al
    rows = crow + 3
    TPU = 2
    NT = NU * TPU
    NP = 4
    MXB = 3
    LOAD = 16 * 2 * len(Q_PARTS) + (16 if causal else 0)
    SETS = SLOTS * (2 if causal else 1) + 1
    STORES = 16 * (GH + 1)
    SHIFT = 16 * 3 * 4
    first_of = {qh: min(u for u in range(NU) if units[u][0] == qh) for qh in range(2)}
    last_of = {qh: max(u for u in range(NU) if units[u][0] == qh) for qh in range(2)}
    LINKS = 5

    with ExitStack() as ctx:
        def sb(name, shape, dt):
            return ctx.enter_context(nc.sbuf_tensor(f"{tag}_{name}", shape, dt))

        def sem(name):
            return ctx.enter_context(nc.semaphore(f"{tag}_{name}"))

        q_sb = [sb(f"q{j}", [rows, GH * S], BF16) for j in range(SLOTS)]
        k_sb = [sb(f"k{j}", [rows, GH * S], BF16) for j in range(SLOTS)]
        v_sb = [sb(f"v{j}", [P, 8, GH * VW], F32) for j in range(SLOTS)]
        p_sb = sb("p", [P, NP, 2, CHUNK], F32)
        o_sb = sb("o", [P, 2, CHUNK], F32)
        mxp = sb("mxp", [P, GH * 8, 2], F32)
        negm = sb("negm", [P, GH * 8], F32)
        rest = sb("rest", [P, GH * 8], F32)
        cparts = sb("cparts", [P, 3, GH * 8], BF16)
        cturned = sb("cturned", [P, 3, GH * 8], BF16)
        ps_s = ctx.enter_context(nc.psum_tensor(f"{tag}_ps_s", [P, 4, CHUNK], F32))
        ps_m = ctx.enter_context(nc.psum_tensor(f"{tag}_ps_m", [P, MXB, CHUNK], F32))
        ps_o = ctx.enter_context(nc.psum_tensor(f"{tag}_ps_o", [P, CHUNK], F32))

        rows_set = sem("rows_set")
        qk_loaded = [sem(f"qk_loaded{j}") for j in range(SLOTS)]
        v_loaded = [sem(f"v_loaded{j}") for j in range(SLOTS)]
        piece_ready = sem("piece_ready")
        piece_taken = sem("piece_taken")
        chain = sem("chain")
        shift_ready = sem("shift_ready")
        shift_loaded = sem("shift_loaded")
        score_ready = sem("score_ready")
        exp_done = sem("exp_done")
        pv_done = sem("pv_done")
        out_copied = sem("out_copied")
        out_stored = [sem(f"out_stored{qh}") for qh in range(2)]

        block = ctx.enter_context(nc.Block())

        @block.sync
        def _(sp):
            def load(g, j):
                for r, part in enumerate(Q_PARTS):
                    sp.dma_start(
                        q_sb[j][DH * r:DH * (r + 1), :].rearrange("d (h t) -> d h t", h=GH),
                        q_d[part, bass.ds(g * GD, GD), :].rearrange("(h d) t -> d h t", d=DH),
                    ).then_inc(qk_loaded[j], 16)
                for r, part in enumerate(K_PARTS):
                    sp.dma_start(
                        k_sb[j][DH * r:DH * (r + 1), :].rearrange("d (h t) -> d h t", h=GH),
                        k_d[part, bass.ds(g * GD, GD), :].rearrange("(h d) t -> d h t", d=DH),
                    ).then_inc(qk_loaded[j], 16)
                if causal:
                    sp.dma_start(k_sb[j][SROWS:crow, :], alibi_d[bass.ds(g * al, al), :]).then_inc(qk_loaded[j], 16)
                sp.dma_start(v_sb[j][:, :, :], v_d[bass.ds(g * P, P), :].rearrange("p (k c) -> p k c", k=8)
                             ).then_inc(v_loaded[j], 16)

            def shift_rows(g, j):
                sp.wait_ge(shift_ready, g + 1)
                for w in range(3):
                    row = q_sb[j][crow + w:crow + w + 1, :].rearrange("w (n i c) -> w n i c", n=GH * 8, i=4)
                    for i in range(4):
                        sp.dma_start(row[:, :, i, :], cturned[32 * i:32 * (i + 1), w, :]).then_inc(shift_loaded, 16)

            def store(s, qh):
                sp.wait_ge(out_copied, 2 * s + qh + 1)
                half = slice(qh * CHUNK, (qh + 1) * CHUNK)
                for h in range(GH):
                    sp.dma_start(o_d[bass.ds(s * GD + h * DH, DH), half],
                                 o_sb[VW * h:VW * h + DH, qh, :]).then_inc(out_stored[qh], 16)
                sp.dma_start(z_d[qh, bass.ds(s * GH, GH), :], o_sb[DH:P:VW, qh, :]).then_inc(out_stored[qh], 16)

            def step(s, j, ahead=True, loads=True):
                store(s, 0)
                if ahead:
                    shift_rows(s + 1, (j + 1) % SLOTS)
                store(s, 1)
                if loads:
                    sp.wait_ge(pv_done, NU * (s + 1))
                    load(s + SLOTS, j)

            if causal:
                sp.wait_ge(rows_set, SETS)
            for g in range(SLOTS):
                load(g, g)
            shift_rows(0, 0)
            step(0, 0)
            with sp.Fori(0, LOOPED // SLOTS) as turn:
                for n in range(SLOTS):
                    step(turn * SLOTS + (n + PEELED_FRONT), (n + PEELED_FRONT) % SLOTS)
            for s in range(PEELED_FRONT + LOOPED, NG):
                step(s, s % SLOTS, ahead=s + 1 < NG, loads=s + SLOTS < NG)
            for qh in range(2):
                sp.wait_ge(out_stored[qh], STORES * NG)

        @block.tensor
        def _(pe):
            def loads(turn, n):
                return n // SLOTS + 1 if turn is None else turn + (n // SLOTS + 1)

            def maxima(g, j, lo, hi, turn, n):
                for i in range(lo, hi):
                    h, qt, half, keys = pieces[i]
                    bank = (NPC * j + i) % MXB
                    if i == 0:
                        pe.wait_ge(qk_loaded[j], loads(turn, n) * LOAD)
                    wait_past(pe, piece_taken, g * NPC + (i - MXB + 1))
                    q = q_sb[j][0:crow, h * S + qt * P:h * S + (qt + 1) * P]
                    k = k_sb[j][0:crow, h * S + half * CHUNK:h * S + half * CHUNK + keys]
                    diagonal = causal and half == qt // 4
                    if diagonal:
                        pe.matmul(ps_m[:, bank, keys - P:keys], consts["ident_bf"][:, :],
                                  consts["mask_qk"][:, :], start=True, stop=False, skip_group_check=True)
                    pe.matmul(ps_m[:, bank, 0:keys], q, k, start=not diagonal, stop=True,
                              skip_group_check=diagonal).then_inc(piece_ready, 1)

            def scores(s, j, u, pair):
                qh, kt = units[u]
                off = max(0, P * kt - CHUNK * qh) if causal else 0
                diagonal = causal and P * kt >= CHUNK * qh
                if u == 0 and pair == 0:
                    pe.wait_ge(shift_loaded, s * SHIFT + SHIFT)
                wait_past(pe, exp_done, s * NT + (2 * u + pair - 1))
                for h in (2 * pair, 2 * pair + 1):
                    k = k_sb[j][0:rows, h * S + kt * P:h * S + (kt + 1) * P]
                    q = q_sb[j][0:rows, h * S + qh * CHUNK + off:h * S + (qh + 1) * CHUNK]
                    if diagonal:
                        pe.matmul(ps_s[:, h, off:off + P], consts["ident_bf"][:, :],
                                  consts["mask_kq"][:, :], start=True, stop=False, skip_group_check=True)
                    mm = pe.matmul(ps_s[:, h, off:CHUNK], k, q, start=not diagonal, stop=True,
                                   skip_group_check=diagonal)
                mm.then_inc(score_ready, 1)

            def values(s, j, u, turn, n):
                qh, kt = units[u]
                off = max(0, P * kt - CHUNK * qh) if causal else 0
                pe.wait_ge(exp_done, s * NT + (2 * u + 2))
                if u == 0:
                    pe.wait_ge(v_loaded[j], loads(turn, n) * 16)
                if u == first_of[qh]:
                    wait_past(pe, out_copied, 2 * s + qh)
                for h in range(GH):
                    mm = pe.matmul(ps_o[VW * h:VW * (h + 1), off:CHUNK], v_sb[j][:, kt, VW * h:VW * (h + 1)],
                                   p_sb[:, (2 * u + h // 2) % NP, h % 2, off:CHUNK],
                                   start=(u == first_of[qh]), stop=(u == last_of[qh]))
                mm.then_inc(pv_done, 1)

            def step(s, j, turn=None, n=0):
                for u in range(NU):
                    past, share = (u + LEAD) // NU + 1, (u + LEAD) % NU * PPU

                    def ahead(lo, hi):
                        if turn is not None or s + past < NG:
                            maxima(s + past, (j + past) % SLOTS, share + lo, share + hi, turn, n + past)
                    scores(s, j, u, 0)
                    ahead(0, PPU // 4)
                    scores(s, j, u, 1)
                    ahead(PPU // 4, PPU // 2)
                    if u:
                        values(s, j, u - 1, turn, n)
                    ahead(PPU // 2, PPU)
                values(s, j, NU - 1, turn, n)

            pe.wait_ge(rows_set, SETS)
            maxima(0, 0, 0, NPC, None, 0)
            maxima(1, 1, 0, PPU * LEAD, None, 1)
            step(0, 0)
            with pe.Fori(0, LOOPED // SLOTS) as turn:
                for n in range(PEELED_FRONT, PEELED_FRONT + SLOTS):
                    step(turn * SLOTS + n, n % SLOTS, turn, n)
            for s in range(PEELED_FRONT + LOOPED, NG):
                step(s, s % SLOTS, None, s)

        @block.scalar
        def _(act):
            def copy_out(s, qh):
                act.wait_ge(pv_done, s * NU + (last_of[qh] + 1))
                wait_past(act, out_stored[qh], s * STORES)
                act.activation(o_sb[:, qh, :], ps_o[:, :], ACT.Copy).then_inc(out_copied, 1)

            def step(s):
                for u, (qh, kt) in enumerate(units):
                    off = max(0, P * kt - CHUNK * qh) if causal else 0
                    wait_past(act, pv_done, s * NU + (u - 1))
                    for pair in range(2):
                        act.wait_ge(score_ready, s * NT + (2 * u + pair + 1))
                        act.activation(p_sb[:, (2 * u + pair) % NP, :, off:CHUNK],
                                       ps_s[:, 2 * pair:2 * pair + 2, off:CHUNK], ACT.Exp,
                                       scale=scale).then_inc(exp_done, 1)
                    if u == last_of[0] + 1:
                        copy_out(s, 0)
                copy_out(s, 1)

            step(0)
            with act.Fori(0, LOOPED) as turn:
                step(turn + PEELED_FRONT)
            for s in range(PEELED_FRONT + LOOPED, NG):
                step(s)

        @block.vector
        def _(dve):
            def reduce_piece(g, j, i):
                h, qt, half, keys = pieces[i]
                dve.wait_ge(piece_ready, g * NPC + (i + 1))
                dve.tensor_reduce(mxp[:, 8 * h + qt, half:half + 1], ps_m[:, (NPC * j + i) % MXB, 0:keys],
                                  AX.X, ALU.max).then_inc(piece_taken, 1)

            def shift(g):
                def link(ins, n):
                    ins.then_inc(chain, 1)
                    dve.wait_ge(chain, g * LINKS + (n + 1))

                dve.wait_ge(piece_taken, g * NPC + NPC)
                wait_past(dve, shift_ready, g)
                link(dve.tensor_reduce(negm[:, :], mxp[:, :, :], AX.X, ALU.max, negate=True), 0)
                link(dve.tensor_copy(cparts[:, 0, :], negm[:, :]), 1)
                link(dve.tensor_tensor(rest[:, :], negm[:, :], cparts[:, 0, :], ALU.subtract), 2)
                link(dve.tensor_copy(cparts[:, 1, :], rest[:, :]), 3)
                link(dve.tensor_tensor(cparts[:, 2, :], rest[:, :], cparts[:, 1, :], ALU.subtract), 4)
                wait_past(dve, shift_loaded, g * SHIFT)
                dve.transpose(cturned[:, :, :], cparts[:, :, :]).then_inc(shift_ready, 1)

            def step(s, j, ahead=True, beyond=True):
                if ahead:
                    for i in range(PPU * LEAD, NPC):
                        reduce_piece(s + 1, (j + 1) % SLOTS, i)
                    shift(s + 1)
                if beyond:
                    for i in range(PPU * LEAD):
                        reduce_piece(s + 2, (j + 2) % SLOTS, i)

            for j in range(SLOTS):
                dve.memset(k_sb[j][SROWS:rows, :], 1.0).then_inc(rows_set, 1)
                if causal:
                    dve.memset(q_sb[j][SROWS:rows, :], 1.0).then_inc(rows_set, 1)
            dve.memset(mxp[:, :, :], LOWEST).then_inc(rows_set, 1)
            dve.wait_ge(rows_set, SETS)
            for i in range(NPC):
                reduce_piece(0, 0, i)
            shift(0)
            for i in range(PPU * LEAD):
                reduce_piece(1, 1, i)
            step(0, 0)
            with dve.Fori(0, LOOPED // SLOTS) as turn:
                for n in range(SLOTS):
                    step(turn * SLOTS + (n + PEELED_FRONT), (n + PEELED_FRONT) % SLOTS)
            for s in range(PEELED_FRONT + LOOPED, NG):
                step(s, s % SLOTS, ahead=s + 1 < NG, beyond=s + 2 < NG)


def bank_plan(tasks):
    return {task: (n % BANKS, n // BANKS) for n, task in enumerate(tasks)}


class Banks:

    def __init__(self, nc, ctx, tag, tasks):
        self.place = bank_plan(tasks)
        assert len(self.place) == len(tasks)
        self.ps = ctx.enter_context(nc.psum_tensor(f"{tag}_ps", [P, BANKS, CHUNK], F32))
        self.full = [ctx.enter_context(nc.semaphore(f"{tag}_full{b}")) for b in range(BANKS)]
        self.drained = [ctx.enter_context(nc.semaphore(f"{tag}_drained{b}")) for b in range(BANKS)]

    def out(self, task):
        return self.ps[:, self.place[task][0], :]

    def wait_empty(self, pe, task):
        bank, before = self.place[task]
        if before:
            pe.wait_ge(self.drained[bank], before)

    def wait_full(self, e, task):
        bank, before = self.place[task]
        e.wait_ge(self.full[bank], before + 1)

    def wait_drained(self, e, task):
        bank, before = self.place[task]
        e.wait_ge(self.drained[bank], before + 1)

    def fill(self, task):
        return self.full[self.place[task][0]]

    def drain(self, task):
        return self.drained[self.place[task][0]]


class Norm:

    def __init__(self, nc, ctx, tag, x_sb, consts):
        def sb(name, shape):
            return ctx.enter_context(nc.sbuf_tensor(f"{tag}_{name}", shape, F32))

        def sem(name):
            return ctx.enter_context(nc.semaphore(f"{tag}_{name}"))
        self.x_sb, self.minus_half = x_sb, consts["minus_half"]
        self.stats = sb("stats", [P, TPC, 6])
        self.mv = sb("mv", [P, TPC, 2])
        self.var = sb("var", [P, TPC])
        self.rstd = sb("rstd", [P, TPC])
        self.xn = sb("xn", [P, 2, TPC, D])
        self.steps = sem("norm_steps")
        self.var_ready = sem("var_ready")
        self.rstd_ready = sem("rstd_ready")
        self.xn_ready = sem("xn_ready")
        self.PER = 2 * TPC + TPC

    def vector(self, dve, nth, c):
        base = nth * 2 * TPC
        for t in range(TPC):
            dve.bn_stats(self.stats[:, t, :], self.x_sb[:, c * TPC + t, :]).then_inc(self.steps, 1)
        for t in range(TPC):
            dve.wait_ge(self.steps, base + t + 1)
            dve.bn_aggr(self.mv[:, t, :], self.stats[:, t, :]).then_inc(self.steps, 1)
        dve.wait_ge(self.steps, base + 2 * TPC)
        dve.tensor_scalar(self.var[:, :], self.mv[:, :, 1], EPS, None, ALU.add).then_inc(self.var_ready, 1)
        dve.wait_ge(self.rstd_ready, nth + 1)
        for t in range(TPC):
            dve.tensor_scalar(self.xn[:, nth % 2, t, :], self.x_sb[:, c * TPC + t, :], self.mv[:, t, 0:1],
                              self.rstd[:, t:t + 1], ALU.subtract, ALU.mult).then_inc(self.xn_ready, 1)

    def gpsimd(self, pool, nth):
        pool.wait_ge(self.var_ready, nth + 1)
        pool.tensor_tensor(self.rstd[:, :], self.var[:, :], self.minus_half[:, 0:TPC],
                           ALU.pow).then_inc(self.rstd_ready, 1)

    def transposes(self, pe, banks, nth, tasks, ident):
        for kc, task in enumerate(tasks):
            banks.wait_empty(pe, task)
            for t in range(TPC):
                if kc == 0:
                    pe.wait_ge(self.xn_ready, nth * TPC + t + 1)
                mm = pe.transpose(banks.out(task)[:, t * P:(t + 1) * P],
                                  self.xn[:, nth % 2, t, kc * P:(kc + 1) * P], ident[:, :])
            mm.then_inc(banks.fill(task), 1)


def project_a(nc, env):
    x_sb, w, consts = env["x_sb"], env["w"], env["consts"]
    order = ["loraB"] + [("fold", kc) for kc in range(KC)]
    turn_tasks = {c: [("turn", c, kc) for kc in range(KC)] for c in range(NC)}
    order += turn_tasks[0]
    for c in range(NC):
        order += [("q", c, m) for m in range(KC)] + [("latent", c)]
        order += turn_tasks[c + 1] if c + 1 < NC else []
        order += [("rotated", c, m) for m in range(KC)]
        order += [("k", c, m) for m in range(KC)]
        order += [("v", c, t) for t in range(TPC)]
        order += [("rotated", c, KC + m) for m in range(KC)]
    MIX, PARTS = 3, 4
    PT = 2 * KC

    def plain_task(c, i):
        return ("q", c, i) if i < KC else ("k", c, i - KC)

    with ExitStack() as ctx:
        def sb(name, shape, dt=F32):
            return ctx.enter_context(nc.sbuf_tensor(f"pa_{name}", shape, dt))

        def sem(name):
            return ctx.enter_context(nc.semaphore(f"pa_{name}"))

        banks = Banks(nc, ctx, "pa", order)
        norm = Norm(nc, ctx, "pa", x_sb, consts)
        w_raw = w["proj"]
        lora_a = sb("lora_a", [RANKS, D])
        lora_b = sb("lora_b", [P, KC, RANKS])
        lora_bt = sb("lora_bt", [RANKS, D])
        coef = sb("coef", [RANKS, 1])
        cos = sb("cos", [P, S])
        sin = sb("sin", [P, S])
        rot = sb("rot", [P, P])
        xnt = sb("xnt", [P, 2, KC, CHUNK])
        latent = sb("latent", [LATENT, 2, CHUNK])
        plain = sb("plain", [P, PT, CHUNK])
        by_cos = sb("by_cos", [P, MIX, CHUNK])
        by_sin = sb("by_sin", [P, CHUNK])
        roped = sb("roped", [P, MIX, CHUNK])
        rest = sb("rest", [P, MIX, CHUNK])
        parts = sb("parts", [P, PARTS, 3, CHUNK], BF16)
        vt = sb("vt", [P, 2, H, VW])

        x_loaded = [sem(f"x_loaded{c}") for c in range(NC)]
        lora_loaded = sem("lora_loaded")
        w_loaded = sem("w_loaded")
        attn_loaded = sem("attn_loaded")
        table_loaded = sem("table_loaded")
        late_loaded = sem("late_loaded")
        ones_set = sem("ones_set")
        cos_ready = sem("cos_ready")
        roped_ready = sem("roped_ready")
        high_ready = sem("high_ready")
        rest_ready = sem("rest_ready")
        middle_ready = sem("middle_ready")
        low_ready = sem("low_ready")
        parts_stored = [sem(f"parts_stored{i}") for i in range(PARTS)]
        v_stored = [sem(f"v_stored{i}") for i in range(2)]

        block = ctx.enter_context(nc.Block())

        @block.sync
        def _(sp):
            for c in range(NC):
                sp.dma_start(x_sb[:, c * TPC:(c + 1) * TPC, :],
                             env["x"][c * CHUNK:(c + 1) * CHUNK, :].rearrange("(t p) d -> p t d", p=P)
                             ).then_inc(x_loaded[c], 16)
                if c == 0:
                    for ot in range(KC):
                        sp.dma_start(lora_b[:, ot, :].rearrange("p (n r) -> p n r", r=DH),
                                     env["lora_B"][:, ot * P:(ot + 1) * P, :].rearrange("n o r -> o n r")
                                     ).then_inc(lora_loaded, 16)
                    sp.dma_start(lora_a[:, :], env["lora_A"].rearrange("n r d -> (n r) d")).then_inc(lora_loaded, 16)
                    sp.dma_start(coef[:, :], env["lora_weights"].rearrange("(n a b) -> n a b", a=1, b=1)
                                 .broadcast_to([RANKS // DH, DH, 1])).then_inc(lora_loaded, 16)
                    sp.dma_start(w_raw[:, :, :], env["W"].rearrange("(o p) d -> p o d", p=P)).then_inc(w_loaded, 16)
                    sp.dma_start(w["q"][:, :, :], env["Wq"].rearrange("(k p) n -> p k n", p=P)).then_inc(attn_loaded, 16)
                    sp.dma_start(w["c"][:, :, :], env["Wc"].rearrange("(k p) n -> p k n", p=P)).then_inc(attn_loaded, 16)
                    sp.dma_start(w["k"][:, :], env["Wk"]).then_inc(attn_loaded, 16)
                    sp.dma_start(w["v"][:, :], env["Wv"]).then_inc(attn_loaded, 16)
                    for t, name in ((cos, "cos"), (sin, "sin"), (rot, "rot")):
                        sp.dma_start(t[:, :], env[name]).then_inc(table_loaded, 16)
            late = [
                (w["o"][:, :, :], env["Wo"].rearrange("(k p) n -> p k n", p=P)),
                (w["qkv"][:, :, :], env["w_attn"].rearrange("(k p) n -> p k n", p=P)),
                (w["proj"][:, :, :], env["w_proj"].rearrange("(k p) n -> p k n", p=P)),
                (w["bv"][:, :], env["b_attn"][2 * D:3 * D].partition_broadcast(P)),
                (w["bias"][:, :], env["bias"].partition_broadcast(P)),
                (w["bproj"][:, :], env["b_proj"].partition_broadcast(P)),
            ]
            n_v = 0
            for c in range(NC):
                b, half = c // 2, c % 2

                def store_v():
                    for t in range(TPC):
                        n = c * TPC + t
                        banks.wait_drained(sp, ("v", c, t))
                        sp.dma_start(
                            env["va_d"].rearrange("(g p) (k c) -> p g k c", p=P, k=8)[
                                :, b * GPB:(b + 1) * GPB, half * TPC + t, :],
                            vt[:, n % 2, :, :].rearrange("p (g h) c -> p g (h c)", h=GH)).then_inc(v_stored[n % 2], 16)
                for i in range(PT):
                    n = c * PT + i
                    sp.wait_ge(low_ready, n + 1)
                    dst = env["qa_d"] if i < KC else env["ka_d"]
                    row = b * D + (i % KC) * P
                    sp.dma_start(dst[:, row:row + P, half * CHUNK:(half + 1) * CHUNK].rearrange("w d t -> d w t"),
                                 parts[:, n % PARTS, :, :]).then_inc(parts_stored[n % PARTS], 16)
                    if i == 1:
                        store_v()
                    if c == 0 and i == 0:
                        banks.wait_full(sp, ("fold", KC - 1))
                        for dst, src in late:
                            sp.dma_start(dst, src).then_inc(late_loaded, 16)
                        sp.dma_start(w["bqk"][:, :], env["b_attn"][0:2 * D].rearrange("(m p) -> p m", p=P),
                                     allow_slow_non_contiguous=True).then_inc(late_loaded, 16)
            for i in range(PARTS):
                sp.wait_ge(parts_stored[i], 16 * (NC * PT // PARTS))
            for i in range(2):
                sp.wait_ge(v_stored[i], 16 * (NC * TPC // 2))
            sp.wait_ge(late_loaded, 16 * (len(late) + 1))

        @block.tensor
        def _(pe):
            ident = consts["ident"]
            pe.wait_ge(lora_loaded, 16 * (KC + 2))
            for ot in range(KC):
                mm = pe.transpose(banks.out("loraB")[:, ot * P:(ot + 1) * P], lora_b[:, ot, :], ident[:, :])
            mm.then_inc(banks.fill("loraB"), 1)
            banks.wait_drained(pe, "loraB")
            pe.wait_ge(w_loaded, 16)
            for kc in range(KC):
                out = banks.out(("fold", kc))
                for ot in range(KC):
                    pe.matmul(out[:, ot * P:(ot + 1) * P], w_raw[:, ot, kc * P:(kc + 1) * P], ident[:, :],
                              start=(ot == 0), stop=False, skip_group_check=True)
                mm = pe.matmul(out, lora_a[:, kc * P:(kc + 1) * P], lora_bt[:, :], start=False, stop=True,
                               skip_group_check=True)
                mm.then_inc(banks.fill(("fold", kc)), 1)
            norm.transposes(pe, banks, 0, turn_tasks[0], ident)
            pe.wait_ge(attn_loaded, 64)
            pe.wait_ge(table_loaded, 48)
            for c in range(NC):
                def rotated(i):
                    task = ("rotated", c, i)
                    banks.wait_empty(pe, task)
                    banks.wait_drained(pe, plain_task(c, i))
                    pe.matmul(banks.out(task), rot[:, :], plain[:, i, :],
                              start=True, stop=True).then_inc(banks.fill(task), 1)
                for task in turn_tasks[c]:
                    banks.wait_drained(pe, task)
                for m in range(KC):
                    task = ("q", c, m)
                    banks.wait_empty(pe, task)
                    for kc in range(KC):
                        mm = pe.matmul(banks.out(task), w["q"][:, kc, m * P:(m + 1) * P], xnt[:, c % 2, kc, :],
                                       start=(kc == 0), stop=(kc == KC - 1))
                    mm.then_inc(banks.fill(task), 1)
                task = ("latent", c)
                banks.wait_empty(pe, task)
                for kc in range(KC):
                    mm = pe.matmul(banks.out(task)[0:LATENT, :], w["c"][:, kc, :], xnt[:, c % 2, kc, :],
                                   start=(kc == 0), stop=(kc == KC - 1))
                mm.then_inc(banks.fill(task), 1)
                if c + 1 < NC:
                    norm.transposes(pe, banks, c + 1, turn_tasks[c + 1], ident)
                for m in range(KC):
                    rotated(m)
                banks.wait_drained(pe, ("latent", c))
                for m in range(KC):
                    task = ("k", c, m)
                    banks.wait_empty(pe, task)
                    pe.matmul(banks.out(task), w["k"][:, m * P:(m + 1) * P], latent[:, c % 2, :],
                              start=True, stop=True).then_inc(banks.fill(task), 1)
                for t in range(TPC):
                    task = ("v", c, t)
                    banks.wait_empty(pe, task)
                    pe.matmul(banks.out(task), latent[:, c % 2, t * P:(t + 1) * P], w["v"][:, :],
                              start=True, stop=True).then_inc(banks.fill(task), 1)
                for m in range(KC):
                    rotated(KC + m)

        @block.scalar
        def _(act):
            def copy(dst, task):
                banks.wait_full(act, task)
                act.activation(dst, banks.out(task), ACT.Copy).then_inc(banks.drain(task), 1)

            def copy_plain(c, i):
                if c:
                    act.wait_ge(roped_ready, (c - 1) * PT + i + 1)
                copy(plain[:, i, :], plain_task(c, i))

            def high(c, i):
                n = c * PT + i
                if n >= PARTS:
                    act.wait_ge(parts_stored[n % PARTS], 16 * (n // PARTS))
                act.wait_ge(roped_ready, n + 1)
                act.activation(parts[:, n % PARTS, 0, :], roped[:, n % MIX, :], ACT.Copy).then_inc(high_ready, 1)

            def middle(c, i):
                n = c * PT + i
                act.wait_ge(rest_ready, n + 1)
                act.activation(parts[:, n % PARTS, 1, :], rest[:, n % MIX, :], ACT.Copy).then_inc(middle_ready, 1)

            def turned(c):
                for kc, task in enumerate(turn_tasks[c]):
                    copy(xnt[:, c % 2, kc, :], task)

            for kc in range(KC):
                copy(w["eff"][:, kc, :], ("fold", kc))
            turned(0)
            act.wait_ge(ones_set, 1)
            for c in range(NC):
                for i in range(KC):
                    copy_plain(c, i)
                banks.wait_full(act, ("latent", c))
                act.activation(latent[:, c % 2, :], banks.out(("latent", c))[0:LATENT, :],
                               ACT.Copy).then_inc(banks.drain(("latent", c)), 1)
                if c + 1 < NC:
                    turned(c + 1)
                for i in range(KC):
                    high(c, i)
                    if i:
                        middle(c, i - 1)
                    copy_plain(c, KC + i)
                for t in range(TPC):
                    n = c * TPC + t
                    if n >= 2:
                        act.wait_ge(v_stored[n % 2], 16 * (n // 2))
                    task = ("v", c, t)
                    banks.wait_full(act, task)
                    act.activation(vt[:, n % 2, :, 0:DH], banks.out(task).rearrange("p (h d) -> p h d", d=DH),
                                   ACT.Copy).then_inc(banks.drain(task), 1)
                for i in range(KC, PT):
                    high(c, i)
                    middle(c, i - 1)
                middle(c, PT - 1)

        @block.gpsimd
        def _(pool):
            pool.memset(vt[:, :, :, :], 1.0).then_inc(ones_set, 1)

            def times_cos(c, i):
                n = c * PT + i
                if n >= MIX:
                    pool.wait_ge(roped_ready, n - MIX + 1)
                if n == 0:
                    pool.wait_ge(table_loaded, 48)
                banks.wait_drained(pool, plain_task(c, i))
                at = (c % 2) * CHUNK
                pool.tensor_tensor(by_cos[:, n % MIX, :], plain[:, i, :], cos[:, at:at + CHUNK],
                                   ALU.mult).then_inc(cos_ready, 1)

            norm.gpsimd(pool, 0)
            norm.gpsimd(pool, 1)
            for c in range(NC):
                for i in range(KC):
                    times_cos(c, i)
                if c + 2 < NC:
                    norm.gpsimd(pool, c + 2)
                for i in range(KC, PT):
                    times_cos(c, i)

        @block.vector
        def _(dve):
            def rope(c, i):
                n = c * PT + i
                task = ("rotated", c, i)
                at = (c % 2) * CHUNK
                banks.wait_full(dve, task)
                if n == 0:
                    dve.wait_ge(table_loaded, 48)
                if n:
                    dve.wait_ge(roped_ready, n)
                dve.tensor_tensor(by_sin[:, :], banks.out(task), sin[:, at:at + CHUNK],
                                  ALU.mult).then_inc(banks.drain(task), 1)
                banks.wait_drained(dve, task)
                dve.wait_ge(cos_ready, n + 1)
                dve.tensor_tensor(roped[:, n % MIX, :], by_cos[:, n % MIX, :], by_sin[:, :],
                                  ALU.add).then_inc(roped_ready, 1)

            def less_high(n):
                dve.wait_ge(high_ready, n + 1)
                dve.tensor_tensor(rest[:, n % MIX, :], roped[:, n % MIX, :], parts[:, n % PARTS, 0, :],
                                  ALU.subtract).then_inc(rest_ready, 1)

            def low(n):
                dve.wait_ge(middle_ready, n + 1)
                dve.tensor_tensor(parts[:, n % PARTS, 2, :], rest[:, n % MIX, :], parts[:, n % PARTS, 1, :],
                                  ALU.subtract).then_inc(low_ready, 1)

            def normalise(c):
                dve.wait_ge(x_loaded[c], 16)
                norm.vector(dve, c, c)

            normalise(0)
            dve.wait_ge(lora_loaded, 16 * (KC + 2))
            banks.wait_full(dve, "loraB")
            dve.tensor_scalar(lora_bt[:, :], banks.out("loraB"), coef[:, 0:1], LORA_SCALE,
                              ALU.mult, ALU.mult).then_inc(banks.drain("loraB"), 1)
            normalise(1)
            for c in range(NC):
                for i in range(PT):
                    n = c * PT + i
                    if i == KC and c + 2 < NC:
                        banks.wait_full(dve, turn_tasks[c][-1])
                        normalise(c + 2)
                    rope(c, i)
                    if i >= 1:
                        less_high(n - 1)
                    if i >= 2:
                        low(n - 2)
                less_high(c * PT + PT - 1)
                low(c * PT + PT - 2)
                low(c * PT + PT - 1)


def output_and_ffn(nc, env, tag, o_d, z_d, rz_d, w_out, out_bias, nxt):
    x_sb, w, consts = env["x_sb"], env["w"], env["consts"]
    STEPS = NC + (2 if nxt else 1)
    MIX, PARTS, PT = 3, 4, 2 * KC
    f_turns = {c: [("f_turn", c, kc) for kc in range(KC)] for c in range(NC)}
    q_turns = {c: [("q_turn", c, kc) for kc in range(KC)] for c in range(NC)}
    order = []
    for k in range(STEPS):
        if k < NC:
            order += [("o", k, t) for t in range(TPC)]
        if 0 <= k - 1 < NC:
            order += f_turns[k - 1] + [("f", k - 1, t) for t in range(TPC)]
        if nxt and 0 <= k - 2 < NC:
            order += q_turns[k - 2] + [("qk", k - 2, m) for m in range(PT)] + [("v", k - 2, t) for t in range(TPC)]

    with ExitStack() as ctx:
        def sb(name, shape, dt=F32):
            return ctx.enter_context(nc.sbuf_tensor(f"{tag}_{name}", shape, dt))

        def sem(name):
            return ctx.enter_context(nc.semaphore(f"{tag}_{name}"))

        banks = Banks(nc, ctx, tag, order)
        f_norm = Norm(nc, ctx, tag + "_f", x_sb, consts)
        z_sb = sb("z", [P, NC, P])
        rz_sb = sb("rz", [P, NC, P])
        o_sb = sb("o", [P, 2, KC, CHUNK])
        rzt = sb("rzt", [P, KC, CHUNK])
        f_xnt = sb("f_xnt", [P, 2, KC, CHUNK])
        z_loaded = sem("z_loaded")
        rz_ready = sem("rz_ready")
        rz_stored = sem("rz_stored")
        o_loaded = [sem(f"o_loaded{i}") for i in range(2)]
        o_scaled = sem("o_scaled")
        added = sem("added")
        out_stored = sem("out_stored")
        if nxt:
            q_norm = Norm(nc, ctx, tag + "_q", x_sb, consts)
            q_xnt = sb("q_xnt", [P, 2, KC, CHUNK])
            rest = sb("rest", [P, MIX, CHUNK])
            parts = sb("parts", [P, PARTS, 3, CHUNK], BF16)
            vt = sb("vt", [P, 2, H, VW])
            ones_set = sem("ones_set")
            high_ready = sem("high_ready")
            middle_ready = sem("middle_ready")
            low_ready = sem("low_ready")
            parts_stored = [sem(f"parts_stored{i}") for i in range(PARTS)]
            v_stored = [sem(f"v_stored{i}") for i in range(2)]
        added_per_chunk = TPC * (2 if out_bias is not None else 1)
        o_added, f_added, n = {}, {}, 0
        for k in range(STEPS):
            if k < NC and out_bias is not None:
                n += TPC
                o_added[k] = n
            if 0 <= k - 1 < NC:
                n += TPC
                f_added[k - 1] = n

        block = ctx.enter_context(nc.Block())

        @block.sync
        def _(sp):
            def chunk_of(t, c):
                return t[c % 2, (c // 2) * H:(c // 2 + 1) * H, :].rearrange("h (a t) -> (h a) t", t=P)

            def load_output(c):
                b, half = c // 2, c % 2
                sp.dma_start(o_sb[:, c % 2, :, :],
                             o_d[b * D:(b + 1) * D, half * CHUNK:(half + 1) * CHUNK].rearrange("(k p) t -> p k t", p=P)
                             ).then_inc(o_loaded[c % 2], 16)
                sp.wait_ge(rz_stored, 16 * NC)
                if c:
                    sp.wait_ge(o_scaled, KC * c)
                for kc in range(KC):
                    heads = rz_d[half, b * H + kc * (P // DH):b * H + (kc + 1) * (P // DH), :]
                    sp.dma_start(rzt[:, kc, :],
                                 heads.unsqueeze(1).broadcast_to([P // DH, DH, CHUNK])
                                 ).then_inc(o_loaded[c % 2], 16)

            for c in range(NC):
                sp.dma_start(z_sb[:, c, :], chunk_of(z_d, c)).then_inc(z_loaded, 16)
            for c in range(NC):
                sp.wait_ge(rz_ready, c + 1)
                sp.dma_start(chunk_of(rz_d, c), rz_sb[:, c, :]).then_inc(rz_stored, 16)
            for c in range(2):
                load_output(c)
            for k in range(STEPS):
                if k + 2 < NC:
                    banks.wait_full(sp, ("o", k, TPC - 1))
                    load_output(k + 2)
                c = k - 1
                if not nxt and 0 <= c < NC:
                    for t in range(TPC):
                        sp.wait_ge(added, f_added[c] - TPC + t + 1)
                        row = (c * TPC + t) * P
                        sp.dma_start(env["out"][row:row + P, :], x_sb[:, c * TPC + t, :]).then_inc(out_stored, 16)
                c = k - 2
                if nxt and 0 <= c < NC:
                    b, half = c // 2, c % 2
                    for i in range(PT):
                        n = c * PT + i
                        sp.wait_ge(low_ready, n + 1)
                        dst = env["qb_d"] if i < KC else env["kb_d"]
                        row = b * D + (i % KC) * P
                        sp.dma_start(dst[:, row:row + P, half * CHUNK:(half + 1) * CHUNK].rearrange("w d t -> d w t"),
                                     parts[:, n % PARTS, :, :]).then_inc(parts_stored[n % PARTS], 16)
                    for t in range(TPC):
                        n = c * TPC + t
                        banks.wait_drained(sp, ("v", c, t))
                        sp.dma_start(
                            env["vb_d"].rearrange("(g p) (k c) -> p g k c", p=P, k=8)[
                                :, b * GPB:(b + 1) * GPB, half * TPC + t, :],
                            vt[:, n % 2, :, :].rearrange("p (g h) c -> p g (h c)", h=GH)).then_inc(v_stored[n % 2], 16)
            if nxt:
                for i in range(PARTS):
                    sp.wait_ge(parts_stored[i], 16 * (NC * PT // PARTS))
                for i in range(2):
                    sp.wait_ge(v_stored[i], 16 * (NC * TPC // 2))
            else:
                sp.wait_ge(out_stored, 16 * TILES)

        @block.tensor
        def _(pe):
            ident = consts["ident"]

            def natural(kind, c, lhs, weights):
                for t in range(TPC):
                    task = (kind, c, t)
                    banks.wait_empty(pe, task)
                    for kc in range(KC):
                        mm = pe.matmul(banks.out(task), lhs(kc)[:, t * P:(t + 1) * P], weights(kc),
                                       start=(kc == 0), stop=(kc == KC - 1))
                    mm.then_inc(banks.fill(task), 1)

            for k in range(STEPS):
                if k < NC:
                    pe.wait_ge(o_scaled, KC * (k + 1))
                    natural("o", k, lambda kc: o_sb[:, k % 2, kc, :], lambda kc: w_out[:, kc, :])
                c = k - 1
                if 0 <= c < NC:
                    f_norm.transposes(pe, banks, c, f_turns[c], ident)
                    for task in f_turns[c]:
                        banks.wait_drained(pe, task)
                    natural("f", c, lambda kc: f_xnt[:, c % 2, kc, :], lambda kc: w["eff"][:, kc, :])
                c = k - 2
                if nxt and 0 <= c < NC:
                    q_norm.transposes(pe, banks, c, q_turns[c], ident)
                    for task in q_turns[c]:
                        banks.wait_drained(pe, task)
                    for m in range(PT):
                        task = ("qk", c, m)
                        banks.wait_empty(pe, task)
                        for kc in range(KC):
                            mm = pe.matmul(banks.out(task), w["qkv"][:, kc, m * P:(m + 1) * P],
                                           q_xnt[:, c % 2, kc, :], start=(kc == 0), stop=(kc == KC - 1))
                        mm.then_inc(banks.fill(task), 1)
                    natural("v", c, lambda kc: q_xnt[:, c % 2, kc, :], lambda kc: w["qkv"][:, kc, 2 * D:3 * D])

        @block.scalar
        def _(act):
            def turned(xnt, c, tasks):
                for kc, task in enumerate(tasks):
                    banks.wait_full(act, task)
                    act.activation(xnt[:, c % 2, kc, :], banks.out(task), ACT.Copy).then_inc(banks.drain(task), 1)

            def high(c, i):
                n = c * PT + i
                if n >= PARTS:
                    act.wait_ge(parts_stored[n % PARTS], 16 * (n // PARTS))
                banks.wait_full(act, ("qk", c, i))
                act.activation(parts[:, n % PARTS, 0, :], banks.out(("qk", c, i)), ACT.Identity,
                               bias=w["bqk"][:, i:i + 1]).then_inc(high_ready, 1)

            def middle(c, i):
                n = c * PT + i
                banks.wait_drained(act, ("qk", c, i))
                act.activation(parts[:, n % PARTS, 1, :], rest[:, n % MIX, :], ACT.Copy).then_inc(middle_ready, 1)

            for k in range(STEPS):
                if 0 <= k - 1 < NC:
                    turned(f_xnt, k - 1, f_turns[k - 1])
                c = k - 2
                if nxt and 0 <= c < NC:
                    turned(q_xnt, c, q_turns[c])
                    for i in range(PT):
                        high(c, i)
                        if i:
                            middle(c, i - 1)
                    middle(c, PT - 1)

        @block.gpsimd
        def _(pool):
            if nxt:
                pool.memset(vt[:, :, :, :], 1.0).then_inc(ones_set, 1)
            for k in range(STEPS):
                if k < NC:
                    f_norm.gpsimd(pool, k)
                if nxt and 0 <= k - 1 < NC:
                    q_norm.gpsimd(pool, k - 1)

        @block.vector
        def _(dve):
            def scale_output(c):
                dve.wait_ge(o_loaded[c % 2], 16 * (KC + 1) * (c // 2 + 1))
                for kc in range(KC):
                    dve.tensor_tensor(o_sb[:, c % 2, kc, :], o_sb[:, c % 2, kc, :], rzt[:, kc, :],
                                      ALU.mult).then_inc(o_scaled, 1)

            def residual(kind, c, bias, counts):
                for t in range(TPC):
                    task, tile = (kind, c, t), x_sb[:, c * TPC + t, :]
                    banks.wait_full(dve, task)
                    dve.tensor_tensor(tile, banks.out(task), tile, ALU.add).then_inc(banks.drain(task), 1)
                for t in range(TPC):
                    task, tile = (kind, c, t), x_sb[:, c * TPC + t, :]
                    banks.wait_drained(dve, task)
                    if bias is not None:
                        dve.tensor_tensor(tile, tile, bias[:, :], ALU.add).then_inc(added, 1)
                if bias is not None:
                    dve.wait_ge(added, counts[c])

            def less_high(c, i):
                n, task = c * PT + i, ("qk", c, i)
                dve.wait_ge(high_ready, n + 1)
                if n >= MIX:
                    dve.wait_ge(low_ready, n - MIX + 1)
                dve.scalar_tensor_tensor(out=rest[:, n % MIX, :], in0=banks.out(task), scalar=w["bqk"][:, i:i + 1],
                                         in1=parts[:, n % PARTS, 0, :], op0=ALU.add,
                                         op1=ALU.subtract).then_inc(banks.drain(task), 1)

            def low(c, i):
                n = c * PT + i
                dve.wait_ge(middle_ready, n + 1)
                dve.tensor_tensor(parts[:, n % PARTS, 2, :], rest[:, n % MIX, :], parts[:, n % PARTS, 1, :],
                                  ALU.subtract).then_inc(low_ready, 1)

            def value(c, t):
                n, task = c * TPC + t, ("v", c, t)
                if n >= 2:
                    dve.wait_ge(v_stored[n % 2], 16 * (n // 2))
                banks.wait_full(dve, task)
                dve.tensor_tensor(vt[:, n % 2, :, 0:DH], banks.out(task).rearrange("p (h d) -> p h d", d=DH),
                                  w["bv"][:, :].rearrange("p (h d) -> p h d", d=DH),
                                  ALU.add).then_inc(banks.drain(task), 1)

            dve.wait_ge(z_loaded, 16 * NC)
            for c in range(NC):
                dve.reciprocal(rz_sb[:, c, :], z_sb[:, c, :]).then_inc(rz_ready, 1)
            scale_output(0)
            if nxt:
                dve.wait_ge(ones_set, 1)
            for k in range(STEPS):
                if k + 1 < NC:
                    scale_output(k + 1)
                if k < NC:
                    residual("o", k, out_bias, o_added)
                    if k >= 2:
                        banks.wait_full(dve, f_turns[k - 2][-1])
                    f_norm.vector(dve, k, k)
                c = k - 1
                if 0 <= c < NC:
                    residual("f", c, w["bias"], f_added)
                    if nxt:
                        if c >= 2:
                            banks.wait_full(dve, q_turns[c - 2][-1])
                        q_norm.vector(dve, c, c)
                c = k - 2
                if nxt and 0 <= c < NC:
                    for i in range(PT):
                        less_high(c, i)
                        if i:
                            low(c, i - 1)
                    low(c, PT - 1)
                    for t in range(TPC):
                        value(c, t)


def build(nc, ins, out):
    env = {
        "x": ins["L0_attn_a_hidden_states"].rearrange("b s d -> (b s) d"),
        "out": out.rearrange("b s d -> (b s) d"),
        "Wq": ins["L0_attn_a_Wq"], "Wc": ins["L0_attn_a_Wc"], "Wk": ins["L0_attn_a_Wk"],
        "Wv": ins["L0_attn_a_Wv"], "Wo": ins["L0_attn_a_Wo"],
        "w_attn": ins["L0_attn_b_w_attn"], "b_attn": ins["L0_attn_b_b_attn"],
        "w_proj": ins["L0_attn_b_w_proj"], "b_proj": ins["L0_attn_b_b_proj"],
        "lora_A": ins["L0_ffn_lora_A"], "lora_B": ins["L0_ffn_lora_B"], "W": ins["L0_ffn_W"],
        "bias": ins["L0_ffn_bias"], "lora_weights": ins["L0_ffn_lora_weights"],
        "cos": ins["cos"], "sin": ins["sin"], "rot": ins["rot"],
    }
    for a in "ab":
        env[f"q{a}_d"] = nc.dram_tensor(f"q{a}_parts", [3, B * D, S], BF16).ap()
        env[f"k{a}_d"] = nc.dram_tensor(f"k{a}_parts", [3, B * D, S], BF16).ap()
        env[f"v{a}_d"] = nc.dram_tensor(f"v{a}_groups", [NG * P, 8 * GH * VW], F32).ap()
        env[f"o{a}_d"] = nc.dram_tensor(f"o{a}_sums", [B * D, S], F32).ap()
        env[f"z{a}_d"] = nc.dram_tensor(f"z{a}_sums", [2, B * H, CHUNK], F32).ap()
        env[f"rz{a}_d"] = nc.dram_tensor(f"z{a}_reciprocals", [2, B * H, CHUNK], F32).ap()

    with ExitStack() as ctx:
        def sb(name, shape, dt=F32):
            return ctx.enter_context(nc.sbuf_tensor(name, shape, dt))

        env["x_sb"] = sb("x_sb", [P, TILES, D])
        env["w"] = {
            "o": sb("w_o", [P, KC, D]), "eff": sb("w_eff", [P, KC, D]), "qkv": sb("w_qkv", [P, KC, 3 * D]),
            "proj": sb("w_proj", [P, KC, D]), "bqk": sb("b_qk", [P, 2 * KC]), "bv": sb("b_v", [P, D]),
            "bias": sb("b_ffn", [P, D]), "bproj": sb("b_proj", [P, D]),
        }
        consts = env["consts"] = {
            "ident": sb("ident", [P, P]), "minus_half": sb("minus_half", [P, 8]),
            "ident_bf": sb("ident_bf", [P, P], BF16), "mask_qk": sb("mask_qk", [P, P], BF16),
            "mask_kq": sb("mask_kq", [P, P], BF16),
        }
        consts_loaded = ctx.enter_context(nc.semaphore("consts_loaded"))
        names = ("ident", "minus_half", "ident_bf", "mask_qk", "mask_kq")
        with nc.Block() as block:
            @block.sync
            def _(sp):
                for name in names:
                    sp.dma_start(consts[name][:, :], ins[name]).then_inc(consts_loaded, 16)
                sp.wait_ge(consts_loaded, 16 * len(names))

        with ExitStack() as early:
            w = env["w"]
            for name, shape in (("q", [P, KC, D]), ("c", [P, KC, LATENT]), ("k", [LATENT, D]), ("v", [LATENT, D])):
                w[name] = early.enter_context(nc.sbuf_tensor(f"w_{name}", shape, F32))
            project_a(nc, env)
        attention(nc, "a", False, DH ** -0.5, consts, env["qa_d"], env["ka_d"], env["va_d"], env["oa_d"],
                  env["za_d"], None)
        output_and_ffn(nc, env, "mid", env["oa_d"], env["za_d"], env["rza_d"], w["o"], None, True)
        attention(nc, "b", True, 1.0 / DH, consts, env["qb_d"], env["kb_d"], env["vb_d"], env["ob_d"],
                  env["zb_d"], ins["alibi"])
        output_and_ffn(nc, env, "fin", env["ob_d"], env["zb_d"], env["rzb_d"], w["proj"], w["bproj"], False)


def in_parts(x, dtype):
    high = x.astype(dtype)
    middle = (x - high.astype(np.float32)).astype(dtype)
    low = (x - high.astype(np.float32) - middle.astype(np.float32)).astype(dtype)
    return high, middle, low


def shape_constants():
    bf16 = np.dtype("bfloat16")
    inv_freq = (1.0 / np.float32(10000.0) ** (np.arange(0, DH, 2, dtype=np.float32) / np.float32(DH))).astype(np.float32)
    freqs = np.arange(S, dtype=np.float32)[:, None] * inv_freq
    angle = np.concatenate([freqs, freqs], axis=-1).T
    rot = np.zeros((P, P), np.float32)
    for i in range(P):
        if i % DH < DH // 2:
            rot[i + DH // 2, i] = -1.0
        else:
            rot[i - DH // 2, i] = 1.0
    key, query = np.arange(P)[:, None], np.arange(P)[None, :]
    mask_kq = np.where(key > query, NEG, 0.0).astype(np.float32)
    base = 2 ** (-2 ** (-(np.log2(H) - 3)))
    slopes = (base ** np.arange(1, H + 1, dtype=np.float32)).astype(np.float32)
    ramp = (slopes[:, None] * np.float32(DH) * np.arange(S, dtype=np.float32)[None, :]).astype(np.float32)
    parts = np.stack(in_parts(ramp, bf16), axis=1)
    alibi = parts.reshape(GPB, GH, 3, S).transpose(0, 2, 1, 3).reshape(GPB * 3, GH * S)
    return {
        "cos": np.tile(np.cos(angle), (P // DH, 1)).astype(np.float32),
        "sin": np.tile(np.sin(angle), (P // DH, 1)).astype(np.float32),
        "rot": rot,
        "ident": np.eye(P, dtype=np.float32),
        "minus_half": np.full((P, 8), -0.5, np.float32),
        "ident_bf": np.eye(P, dtype=np.float32).astype(bf16),
        "mask_kq": mask_kq.astype(bf16),
        "mask_qk": mask_kq.T.copy().astype(bf16),
        "alibi": np.concatenate([alibi, alibi]),
    }


NAMES = ["L0_attn_a_hidden_states", "L0_attn_a_Wq", "L0_attn_a_Wc", "L0_attn_a_Wk", "L0_attn_a_Wv",
         "L0_attn_a_Wo", "L0_attn_b_w_attn", "L0_attn_b_b_attn", "L0_attn_b_w_proj", "L0_attn_b_b_proj",
         "L0_ffn_lora_A", "L0_ffn_lora_B", "L0_ffn_W", "L0_ffn_bias", "L0_ffn_lora_weights"]


def kernel(**inputs):
    import concourse.bacc as bacc
    from concourse.bass_utils import run_bass_kernel_spmd

    nc = bacc.Bacc("TRN2", target_bir_lowering=False, num_devices=1)
    host = {name: np.ascontiguousarray(inputs[name]) for name in NAMES}
    host.update(shape_constants())
    arrays, ins = {}, {}
    for name, a in host.items():
        arrays[f"in_{name}"] = a
        ins[name] = nc.dram_tensor(f"in_{name}", a.shape, mybir.dt.from_np(a.dtype), kind="ExternalInput").ap()
    out = nc.dram_tensor("out", (B, S, D), F32, kind="ExternalOutput").ap()
    build(nc, ins, out)
    r = run_bass_kernel_spmd(nc, [arrays], core_ids=[0])
    return r.results[0]["out"]
```

```python
from contextlib import ExitStack

import numpy as np

import concourse.bass as bass
from concourse import mybir

ALU = mybir.AluOpType
ACT = mybir.ActivationFunctionType
AX = mybir.AxisListType
BF16 = mybir.dt.bfloat16
F32 = mybir.dt.float32

P = 128
B, S, D = 2, 1024, 512
H, DH = 32, 16
LATENT = 64
RANKS = 128
T = B * S
TILES = T // P
CHUNK = 512
NC = T // CHUNK
TPC = CHUNK // P
KC = D // P
GH = 4
GPB = H // GH
NG = B * GPB
GD = GH * DH
VW = 32
EPS = 1e-5
LORA_SCALE = 2.0
NEG = -1e30
LOWEST = -3e38
BANKS = 8
Q_PARTS = (0, 0, 0, 1, 1, 2)
K_PARTS = (0, 1, 2, 0, 1, 0)
SROWS = DH * len(Q_PARTS)
SLOTS = 3
PEELED_FRONT = 1
LOOPED = 12


def wait_past(e, sem, value):
    if not isinstance(value, int) or value > 0:
        e.wait_ge(sem, value)


def attention(nc, tag, causal, scale, consts, q_d, k_d, v_d, o_d, z_d, alibi_d, ones_d, output):
    units = [(qh, kt) for qh in range(2) for kt in range((4 * (qh + 1)) if causal else 8)]
    NU = len(units)
    LEAD = 13 if causal else 11
    pieces = []
    for qh in range(2):
        for h in range(GH):
            for qt in range(4 * qh, 4 * qh + 4):
                for half in range(2):
                    n = min(CHUNK, P * (qt + 1) - CHUNK * half) if causal else CHUNK
                    if n > 0:
                        pieces.append((h, qt, half, n))
    NPC = len(pieces)
    PPU = NPC // NU
    NPH = PPU * sum(qh == 0 for qh, _ in units)
    al = 3 if causal else 0
    crow = SROWS + al
    rows = crow + 3
    ROWS_H = GH * 4
    TPU = 2
    NT = NU * TPU
    NP = 4
    MXB = 3
    K_LOAD = 16 * len(K_PARTS) + (16 if causal else 0)
    LOAD = 16 * len(Q_PARTS) + K_LOAD
    SETS = 16 * SLOTS * (2 if causal else 1)
    STORES = 16 * (GH + 1)
    SHIFT = 16
    ITEMS = NPC + 2
    first_of = {qh: min(u for u in range(NU) if units[u][0] == qh) for qh in range(2)}
    last_of = {qh: max(u for u in range(NU) if units[u][0] == qh) for qh in range(2)}
    LINKS = 3

    def item(g, i):
        if isinstance(g, int) and g == 0 and i < PPU:
            return i
        return g * ITEMS + (i - 1 if i < PPU else i if i < NPH + PPU else i + 1)

    def turned_item(g, qh):
        if qh == 0:
            return g * ITEMS + (NPH + PPU)
        if isinstance(g, int) and g == NG - 1:
            return NG * ITEMS - 1
        return g * ITEMS + (ITEMS - 1 + PPU)

    def at_bank(g, j):
        return g if isinstance(g, int) else j + SLOTS

    def bank_of(g, j, i):
        return item(at_bank(g, j), i) % MXB

    def turned_bank(g, j, qh):
        return turned_item(at_bank(g, j), qh) % MXB

    with ExitStack() as ctx:
        def sb(name, shape, dt):
            return ctx.enter_context(nc.sbuf_tensor(f"{tag}_{name}", shape, dt))

        def sem(name):
            return ctx.enter_context(nc.semaphore(f"{tag}_{name}"))

        q_sb = [sb(f"q{j}", [rows, GH * S], BF16) for j in range(SLOTS)]
        k_sb = [sb(f"k{j}", [rows, GH * S], BF16) for j in range(SLOTS)]
        v_sb = [sb(f"v{j}", [P, 8, GH * VW], F32) for j in range(SLOTS)]
        p_sb = sb("p", [P, NP, 2, CHUNK], F32)
        o_sb = sb("o", [P, 2, CHUNK], F32)
        mxp = sb("mxp", [P, 2, ROWS_H, 2], F32)
        negm = sb("negm", [P, ROWS_H], F32)
        rest = sb("rest", [P, ROWS_H], F32)
        zeros = sb("zeros", [P, ROWS_H], F32)
        cparts = sb("cparts", [P, 3, ROWS_H], BF16)
        cturned = sb("cturned", [3 * ROWS_H, P], BF16)
        ps_s = ctx.enter_context(nc.psum_tensor(f"{tag}_ps_s", [P, 4, CHUNK], F32))
        ps_m = ctx.enter_context(nc.psum_tensor(f"{tag}_ps_m", [P, MXB, CHUNK], F32))
        ps_o = ctx.enter_context(nc.psum_tensor(f"{tag}_ps_o", [P, CHUNK], F32))

        rows_set = sem("rows_set")
        qk_loaded = [sem(f"qk_loaded{j}") for j in range(SLOTS)]
        first_loaded = [sem(f"first_loaded{j}") for j in range(SLOTS)]
        v_loaded = [sem(f"v_loaded{j}") for j in range(SLOTS)]
        piece_ready = sem("piece_ready")
        piece_taken = sem("piece_taken")
        filled = sem("filled")
        negated = sem("negated")
        chain = sem("chain")
        parts_ready = sem("parts_ready")
        shift_loaded = sem("shift_loaded")
        score_ready = sem("score_ready")
        exp_done = sem("exp_done")
        pv_done = sem("pv_done")
        out_copied = sem("out_copied")
        out_stored = [sem(f"out_stored{qh}") for qh in range(2)]

        block = ctx.enter_context(nc.Block())

        def load_q(e, g, j):
            for r, part in enumerate(Q_PARTS):
                e.dma_start(q_sb[j][DH * r:DH * (r + 1), :].rearrange("d (n t) -> d n t", t=CHUNK),
                            q_d[part, bass.ds(g * 2 * GD, 2 * GD), :].rearrange("(n d) t -> d n t", d=DH),
                            ).then_inc(qk_loaded[j], 16)

        def load_k(e, g, j, loaded):
            for r, part in enumerate(K_PARTS):
                e.dma_start(k_sb[j][DH * r:DH * (r + 1), :].rearrange("d (h t) -> d h t", h=GH),
                            k_d[part, bass.ds(g * GD, GD), :].rearrange("(h d) t -> d h t", d=DH),
                            ).then_inc(loaded, 16)

            if causal:
                e.dma_start(k_sb[j][SROWS:crow, :], alibi_d[bass.ds(g * al, al), :]).then_inc(loaded, 16)

        def load_v(e, g, j):
            e.dma_start(v_sb[j][:, :, :], v_d[bass.ds(g * P, P), :].rearrange("p (k c) -> p k c", k=8)
                        ).then_inc(v_loaded[j], 16)

        @block.gpsimd
        def _(pool):
            for g in range(SLOTS):
                load_k(pool, g, g, first_loaded[g])

            def parts_of_maxima(g, qh):
                def link(ins, n):
                    ins.then_inc(chain, 1)
                    pool.wait_ge(chain, (g * 2 + qh) * LINKS + (n + 1))

                pool.wait_ge(negated, g * 2 + (qh + 1))
                if not (isinstance(g, int) and (g, qh) == (0, 0)):
                    before = turned_item(g, 0) if qh else turned_item(g - 1, 1)
                    pool.wait_ge(piece_taken, before + 1)
                link(pool.tensor_tensor(cparts[:, 0, :], negm[:, :], zeros[:, :], ALU.subtract), 1)
                link(pool.tensor_tensor(rest[:, :], negm[:, :], cparts[:, 0, :], ALU.subtract), 2)
                link(pool.tensor_tensor(cparts[:, 1, :], rest[:, :], zeros[:, :], ALU.subtract), 3)
                pool.tensor_tensor(cparts[:, 2, :], rest[:, :], cparts[:, 1, :],
                                   ALU.subtract).then_inc(parts_ready, 1)

            pool.memset(zeros[:, :], 0.0).then_inc(chain, 1)
            pool.wait_ge(chain, 1)
            for qh in range(2):
                parts_of_maxima(0, qh)
            with pool.Fori(0, NG - 2) as turn:
                for qh in range(2):
                    parts_of_maxima(turn + 1, qh)
            for qh in range(2):
                parts_of_maxima(NG - 1, qh)

        @block.sync
        def _(sp):
            def load(g, j):
                load_q(sp, g, j)
                load_k(sp, g, j, qk_loaded[j])
                load_v(sp, g, j)

            def shift_rows(g, j, qh):
                sp.wait_ge(piece_taken, turned_item(g, qh) + 1)
                half = slice(qh * GH * CHUNK, (qh + 1) * GH * CHUNK)
                sp.dma_start(q_sb[j][crow:rows, half].rearrange("w (n t) -> w n t", t=P),
                             cturned[:, :]).then_inc(shift_loaded, 16)

            def store(s, qh):
                sp.wait_ge(out_copied, 2 * s + qh + 1)
                sp.dma_start(z_d[qh, bass.ds(s * GH, GH), :], o_sb[DH:P:VW, qh, :]).then_inc(out_stored[qh], 16)
                half = slice(qh * CHUNK, (qh + 1) * CHUNK)
                for h in range(GH):
                    sp.dma_start(o_d[bass.ds(s * GD + h * DH, DH), half],
                                 o_sb[VW * h:VW * h + DH, qh, :]).then_inc(out_stored[qh], 16)

            def step(s, j, ahead=True, loads=True):
                shift_rows(s, j, 1)
                if loads:
                    sp.wait_ge(pv_done, s * NU)
                    load(s + (SLOTS - 1), (j + SLOTS - 1) % SLOTS)
                store(s, 0)
                if ahead:
                    shift_rows(s + 1, (j + 1) % SLOTS, 0)
                store(s, 1)

            for g in range(SLOTS):
                load_q(sp, g, g)
                sp.dma_start(k_sb[g][crow:rows, :], ones_d[0:3, :]).then_inc(rows_set, 16)
                if causal:
                    sp.dma_start(q_sb[g][SROWS:crow, :], ones_d[0:al, :]).then_inc(rows_set, 16)
                load_v(sp, g, g)
            shift_rows(0, 0, 0)
            step(0, 0, loads=False)
            with sp.Fori(0, LOOPED // SLOTS) as turn:
                for n in range(SLOTS):
                    step(turn * SLOTS + (n + PEELED_FRONT), (n + PEELED_FRONT) % SLOTS)
            for s in range(PEELED_FRONT + LOOPED, NG):
                step(s, s % SLOTS, ahead=s + 1 < NG, loads=s + SLOTS - 1 < NG)
                if s == NG - 3:
                    for qh in range(2):
                        sp.wait_ge(out_stored[qh], STORES * (s + 1))
                    output.load_denominators(sp, 0)
                if s == NG - 2:
                    output.store_reciprocals(sp, 0)
                    output.load(sp, 0)
            for qh in range(2):
                sp.wait_ge(out_stored[qh], STORES * NG)

        @block.tensor
        def _(pe):
            def loads(turn, n):
                return n // SLOTS + 1 if turn is None else turn + (n // SLOTS + 1)

            def maxima(g, j, lo, hi, turn, n):
                for i in range(lo, hi):
                    h, qt, half, keys = pieces[i]
                    bank = bank_of(g, j, i)
                    if i == 0:
                        pe.wait_ge(first_loaded[j], K_LOAD)
                        pe.wait_ge(qk_loaded[j], loads(turn, n) * LOAD - K_LOAD)
                    wait_past(pe, piece_taken, item(g, i) + (1 - MXB))
                    at = (qt // 4 * GH + h) * CHUNK + qt % 4 * P
                    q = q_sb[j][0:crow, at:at + P]
                    k = k_sb[j][0:crow, h * S + half * CHUNK:h * S + half * CHUNK + keys]
                    diagonal = causal and half == qt // 4
                    if diagonal:
                        pe.matmul(ps_m[:, bank, keys - P:keys], consts["ident_bf"][:, :],
                                  consts["mask_qk"][:, :], start=True, stop=False, skip_group_check=True)
                    pe.matmul(ps_m[:, bank, 0:keys], q, k, start=not diagonal, stop=True,
                              skip_group_check=diagonal).then_inc(piece_ready, 1)

            def turn_maxima(g, j, qh):
                pe.wait_ge(parts_ready, g * 2 + (qh + 1))
                pe.wait_ge(piece_taken, turned_item(g, qh) + (1 - MXB))
                pe.matmul(ps_m[0:3 * ROWS_H, turned_bank(g, j, qh), 0:P], cparts[:, :, :].rearrange("p w n -> p (w n)"),
                          consts["ident_bf"][:, :], start=True, stop=True).then_inc(piece_ready, 1)

            def turns_due(g, j, share):
                if share == 0 and not (isinstance(g, int) and g == 0):
                    turn_maxima(g - 1, (j - 1) % SLOTS, 1)
                if share == NPH:
                    turn_maxima(g, j, 0)

            def scores(s, j, u, pair):
                qh, kt = units[u]
                off = max(0, P * kt - CHUNK * qh) if causal else 0
                diagonal = causal and P * kt >= CHUNK * qh
                if u == first_of[qh] and pair == 0:
                    pe.wait_ge(shift_loaded, s * (2 * SHIFT) + SHIFT * (qh + 1))
                wait_past(pe, exp_done, s * NT + (2 * u + pair - 1))
                for h in (2 * pair, 2 * pair + 1):
                    k = k_sb[j][0:rows, h * S + kt * P:h * S + (kt + 1) * P]
                    q = q_sb[j][0:rows, (qh * GH + h) * CHUNK + off:(qh * GH + h + 1) * CHUNK]
                    if diagonal:
                        pe.matmul(ps_s[:, h, off:off + P], consts["ident_bf"][:, :],
                                  consts["mask_kq"][:, :], start=True, stop=False, skip_group_check=True)
                    mm = pe.matmul(ps_s[:, h, off:CHUNK], k, q, start=not diagonal, stop=True,
                                   skip_group_check=diagonal)
                mm.then_inc(score_ready, 1)

            def values(s, j, u, turn, n):
                qh, kt = units[u]
                off = max(0, P * kt - CHUNK * qh) if causal else 0
                pe.wait_ge(exp_done, s * NT + (2 * u + 2))
                if u == 0:
                    pe.wait_ge(v_loaded[j], loads(turn, n) * 16)
                if u == first_of[qh]:
                    wait_past(pe, out_copied, 2 * s + qh)
                for h in range(GH):
                    mm = pe.matmul(ps_o[VW * h:VW * (h + 1), off:CHUNK], v_sb[j][:, kt, VW * h:VW * (h + 1)],
                                   p_sb[:, (2 * u + h // 2) % NP, h % 2, off:CHUNK],
                                   start=(u == first_of[qh]), stop=(u == last_of[qh]))
                mm.then_inc(pv_done, 1)

            def step(s, j, turn=None, n=0):
                for u in range(NU):
                    past, share = (u + LEAD) // NU, (u + LEAD) % NU * PPU

                    def ahead(lo, hi):
                        if turn is not None or s + past < NG:
                            maxima(s + past, (j + past) % SLOTS, share + lo, share + hi, turn, n + past)
                    scores(s, j, u, 0)
                    ahead(0, PPU // 4)
                    scores(s, j, u, 1)
                    ahead(PPU // 4, PPU // 2)
                    if u:
                        values(s, j, u - 1, turn, n)
                    ahead(PPU // 2, PPU)
                    if turn is not None or s + past < NG or (s + past == NG and share == 0):
                        turns_due(s + past, (j + past) % SLOTS, share)
                values(s, j, NU - 1, turn, n)

            pe.wait_ge(rows_set, SETS)
            for u in range(LEAD):
                g, share = u // NU, u % NU * PPU
                maxima(g, g, share, share + PPU, None, g)
                turns_due(g, g, share)
            step(0, 0)
            with pe.Fori(0, LOOPED // SLOTS) as turn:
                for n in range(PEELED_FRONT, PEELED_FRONT + SLOTS):
                    step(turn * SLOTS + n, n % SLOTS, turn, n)
            for s in range(PEELED_FRONT + LOOPED, NG):
                step(s, s % SLOTS, None, s)

        @block.scalar
        def _(act):
            def copy_out(s, qh):
                act.wait_ge(pv_done, s * NU + (last_of[qh] + 1))
                wait_past(act, out_stored[qh], s * STORES)
                act.activation(o_sb[:, qh, :], ps_o[:, :], ACT.Copy).then_inc(out_copied, 1)

            def step(s):
                for u, (qh, kt) in enumerate(units):
                    off = max(0, P * kt - CHUNK * qh) if causal else 0
                    wait_past(act, pv_done, s * NU + (u - 1))
                    for pair in range(2):
                        act.wait_ge(score_ready, s * NT + (2 * u + pair + 1))
                        act.activation(p_sb[:, (2 * u + pair) % NP, :, off:CHUNK],
                                       ps_s[:, 2 * pair:2 * pair + 2, off:CHUNK], ACT.Exp,
                                       scale=scale).then_inc(exp_done, 1)
                    if u == last_of[0] + 1:
                        copy_out(s, 0)
                copy_out(s, 1)

            step(0)
            with act.Fori(0, LOOPED) as turn:
                step(turn + PEELED_FRONT)
            for s in range(PEELED_FRONT + LOOPED, NG):
                step(s)

        @block.vector
        def _(dve):
            def reduce_piece(g, j, i):
                h, qt, half, keys = pieces[i]
                dve.wait_ge(piece_ready, item(g, i) + 1)
                dve.tensor_reduce(mxp[:, qt // 4, 4 * h + qt % 4, half:half + 1],
                                  ps_m[:, bank_of(g, j, i), 0:keys], AX.X, ALU.max).then_inc(piece_taken, 1)

            def negated_maxima(g, qh):
                dve.wait_ge(piece_taken, item(g, (NPH, NPC)[qh] - 1) + 1)
                wait_past(dve, parts_ready, g * 2 + qh)
                dve.tensor_reduce(negm[:, :], mxp[:, qh, :, :], AX.X, ALU.max, negate=True).then_inc(negated, 1)

            def copy_turned(g, j, qh):
                dve.wait_ge(piece_ready, turned_item(g, qh) + 1)
                wait_past(dve, shift_loaded, g * (2 * SHIFT) + SHIFT * qh)
                dve.tensor_copy(cturned[:, :], ps_m[0:3 * ROWS_H, turned_bank(g, j, qh), 0:P]).then_inc(piece_taken, 1)

            def maxima_unit(g, j, share, live=True):
                if live:
                    for i in range(share * PPU, (share + 1) * PPU):
                        reduce_piece(g, j, i)
                if share == 0 and not (isinstance(g, int) and g == 0):
                    copy_turned(g - 1, (j - 1) % SLOTS, 1)
                if live:
                    if share * PPU == NPH:
                        copy_turned(g, j, 0)
                    if (share + 1) * PPU in (NPH, NPC):
                        negated_maxima(g, int((share + 1) * PPU == NPC))

            def step(s, j, looped=False):
                for u in range(LEAD, NU + LEAD):
                    past = u // NU
                    if looped or s + past < NG or (s + past == NG and u % NU == 0):
                        maxima_unit(s + past, (j + past) % SLOTS, u % NU, looped or s + past < NG)

            dve.memset(mxp[:, :, :, :], LOWEST).then_inc(filled, 1)
            dve.wait_ge(filled, 1)
            for u in range(LEAD):
                maxima_unit(u // NU, u // NU, u % NU)
            step(0, 0)
            with dve.Fori(0, LOOPED // SLOTS) as turn:
                for n in range(SLOTS):
                    step(turn * SLOTS + (n + PEELED_FRONT), (n + PEELED_FRONT) % SLOTS, True)
            for s in range(PEELED_FRONT + LOOPED, NG):
                step(s, s % SLOTS)
                if s == NG - 3:
                    output.reciprocals(dve, 0)
            output.scale(dve, 0)


def bank_plan(tasks):
    return {task: (n % BANKS, n // BANKS) for n, task in enumerate(tasks)}


class Banks:

    def __init__(self, nc, ctx, tag, tasks):
        self.place = bank_plan(tasks)
        self.done = 0
        assert len(self.place) == len(tasks)
        self.ps = ctx.enter_context(nc.psum_tensor(f"{tag}_ps", [P, BANKS, CHUNK], F32))
        self.filled = ctx.enter_context(nc.semaphore(f"{tag}_filled"))
        self.drained = [ctx.enter_context(nc.semaphore(f"{tag}_drained{b}")) for b in range(BANKS)]

    def out(self, task):
        return self.ps[:, self.place[task][0], :]

    def wait_empty(self, pe, task):
        bank, before = self.place[task]
        if before:
            pe.wait_ge(self.drained[bank], before)

    def wait_full(self, e, task):
        bank, before = self.place[task]
        e.wait_ge(self.filled, before * BANKS + bank + 1)

    def wait_drained(self, e, task):
        bank, before = self.place[task]
        e.wait_ge(self.drained[bank], before + 1)

    def fill(self, task):
        bank, before = self.place[task]
        assert before * BANKS + bank == self.done, task
        self.done += 1
        return self.filled

    def drain(self, task):
        return self.drained[self.place[task][0]]


PARTS = 4


def store_parts(sp, q_d, k_d, c, i, parts, sem):
    b, half = c // 2, c % 2
    if i < KC:
        for n in range(P // GD):
            row = ((b * GPB + i * (P // GD) + n) * 2 + half) * GD
            sp.dma_start(q_d[:, row:row + GD, :].rearrange("w d t -> d w t"),
                         parts[n * GD:(n + 1) * GD]).then_inc(sem, 16)
    else:
        row = b * D + (i - KC) * P
        sp.dma_start(k_d[:, row:row + P, half * CHUNK:(half + 1) * CHUNK].rearrange("w d t -> d w t"),
                     parts).then_inc(sem, 16)


def stored_counts(uses):
    return 16 * (uses + (uses + 1) // 2)


class Norm:

    def __init__(self, nc, ctx, tag, x_sb, consts):
        def sb(name, shape):
            return ctx.enter_context(nc.sbuf_tensor(f"{tag}_{name}", shape, F32))

        def sem(name):
            return ctx.enter_context(nc.semaphore(f"{tag}_{name}"))
        self.x_sb, self.minus_half = x_sb, consts["minus_half"]
        self.stats = sb("stats", [P, TPC, 6])
        self.mv = sb("mv", [P, TPC, 2])
        self.var = sb("var", [P, TPC])
        self.rstd = sb("rstd", [P, TPC])
        self.xn = sb("xn", [P, 2, TPC, D])
        self.steps = sem("norm_steps")
        self.var_ready = sem("var_ready")
        self.rstd_ready = sem("rstd_ready")
        self.xn_ready = sem("xn_ready")
        self.PER = 2 * TPC + TPC

    def vector(self, dve, nth, c):
        base = nth * 2 * TPC
        for t in range(TPC):
            dve.bn_stats(self.stats[:, t, :], self.x_sb[:, c * TPC + t, :]).then_inc(self.steps, 1)
        for t in range(TPC):
            dve.wait_ge(self.steps, base + t + 1)
            dve.bn_aggr(self.mv[:, t, :], self.stats[:, t, :]).then_inc(self.steps, 1)
        dve.wait_ge(self.steps, base + 2 * TPC)
        dve.tensor_scalar(self.var[:, :], self.mv[:, :, 1], EPS, None, ALU.add).then_inc(self.var_ready, 1)
        dve.wait_ge(self.rstd_ready, nth + 1)
        for t in range(TPC):
            dve.tensor_scalar(self.xn[:, nth % 2, t, :], self.x_sb[:, c * TPC + t, :], self.mv[:, t, 0:1],
                              self.rstd[:, t:t + 1], ALU.subtract, ALU.mult).then_inc(self.xn_ready, 1)

    def gpsimd(self, pool, nth):
        pool.wait_ge(self.var_ready, nth + 1)
        pool.tensor_tensor(self.rstd[:, :], self.var[:, :], self.minus_half[:, 0:TPC],
                           ALU.pow).then_inc(self.rstd_ready, 1)

    def transposes(self, pe, banks, nth, tasks, ident):
        for kc, task in enumerate(tasks):
            banks.wait_empty(pe, task)
            for t in range(TPC):
                if kc == 0:
                    pe.wait_ge(self.xn_ready, nth * TPC + t + 1)
                mm = pe.transpose(banks.out(task)[:, t * P:(t + 1) * P],
                                  self.xn[:, nth % 2, t, kc * P:(kc + 1) * P], ident[:, :])
            mm.then_inc(banks.fill(task), 1)


def project_a(nc, env):
    x_sb, w, consts = env["x_sb"], env["w"], env["consts"]
    order = ["loraB"] + [("fold", kc) for kc in range(KC)]
    turn_tasks = {c: [("turn", c, kc) for kc in range(KC)] for c in range(NC)}
    order += turn_tasks[0]
    for c in range(NC):
        order += [("q", c, m) for m in range(KC)] + [("latent", c)]
        order += turn_tasks[c + 1] if c + 1 < NC else []
        order += [("rotated", c, m) for m in range(KC)]
        order += [("k", c, m) for m in range(KC)]
        order += [("v", c, t) for t in range(TPC)]
        order += [("rotated", c, KC + m) for m in range(KC)]
    MIX = 3
    PT = 2 * KC

    def plain_task(c, i):
        return ("q", c, i) if i < KC else ("k", c, i - KC)

    with ExitStack() as ctx:
        def sb(name, shape, dt=F32):
            return ctx.enter_context(nc.sbuf_tensor(f"pa_{name}", shape, dt))

        def sem(name):
            return ctx.enter_context(nc.semaphore(f"pa_{name}"))

        banks = Banks(nc, ctx, "pa", order)
        norm = Norm(nc, ctx, "pa", x_sb, consts)
        w_raw = w["proj"]
        lora_a = sb("lora_a", [RANKS, D])
        lora_b = sb("lora_b", [P, KC, RANKS])
        lora_bt = sb("lora_bt", [RANKS, D])
        coef = sb("coef", [RANKS, 1])
        cos = sb("cos", [P, S])
        sin = sb("sin", [P, S])
        rot = sb("rot", [P, P])
        xnt = sb("xnt", [P, 2, KC, CHUNK])
        latent = sb("latent", [LATENT, 2, CHUNK])
        plain = sb("plain", [P, PT, CHUNK])
        by_cos = sb("by_cos", [P, MIX, CHUNK])
        by_sin = sb("by_sin", [P, CHUNK])
        roped = sb("roped", [P, MIX, CHUNK])
        rest = sb("rest", [P, MIX, CHUNK])
        parts = sb("parts", [P, PARTS, 3, CHUNK], BF16)
        vt = sb("vt", [P, 2, H, VW])

        x_loaded = [sem(f"x_loaded{c}") for c in range(NC)]
        lora_loaded = sem("lora_loaded")
        w_loaded = sem("w_loaded")
        attn_loaded = sem("attn_loaded")
        table_loaded = sem("table_loaded")
        late_loaded = sem("late_loaded")
        ones_set = sem("ones_set")
        cos_ready = sem("cos_ready")
        roped_ready = sem("roped_ready")
        high_ready = sem("high_ready")
        rest_ready = sem("rest_ready")
        middle_ready = sem("middle_ready")
        low_ready = sem("low_ready")
        parts_stored = [sem(f"parts_stored{i}") for i in range(PARTS)]
        v_stored = [sem(f"v_stored{i}") for i in range(2)]

        block = ctx.enter_context(nc.Block())

        @block.sync
        def _(sp):
            for c in range(NC):
                sp.dma_start(x_sb[:, c * TPC:(c + 1) * TPC, :],
                             env["x"][c * CHUNK:(c + 1) * CHUNK, :].rearrange("(t p) d -> p t d", p=P)
                             ).then_inc(x_loaded[c], 16)
                if c == 0:
                    for ot in range(KC):
                        sp.dma_start(lora_b[:, ot, :].rearrange("p (n r) -> p n r", r=DH),
                                     env["lora_B"][:, ot * P:(ot + 1) * P, :].rearrange("n o r -> o n r")
                                     ).then_inc(lora_loaded, 16)
                    sp.dma_start(lora_a[:, :], env["lora_A"].rearrange("n r d -> (n r) d")).then_inc(lora_loaded, 16)
                    sp.dma_start(coef[:, :], env["lora_weights"].rearrange("(n a b) -> n a b", a=1, b=1)
                                 .broadcast_to([RANKS // DH, DH, 1])).then_inc(lora_loaded, 16)
                    sp.dma_start(w_raw[:, :, :], env["W"].rearrange("(o p) d -> p o d", p=P)).then_inc(w_loaded, 16)
                    sp.dma_start(w["q"][:, :, :], env["Wq"].rearrange("(k p) n -> p k n", p=P)).then_inc(attn_loaded, 16)
                    sp.dma_start(w["c"][:, :, :], env["Wc"].rearrange("(k p) n -> p k n", p=P)).then_inc(attn_loaded, 16)
                    sp.dma_start(w["k"][:, :], env["Wk"]).then_inc(attn_loaded, 16)
                    sp.dma_start(w["v"][:, :], env["Wv"]).then_inc(attn_loaded, 16)
                    for t, name in ((cos, "cos"), (sin, "sin"), (rot, "rot")):
                        sp.dma_start(t[:, :], env[name]).then_inc(table_loaded, 16)
            late = [
                (w["o"][:, :, :], env["Wo"].rearrange("(k p) n -> p k n", p=P)),
                (w["qkv"][:, :, :], env["w_attn"].rearrange("(k p) n -> p k n", p=P)),
                (w["proj"][:, :, :], env["w_proj"].rearrange("(k p) n -> p k n", p=P)),
                (w["bv"][:, :], env["b_attn"][2 * D:3 * D].partition_broadcast(P)),
                (w["bias"][:, :], env["bias"].partition_broadcast(P)),
                (w["bproj"][:, :], env["b_proj"].partition_broadcast(P)),
            ]
            n_v = 0
            for c in range(NC):
                b, half = c // 2, c % 2

                def store_v():
                    for t in range(TPC):
                        n = c * TPC + t
                        banks.wait_drained(sp, ("v", c, t))
                        sp.dma_start(
                            env["va_d"].rearrange("(g p) (k c) -> p g k c", p=P, k=8)[
                                :, b * GPB:(b + 1) * GPB, half * TPC + t, :],
                            vt[:, n % 2, :, :].rearrange("p (g h) c -> p g (h c)", h=GH)).then_inc(v_stored[n % 2], 16)
                for i in range(PT):
                    n = c * PT + i
                    sp.wait_ge(low_ready, n + 1)
                    store_parts(sp, env["qa_d"], env["ka_d"], c, i, parts[:, n % PARTS, :, :],
                                parts_stored[n % PARTS])
                    if i == 1:
                        store_v()
                    if c == 0 and i == 0:
                        banks.wait_full(sp, ("fold", KC - 1))
                        for dst, src in late:
                            sp.dma_start(dst, src).then_inc(late_loaded, 16)
                        sp.dma_start(w["bqk"][:, :], env["b_attn"][0:2 * D].rearrange("(m p) -> p m", p=P),
                                     allow_slow_non_contiguous=True).then_inc(late_loaded, 16)
            for i in range(PARTS):
                sp.wait_ge(parts_stored[i], stored_counts(NC * PT // PARTS))
            for i in range(2):
                sp.wait_ge(v_stored[i], 16 * (NC * TPC // 2))
            sp.wait_ge(late_loaded, 16 * (len(late) + 1))

        @block.tensor
        def _(pe):
            ident = consts["ident"]
            pe.wait_ge(lora_loaded, 16 * (KC + 2))
            for ot in range(KC):
                mm = pe.transpose(banks.out("loraB")[:, ot * P:(ot + 1) * P], lora_b[:, ot, :], ident[:, :])
            mm.then_inc(banks.fill("loraB"), 1)
            banks.wait_drained(pe, "loraB")
            pe.wait_ge(w_loaded, 16)
            for kc in range(KC):
                out = banks.out(("fold", kc))
                for ot in range(KC):
                    pe.matmul(out[:, ot * P:(ot + 1) * P], w_raw[:, ot, kc * P:(kc + 1) * P], ident[:, :],
                              start=(ot == 0), stop=False, skip_group_check=True)
                mm = pe.matmul(out, lora_a[:, kc * P:(kc + 1) * P], lora_bt[:, :], start=False, stop=True,
                               skip_group_check=True)
                mm.then_inc(banks.fill(("fold", kc)), 1)
            norm.transposes(pe, banks, 0, turn_tasks[0], ident)
            pe.wait_ge(attn_loaded, 64)
            pe.wait_ge(table_loaded, 48)
            for c in range(NC):
                def rotated(i):
                    task = ("rotated", c, i)
                    banks.wait_empty(pe, task)
                    banks.wait_drained(pe, plain_task(c, i))
                    pe.matmul(banks.out(task), rot[:, :], plain[:, i, :],
                              start=True, stop=True).then_inc(banks.fill(task), 1)
                for task in turn_tasks[c]:
                    banks.wait_drained(pe, task)
                for m in range(KC):
                    task = ("q", c, m)
                    banks.wait_empty(pe, task)
                    for kc in range(KC):
                        mm = pe.matmul(banks.out(task), w["q"][:, kc, m * P:(m + 1) * P], xnt[:, c % 2, kc, :],
                                       start=(kc == 0), stop=(kc == KC - 1))
                    mm.then_inc(banks.fill(task), 1)
                task = ("latent", c)
                banks.wait_empty(pe, task)
                for kc in range(KC):
                    mm = pe.matmul(banks.out(task)[0:LATENT, :], w["c"][:, kc, :], xnt[:, c % 2, kc, :],
                                   start=(kc == 0), stop=(kc == KC - 1))
                mm.then_inc(banks.fill(task), 1)
                if c + 1 < NC:
                    norm.transposes(pe, banks, c + 1, turn_tasks[c + 1], ident)
                for m in range(KC):
                    rotated(m)
                banks.wait_drained(pe, ("latent", c))
                for m in range(KC):
                    task = ("k", c, m)
                    banks.wait_empty(pe, task)
                    pe.matmul(banks.out(task), w["k"][:, m * P:(m + 1) * P], latent[:, c % 2, :],
                              start=True, stop=True).then_inc(banks.fill(task), 1)
                for t in range(TPC):
                    task = ("v", c, t)
                    banks.wait_empty(pe, task)
                    pe.matmul(banks.out(task), latent[:, c % 2, t * P:(t + 1) * P], w["v"][:, :],
                              start=True, stop=True).then_inc(banks.fill(task), 1)
                for m in range(KC):
                    rotated(KC + m)

        @block.scalar
        def _(act):
            def copy(dst, task):
                banks.wait_full(act, task)
                act.activation(dst, banks.out(task), ACT.Copy).then_inc(banks.drain(task), 1)

            def copy_plain(c, i):
                if c:
                    act.wait_ge(roped_ready, (c - 1) * PT + i + 1)
                copy(plain[:, i, :], plain_task(c, i))

            def high(c, i):
                n = c * PT + i
                if n >= PARTS:
                    act.wait_ge(parts_stored[n % PARTS], stored_counts(n // PARTS))
                act.wait_ge(roped_ready, n + 1)
                act.activation(parts[:, n % PARTS, 0, :], roped[:, n % MIX, :], ACT.Copy).then_inc(high_ready, 1)

            def middle(c, i):
                n = c * PT + i
                act.wait_ge(rest_ready, n + 1)
                act.activation(parts[:, n % PARTS, 1, :], rest[:, n % MIX, :], ACT.Copy).then_inc(middle_ready, 1)

            def turned(c):
                for kc, task in enumerate(turn_tasks[c]):
                    copy(xnt[:, c % 2, kc, :], task)

            for kc in range(KC):
                copy(w["eff"][:, kc, :], ("fold", kc))
            turned(0)
            act.wait_ge(ones_set, 1)
            for c in range(NC):
                for i in range(KC):
                    copy_plain(c, i)
                banks.wait_full(act, ("latent", c))
                act.activation(latent[:, c % 2, :], banks.out(("latent", c))[0:LATENT, :],
                               ACT.Copy).then_inc(banks.drain(("latent", c)), 1)
                if c + 1 < NC:
                    turned(c + 1)
                for i in range(KC):
                    high(c, i)
                    if i:
                        middle(c, i - 1)
                    copy_plain(c, KC + i)
                for t in range(TPC):
                    n = c * TPC + t
                    if n >= 2:
                        act.wait_ge(v_stored[n % 2], 16 * (n // 2))
                    task = ("v", c, t)
                    banks.wait_full(act, task)
                    act.activation(vt[:, n % 2, :, 0:DH], banks.out(task).rearrange("p (h d) -> p h d", d=DH),
                                   ACT.Copy).then_inc(banks.drain(task), 1)
                for i in range(KC, PT):
                    high(c, i)
                    middle(c, i - 1)
                middle(c, PT - 1)

        @block.gpsimd
        def _(pool):
            pool.memset(vt[:, :, :, :], 1.0).then_inc(ones_set, 1)

            def times_cos(c, i):
                n = c * PT + i
                if n >= MIX:
                    pool.wait_ge(roped_ready, n - MIX + 1)
                if n == 0:
                    pool.wait_ge(table_loaded, 48)
                banks.wait_drained(pool, plain_task(c, i))
                at = (c % 2) * CHUNK
                pool.tensor_tensor(by_cos[:, n % MIX, :], plain[:, i, :], cos[:, at:at + CHUNK],
                                   ALU.mult).then_inc(cos_ready, 1)

            norm.gpsimd(pool, 0)
            norm.gpsimd(pool, 1)
            for c in range(NC):
                for i in range(KC):
                    times_cos(c, i)
                if c + 2 < NC:
                    norm.gpsimd(pool, c + 2)
                for i in range(KC, PT):
                    times_cos(c, i)

        @block.vector
        def _(dve):
            def rope(c, i):
                n = c * PT + i
                task = ("rotated", c, i)
                at = (c % 2) * CHUNK
                banks.wait_full(dve, task)
                if n == 0:
                    dve.wait_ge(table_loaded, 48)
                if n:
                    dve.wait_ge(roped_ready, n)
                dve.tensor_tensor(by_sin[:, :], banks.out(task), sin[:, at:at + CHUNK],
                                  ALU.mult).then_inc(banks.drain(task), 1)
                banks.wait_drained(dve, task)
                dve.wait_ge(cos_ready, n + 1)
                dve.tensor_tensor(roped[:, n % MIX, :], by_cos[:, n % MIX, :], by_sin[:, :],
                                  ALU.add).then_inc(roped_ready, 1)

            def less_high(n):
                dve.wait_ge(high_ready, n + 1)
                dve.tensor_tensor(rest[:, n % MIX, :], roped[:, n % MIX, :], parts[:, n % PARTS, 0, :],
                                  ALU.subtract).then_inc(rest_ready, 1)

            def low(n):
                dve.wait_ge(middle_ready, n + 1)
                dve.tensor_tensor(parts[:, n % PARTS, 2, :], rest[:, n % MIX, :], parts[:, n % PARTS, 1, :],
                                  ALU.subtract).then_inc(low_ready, 1)

            def normalise(c):
                dve.wait_ge(x_loaded[c], 16)
                norm.vector(dve, c, c)

            normalise(0)
            dve.wait_ge(lora_loaded, 16 * (KC + 2))
            banks.wait_full(dve, "loraB")
            dve.tensor_scalar(lora_bt[:, :], banks.out("loraB"), coef[:, 0:1], LORA_SCALE,
                              ALU.mult, ALU.mult).then_inc(banks.drain("loraB"), 1)
            normalise(1)
            for c in range(NC):
                for i in range(PT):
                    n = c * PT + i
                    if i == KC and c + 2 < NC:
                        banks.wait_full(dve, turn_tasks[c][-1])
                        normalise(c + 2)
                    rope(c, i)
                    if i >= 1:
                        less_high(n - 1)
                    if i >= 2:
                        low(n - 2)
                less_high(c * PT + PT - 1)
                low(c * PT + PT - 2)
                low(c * PT + PT - 1)


class Output:

    def __init__(self, nc, ctx, tag, o_d, z_d, rz_d):
        def sb(name, shape):
            return ctx.enter_context(nc.sbuf_tensor(f"{tag}_{name}", shape, F32))

        def sem(name):
            return ctx.enter_context(nc.semaphore(f"{tag}_{name}"))
        self.o_d, self.z_d, self.rz_d = o_d, z_d, rz_d
        self.z_sb = sb("z", [P, NC, P])
        self.rz_sb = sb("rz", [P, NC, P])
        self.o_sb = sb("o_t", [P, 2, KC, CHUNK])
        self.rzt = sb("rzt", [P, KC, CHUNK])
        self.z_loaded = sem("z_loaded")
        self.rz_ready = sem("rz_ready")
        self.rz_stored = sem("rz_stored")
        self.o_loaded = [sem(f"o_loaded{i}") for i in range(2)]
        self.o_scaled = sem("o_scaled")

    @staticmethod
    def heads_of(t, c):
        return t[c % 2, (c // 2) * H:(c // 2 + 1) * H, :].rearrange("h (a t) -> (h a) t", t=P)

    def load_denominators(self, sp, b):
        for c in (2 * b, 2 * b + 1):
            sp.dma_start(self.z_sb[:, c, :], self.heads_of(self.z_d, c)).then_inc(self.z_loaded, 16)

    def reciprocals(self, dve, b):
        dve.wait_ge(self.z_loaded, 32 * (b + 1))
        for c in (2 * b, 2 * b + 1):
            dve.reciprocal(self.rz_sb[:, c, :], self.z_sb[:, c, :]).then_inc(self.rz_ready, 1)

    def store_reciprocals(self, sp, b):
        for c in (2 * b, 2 * b + 1):
            sp.wait_ge(self.rz_ready, c + 1)
            sp.dma_start(self.heads_of(self.rz_d, c), self.rz_sb[:, c, :]).then_inc(self.rz_stored, 16)

    def load(self, sp, c):
        b, half = c // 2, c % 2
        sp.dma_start(self.o_sb[:, c % 2, :, :],
                     self.o_d[b * D:(b + 1) * D, half * CHUNK:(half + 1) * CHUNK].rearrange("(k p) t -> p k t", p=P)
                     ).then_inc(self.o_loaded[c % 2], 16)
        sp.wait_ge(self.rz_stored, 32 * (b + 1))
        if c:
            sp.wait_ge(self.o_scaled, KC * c)
        for kc in range(KC):
            heads = self.rz_d[half, b * H + kc * (P // DH):b * H + (kc + 1) * (P // DH), :]
            sp.dma_start(self.rzt[:, kc, :], heads.unsqueeze(1).broadcast_to([P // DH, DH, CHUNK])
                         ).then_inc(self.o_loaded[c % 2], 16)

    def scale(self, dve, c):
        dve.wait_ge(self.o_loaded[c % 2], 16 * (KC + 1) * (c // 2 + 1))
        for kc in range(KC):
            dve.tensor_tensor(self.o_sb[:, c % 2, kc, :], self.o_sb[:, c % 2, kc, :], self.rzt[:, kc, :],
                              ALU.mult).then_inc(self.o_scaled, 1)


def output_and_ffn(nc, env, tag, output, w_out, out_bias, nxt):
    x_sb, w, consts = env["x_sb"], env["w"], env["consts"]
    STEPS = NC + (2 if nxt else 1)
    MIX, PT = 3, 2 * KC
    f_turns = {c: [("f_turn", c, kc) for kc in range(KC)] for c in range(NC)}
    q_turns = {c: [("q_turn", c, kc) for kc in range(KC)] for c in range(NC)}
    order = []
    for k in range(STEPS):
        if k < NC:
            order += [("o", k, t) for t in range(TPC)]
        if 0 <= k - 1 < NC:
            order += f_turns[k - 1] + [("f", k - 1, t) for t in range(TPC)]
        if nxt and 0 <= k - 2 < NC:
            order += q_turns[k - 2] + [("qk", k - 2, m) for m in range(PT)] + [("v", k - 2, t) for t in range(TPC)]

    with ExitStack() as ctx:
        def sb(name, shape, dt=F32):
            return ctx.enter_context(nc.sbuf_tensor(f"{tag}_{name}", shape, dt))

        def sem(name):
            return ctx.enter_context(nc.semaphore(f"{tag}_{name}"))

        banks = Banks(nc, ctx, tag, order)
        f_norm = Norm(nc, ctx, tag + "_f", x_sb, consts)
        f_xnt = sb("f_xnt", [P, 2, KC, CHUNK])
        added = sem("added")
        out_stored = sem("out_stored")
        if nxt:
            q_norm = Norm(nc, ctx, tag + "_q", x_sb, consts)
            q_xnt = sb("q_xnt", [P, 2, KC, CHUNK])
            rest = sb("rest", [P, MIX, CHUNK])
            parts = sb("parts", [P, PARTS, 3, CHUNK], BF16)
            vt = sb("vt", [P, 2, H, VW])
            ones_set = sem("ones_set")
            high_ready = sem("high_ready")
            middle_ready = sem("middle_ready")
            low_ready = sem("low_ready")
            parts_stored = [sem(f"parts_stored{i}") for i in range(PARTS)]
            v_stored = [sem(f"v_stored{i}") for i in range(2)]
        added_per_chunk = TPC * (2 if out_bias is not None else 1)
        o_added, f_added, n = {}, {}, 0
        for k in range(STEPS):
            if k < NC and out_bias is not None:
                n += TPC
                o_added[k] = n
            if 0 <= k - 1 < NC:
                n += TPC
                f_added[k - 1] = n

        block = ctx.enter_context(nc.Block())

        @block.sync
        def _(sp):
            output.load(sp, 1)
            output.load_denominators(sp, 1)
            output.store_reciprocals(sp, 1)
            for k in range(STEPS):
                if k + 2 < NC:
                    banks.wait_full(sp, ("o", k, TPC - 1))
                    output.load(sp, k + 2)
                c = k - 1
                if not nxt and 0 <= c < NC:
                    for t in range(TPC):
                        sp.wait_ge(added, f_added[c] - TPC + t + 1)
                        row = (c * TPC + t) * P
                        sp.dma_start(env["out"][row:row + P, :], x_sb[:, c * TPC + t, :]).then_inc(out_stored, 16)
                c = k - 2
                if nxt and 0 <= c < NC:
                    b, half = c // 2, c % 2
                    for i in range(PT):
                        n = c * PT + i
                        sp.wait_ge(low_ready, n + 1)
                        store_parts(sp, env["qb_d"], env["kb_d"], c, i, parts[:, n % PARTS, :, :],
                                    parts_stored[n % PARTS])
                    for t in range(TPC):
                        n = c * TPC + t
                        banks.wait_drained(sp, ("v", c, t))
                        sp.dma_start(
                            env["vb_d"].rearrange("(g p) (k c) -> p g k c", p=P, k=8)[
                                :, b * GPB:(b + 1) * GPB, half * TPC + t, :],
                            vt[:, n % 2, :, :].rearrange("p (g h) c -> p g (h c)", h=GH)).then_inc(v_stored[n % 2], 16)
            if nxt:
                for i in range(PARTS):
                    sp.wait_ge(parts_stored[i], stored_counts(NC * PT // PARTS))
                for i in range(2):
                    sp.wait_ge(v_stored[i], 16 * (NC * TPC // 2))
            else:
                sp.wait_ge(out_stored, 16 * TILES)

        @block.tensor
        def _(pe):
            ident = consts["ident"]

            def natural(kind, c, lhs, weights):
                for t in range(TPC):
                    task = (kind, c, t)
                    banks.wait_empty(pe, task)
                    for kc in range(KC):
                        mm = pe.matmul(banks.out(task), lhs(kc)[:, t * P:(t + 1) * P], weights(kc),
                                       start=(kc == 0), stop=(kc == KC - 1))
                    mm.then_inc(banks.fill(task), 1)

            for k in range(STEPS):
                if k < NC:
                    pe.wait_ge(output.o_scaled, KC * (k + 1))
                    natural("o", k, lambda kc: output.o_sb[:, k % 2, kc, :], lambda kc: w_out[:, kc, :])
                c = k - 1
                if 0 <= c < NC:
                    f_norm.transposes(pe, banks, c, f_turns[c], ident)
                    for task in f_turns[c]:
                        banks.wait_drained(pe, task)
                    natural("f", c, lambda kc: f_xnt[:, c % 2, kc, :], lambda kc: w["eff"][:, kc, :])
                c = k - 2
                if nxt and 0 <= c < NC:
                    q_norm.transposes(pe, banks, c, q_turns[c], ident)
                    for task in q_turns[c]:
                        banks.wait_drained(pe, task)
                    for m in range(PT):
                        task = ("qk", c, m)
                        banks.wait_empty(pe, task)
                        for kc in range(KC):
                            mm = pe.matmul(banks.out(task), w["qkv"][:, kc, m * P:(m + 1) * P],
                                           q_xnt[:, c % 2, kc, :], start=(kc == 0), stop=(kc == KC - 1))
                        mm.then_inc(banks.fill(task), 1)
                    natural("v", c, lambda kc: q_xnt[:, c % 2, kc, :], lambda kc: w["qkv"][:, kc, 2 * D:3 * D])

        @block.scalar
        def _(act):
            def turned(xnt, c, tasks):
                for kc, task in enumerate(tasks):
                    banks.wait_full(act, task)
                    act.activation(xnt[:, c % 2, kc, :], banks.out(task), ACT.Copy).then_inc(banks.drain(task), 1)

            def high(c, i):
                n = c * PT + i
                if n >= PARTS:
                    act.wait_ge(parts_stored[n % PARTS], stored_counts(n // PARTS))
                banks.wait_full(act, ("qk", c, i))
                act.activation(parts[:, n % PARTS, 0, :], banks.out(("qk", c, i)), ACT.Identity,
                               bias=w["bqk"][:, i:i + 1]).then_inc(high_ready, 1)

            def middle(c, i):
                n = c * PT + i
                banks.wait_drained(act, ("qk", c, i))
                act.activation(parts[:, n % PARTS, 1, :], rest[:, n % MIX, :], ACT.Copy).then_inc(middle_ready, 1)

            for k in range(STEPS):
                if 0 <= k - 1 < NC:
                    turned(f_xnt, k - 1, f_turns[k - 1])
                c = k - 2
                if nxt and 0 <= c < NC:
                    turned(q_xnt, c, q_turns[c])
                    for i in range(PT):
                        high(c, i)
                        if i:
                            middle(c, i - 1)
                    middle(c, PT - 1)

        @block.gpsimd
        def _(pool):
            if nxt:
                pool.memset(vt[:, :, :, :], 1.0).then_inc(ones_set, 1)
            for k in range(STEPS):
                if k < NC:
                    f_norm.gpsimd(pool, k)
                if nxt and 0 <= k - 1 < NC:
                    q_norm.gpsimd(pool, k - 1)

        @block.vector
        def _(dve):
            def residual(kind, c, bias, counts):
                for t in range(TPC):
                    task, tile = (kind, c, t), x_sb[:, c * TPC + t, :]
                    banks.wait_full(dve, task)
                    dve.tensor_tensor(tile, banks.out(task), tile, ALU.add).then_inc(banks.drain(task), 1)
                for t in range(TPC):
                    task, tile = (kind, c, t), x_sb[:, c * TPC + t, :]
                    banks.wait_drained(dve, task)
                    if bias is not None:
                        dve.tensor_tensor(tile, tile, bias[:, :], ALU.add).then_inc(added, 1)
                if bias is not None:
                    dve.wait_ge(added, counts[c])

            def less_high(c, i):
                n, task = c * PT + i, ("qk", c, i)
                dve.wait_ge(high_ready, n + 1)
                if n >= MIX:
                    dve.wait_ge(low_ready, n - MIX + 1)
                dve.scalar_tensor_tensor(out=rest[:, n % MIX, :], in0=banks.out(task), scalar=w["bqk"][:, i:i + 1],
                                         in1=parts[:, n % PARTS, 0, :], op0=ALU.add,
                                         op1=ALU.subtract).then_inc(banks.drain(task), 1)

            def low(c, i):
                n = c * PT + i
                dve.wait_ge(middle_ready, n + 1)
                dve.tensor_tensor(parts[:, n % PARTS, 2, :], rest[:, n % MIX, :], parts[:, n % PARTS, 1, :],
                                  ALU.subtract).then_inc(low_ready, 1)

            def value(c, t):
                n, task = c * TPC + t, ("v", c, t)
                if n >= 2:
                    dve.wait_ge(v_stored[n % 2], 16 * (n // 2))
                banks.wait_full(dve, task)
                dve.tensor_tensor(vt[:, n % 2, :, 0:DH], banks.out(task).rearrange("p (h d) -> p h d", d=DH),
                                  w["bv"][:, :].rearrange("p (h d) -> p h d", d=DH),
                                  ALU.add).then_inc(banks.drain(task), 1)

            output.reciprocals(dve, 1)
            if nxt:
                dve.wait_ge(ones_set, 1)
            for k in range(STEPS):
                if k + 1 < NC:
                    output.scale(dve, k + 1)
                if k < NC:
                    residual("o", k, out_bias, o_added)
                    if k >= 2:
                        banks.wait_full(dve, f_turns[k - 2][-1])
                    f_norm.vector(dve, k, k)
                c = k - 1
                if 0 <= c < NC:
                    residual("f", c, w["bias"], f_added)
                    if nxt:
                        if c >= 2:
                            banks.wait_full(dve, q_turns[c - 2][-1])
                        q_norm.vector(dve, c, c)
                c = k - 2
                if nxt and 0 <= c < NC:
                    for i in range(PT):
                        less_high(c, i)
                        if i:
                            low(c, i - 1)
                    low(c, PT - 1)
                    for t in range(TPC):
                        value(c, t)


def build(nc, ins, out):
    env = {
        "x": ins["L0_attn_a_hidden_states"].rearrange("b s d -> (b s) d"),
        "out": out.rearrange("b s d -> (b s) d"),
        "Wq": ins["L0_attn_a_Wq"], "Wc": ins["L0_attn_a_Wc"], "Wk": ins["L0_attn_a_Wk"],
        "Wv": ins["L0_attn_a_Wv"], "Wo": ins["L0_attn_a_Wo"],
        "w_attn": ins["L0_attn_b_w_attn"], "b_attn": ins["L0_attn_b_b_attn"],
        "w_proj": ins["L0_attn_b_w_proj"], "b_proj": ins["L0_attn_b_b_proj"],
        "lora_A": ins["L0_ffn_lora_A"], "lora_B": ins["L0_ffn_lora_B"], "W": ins["L0_ffn_W"],
        "bias": ins["L0_ffn_bias"], "lora_weights": ins["L0_ffn_lora_weights"],
        "cos": ins["cos"], "sin": ins["sin"], "rot": ins["rot"],
    }
    for a in "ab":
        env[f"q{a}_d"] = nc.dram_tensor(f"q{a}_parts", [3, 2 * B * D, CHUNK], BF16).ap()
        env[f"k{a}_d"] = nc.dram_tensor(f"k{a}_parts", [3, B * D, S], BF16).ap()
        env[f"v{a}_d"] = nc.dram_tensor(f"v{a}_groups", [NG * P, 8 * GH * VW], F32).ap()
        env[f"o{a}_d"] = nc.dram_tensor(f"o{a}_sums", [B * D, S], F32).ap()
        env[f"z{a}_d"] = nc.dram_tensor(f"z{a}_sums", [2, B * H, CHUNK], F32).ap()
        env[f"rz{a}_d"] = nc.dram_tensor(f"z{a}_reciprocals", [2, B * H, CHUNK], F32).ap()

    with ExitStack() as ctx:
        def sb(name, shape, dt=F32):
            return ctx.enter_context(nc.sbuf_tensor(name, shape, dt))

        env["x_sb"] = sb("x_sb", [P, TILES, D])
        env["w"] = {
            "o": sb("w_o", [P, KC, D]), "eff": sb("w_eff", [P, KC, D]), "qkv": sb("w_qkv", [P, KC, 3 * D]),
            "proj": sb("w_proj", [P, KC, D]), "bqk": sb("b_qk", [P, 2 * KC]), "bv": sb("b_v", [P, D]),
            "bias": sb("b_ffn", [P, D]), "bproj": sb("b_proj", [P, D]),
        }
        consts = env["consts"] = {
            "ident": sb("ident", [P, P]), "minus_half": sb("minus_half", [P, 8]),
            "ident_bf": sb("ident_bf", [P, P], BF16), "mask_qk": sb("mask_qk", [P, P], BF16),
            "mask_kq": sb("mask_kq", [P, P], BF16),
        }
        consts_loaded = ctx.enter_context(nc.semaphore("consts_loaded"))
        names = ("ident", "minus_half", "ident_bf", "mask_qk", "mask_kq")
        with nc.Block() as block:
            @block.sync
            def _(sp):
                for name in names:
                    sp.dma_start(consts[name][:, :], ins[name]).then_inc(consts_loaded, 16)
                sp.wait_ge(consts_loaded, 16 * len(names))

        with ExitStack() as early:
            w = env["w"]
            for name, shape in (("q", [P, KC, D]), ("c", [P, KC, LATENT]), ("k", [LATENT, D]), ("v", [LATENT, D])):
                w[name] = early.enter_context(nc.sbuf_tensor(f"w_{name}", shape, F32))
            project_a(nc, env)
        for a, causal, scale, alibi, w_out, bias in (("a", False, DH ** -0.5, None, w["o"], None),
                                                     ("b", True, 1.0 / DH, ins["alibi"], w["proj"], w["bproj"])):
            with ExitStack() as both:
                output = Output(nc, both, f"out_{a}", env[f"o{a}_d"], env[f"z{a}_d"], env[f"rz{a}_d"])
                attention(nc, a, causal, scale, consts, env[f"q{a}_d"], env[f"k{a}_d"], env[f"v{a}_d"],
                          env[f"o{a}_d"], env[f"z{a}_d"], alibi, ins["ones"], output)
                output_and_ffn(nc, env, "mid" if a == "a" else "fin", output, w_out, bias, a == "a")


def in_parts(x, dtype):
    high = x.astype(dtype)
    middle = (x - high.astype(np.float32)).astype(dtype)
    low = (x - high.astype(np.float32) - middle.astype(np.float32)).astype(dtype)
    return high, middle, low


def shape_constants():
    bf16 = np.dtype("bfloat16")
    inv_freq = (1.0 / np.float32(10000.0) ** (np.arange(0, DH, 2, dtype=np.float32) / np.float32(DH))).astype(np.float32)
    freqs = np.arange(S, dtype=np.float32)[:, None] * inv_freq
    angle = np.concatenate([freqs, freqs], axis=-1).T
    rot = np.zeros((P, P), np.float32)
    for i in range(P):
        if i % DH < DH // 2:
            rot[i + DH // 2, i] = -1.0
        else:
            rot[i - DH // 2, i] = 1.0
    key, query = np.arange(P)[:, None], np.arange(P)[None, :]
    mask_kq = np.where(key > query, NEG, 0.0).astype(np.float32)
    base = 2 ** (-2 ** (-(np.log2(H) - 3)))
    slopes = (base ** np.arange(1, H + 1, dtype=np.float32)).astype(np.float32)
    ramp = (slopes[:, None] * np.float32(DH) * np.arange(S, dtype=np.float32)[None, :]).astype(np.float32)
    parts = np.stack(in_parts(ramp, bf16), axis=1)
    alibi = parts.reshape(GPB, GH, 3, S).transpose(0, 2, 1, 3).reshape(GPB * 3, GH * S)
    return {
        "cos": np.tile(np.cos(angle), (P // DH, 1)).astype(np.float32),
        "sin": np.tile(np.sin(angle), (P // DH, 1)).astype(np.float32),
        "rot": rot,
        "ident": np.eye(P, dtype=np.float32),
        "minus_half": np.full((P, 8), -0.5, np.float32),
        "ident_bf": np.eye(P, dtype=np.float32).astype(bf16),
        "mask_kq": mask_kq.astype(bf16),
        "mask_qk": mask_kq.T.copy().astype(bf16),
        "ones": np.ones((3, GH * S), bf16),
        "alibi": np.concatenate([alibi, alibi]),
    }


NAMES = ["L0_attn_a_hidden_states", "L0_attn_a_Wq", "L0_attn_a_Wc", "L0_attn_a_Wk", "L0_attn_a_Wv",
         "L0_attn_a_Wo", "L0_attn_b_w_attn", "L0_attn_b_b_attn", "L0_attn_b_w_proj", "L0_attn_b_b_proj",
         "L0_ffn_lora_A", "L0_ffn_lora_B", "L0_ffn_W", "L0_ffn_bias", "L0_ffn_lora_weights"]


def kernel(**inputs):
    import concourse.bacc as bacc
    from concourse.bass_utils import run_bass_kernel_spmd

    nc = bacc.Bacc("TRN2", target_bir_lowering=False, num_devices=1)
    host = {name: np.ascontiguousarray(inputs[name]) for name in NAMES}
    host.update(shape_constants())
    arrays, ins = {}, {}
    for name, a in host.items():
        arrays[f"in_{name}"] = a
        ins[name] = nc.dram_tensor(f"in_{name}", a.shape, mybir.dt.from_np(a.dtype), kind="ExternalInput").ap()
    out = nc.dram_tensor("out", (B, S, D), F32, kind="ExternalOutput").ap()
    build(nc, ins, out)
    r = run_bass_kernel_spmd(nc, [arrays], core_ids=[0])
    return r.results[0]["out"]
```

```python
from contextlib import ExitStack

import numpy as np

import concourse.bass as bass
from concourse import mybir

ALU = mybir.AluOpType
ACT = mybir.ActivationFunctionType
AX = mybir.AxisListType
BF16 = mybir.dt.bfloat16
F32 = mybir.dt.float32
F32R = mybir.dt.float32r

P = 128
B, S, D = 2, 1024, 512
H, DH = 32, 16
LATENT = 64
RANKS = 128
T = B * S
TILES = T // P
CHUNK = 512
NC = T // CHUNK
TPC = CHUNK // P
KC = D // P
GH = 4
GPB = H // GH
NG = B * GPB
GD = GH * DH
VW = 32
EPS = 1e-5
LORA_SCALE = 2.0
NEG = -1e30
LOWEST = -3e38
BANKS = 8
Q_PARTS = (0, 0, 0, 1, 1, 2)
K_PARTS = (0, 1, 2, 0, 1, 0)
SROWS = DH * len(Q_PARTS)
SLOTS = 3
PEELED_FRONT = 1
LOOPED = 12


def wait_past(e, sem, value):
    if not isinstance(value, int) or value > 0:
        e.wait_ge(sem, value)


class Slot:

    QK_WORDS = GH * S // 2
    V_WORDS = 8 * GH * VW
    WORDS = 2 * QK_WORDS + V_WORDS

    def __init__(self, memory, rows, v_memory=None):
        self.rows = rows
        self.crow = rows - 3
        self.al = self.crow - SROWS
        n = self.QK_WORDS
        self.q = memory[0:rows, 0:n].bitcast(BF16)
        self.k = memory[0:rows, n:2 * n].bitcast(BF16)
        self.v = (memory[:, 2 * n:self.WORDS] if v_memory is None else v_memory).rearrange("p (k c) -> p k c", k=8)

    def load_q_row(self, e, r, q_d, g, loaded):
        e.dma_start(self.q[DH * r:DH * (r + 1), :].rearrange("d (n t) -> d n t", t=CHUNK),
                    q_d[Q_PARTS[r], bass.ds(g * 2 * GD, 2 * GD), :].rearrange("(n d) t -> d n t", d=DH),
                    ).then_inc(loaded, 16)

    def load_k_row(self, e, r, k_d, g, loaded):
        e.dma_start(self.k[DH * r:DH * (r + 1), :].rearrange("d (h t) -> d h t", h=GH),
                    k_d[K_PARTS[r], bass.ds(g * GD, GD), :].rearrange("(h d) t -> d h t", d=DH),
                    ).then_inc(loaded, 16)

    def load_q(self, e, q_d, g, loaded):
        for r in range(len(Q_PARTS)):
            self.load_q_row(e, r, q_d, g, loaded)

    def load_k(self, e, k_d, g, alibi_d, loaded):
        for r in range(len(K_PARTS)):
            self.load_k_row(e, r, k_d, g, loaded)
        if self.al:
            e.dma_start(self.k[SROWS:self.crow, :], alibi_d[bass.ds(g * self.al, self.al), :]).then_inc(loaded, 16)

    def load_v(self, e, v_d, g, loaded):
        e.dma_start(self.v[:, :, :], v_d[bass.ds(g * P, P), :].rearrange("p (k c) -> p k c", k=8)
                    ).then_inc(loaded, 16)

    def set_rows(self, e, ones_d, done):
        e.dma_start(self.k[self.crow:self.rows, :], ones_d[0:3, :]).then_inc(done, 16)
        if self.al:
            e.dma_start(self.q[SROWS:self.crow, :], ones_d[0:self.al, :]).then_inc(done, 16)

    def count_loads(self, nc, ctx, name):
        self.all_loaded = ctx.enter_context(nc.semaphore(f"{name}_loaded"))

    def load_share(self, e, i, q_d, k_d, v_d, alibi_d, ones_d):
        if i < len(Q_PARTS):
            self.load_q_row(e, i, q_d, 0, self.all_loaded)
            self.load_k_row(e, i, k_d, 0, self.all_loaded)
        elif i == len(Q_PARTS):
            self.load_v(e, v_d, 0, self.all_loaded)
        else:
            self.set_rows(e, ones_d, self.all_loaded)
            if self.al:
                e.dma_start(self.k[SROWS:self.crow, :], alibi_d[0:self.al, :]).then_inc(self.all_loaded, 16)

    def wait_loaded(self, e):
        e.wait_ge(self.all_loaded, 16 * (len(Q_PARTS) + len(K_PARTS) + 2 + (2 if self.al else 0)))


def attention(nc, tag, causal, scale, consts, q_d, k_d, v_d, o_d, z_d, alibi_d, ones_d, memories, first, output, late, to_split):
    units = [(qh, kt) for qh in range(2) for kt in range((4 * (qh + 1)) if causal else 8)]
    NU = len(units)
    pieces = []
    for qh in range(2):
        for h in range(GH):
            for qt in range(4 * qh, 4 * qh + 4):
                for half in range(2):
                    n = min(CHUNK, P * (qt + 1) - CHUNK * half) if causal else CHUNK
                    if n > 0:
                        pieces.append((h, qt, half, n))
    NPC = len(pieces)
    PPU = NPC // NU
    NPH = PPU * sum(qh == 0 for qh, _ in units)
    AHEAD = PPU * (13 if causal else 11)
    columns = [CHUNK - (max(0, P * kt - CHUNK * qh) if causal else 0) for qh, kt in units]
    before_unit = [round(NPC * sum(columns[:u]) / sum(columns)) for u in range(NU + 1)]
    crow, rows = first.crow, first.rows
    ROWS_H = GH * 4
    TPU = 2
    NT = NU * TPU
    NP = 4
    MXB = 3
    K_LOAD = 16 * len(K_PARTS) + (16 if causal else 0)
    LOAD = 16 * len(Q_PARTS) + K_LOAD
    SETS = 16 * (SLOTS - 1) * (2 if causal else 1)
    SHIFT = 16
    ITEMS = NPC + 2
    first_of = {qh: min(u for u in range(NU) if units[u][0] == qh) for qh in range(2)}
    last_of = {qh: max(u for u in range(NU) if units[u][0] == qh) for qh in range(2)}
    LINKS = 3

    def item(g, i):
        if isinstance(g, int) and g == 0 and i < PPU:
            return i
        return g * ITEMS + (i - 1 if i < PPU else i if i < NPH + PPU else i + 1)

    def turned_item(g, qh):
        if qh == 0:
            return g * ITEMS + (NPH + PPU)
        if isinstance(g, int) and g == NG - 1:
            return NG * ITEMS - 1
        return g * ITEMS + (ITEMS - 1 + PPU)

    def at_bank(g, j):
        return g if isinstance(g, int) else j + SLOTS

    def bank_of(g, j, i):
        return item(at_bank(g, j), i) % MXB

    def turned_bank(g, j, qh):
        return turned_item(at_bank(g, j), qh) % MXB

    with ExitStack() as ctx:
        def sb(name, shape, dt):
            return ctx.enter_context(nc.sbuf_tensor(f"{tag}_{name}", shape, dt))

        def sem(name):
            return ctx.enter_context(nc.semaphore(f"{tag}_{name}"))

        memories = memories + [sb(f"slot{n}", [P, Slot.WORDS], F32) for n in range(SLOTS - 1 - len(memories))]
        slots = [first] + [Slot(memory, rows) for memory in memories]
        p_sb = sb("p", [P, NP, 2, CHUNK], F32)
        o_sb, out_stored = output.sums, output.sums_stored
        mxp = sb("mxp", [P, 2, ROWS_H, 2], F32)
        negm = sb("negm", [P, ROWS_H], F32)
        rest = sb("rest", [P, ROWS_H], F32)
        zeros = sb("zeros", [P, ROWS_H], F32)
        cparts = sb("cparts", [P, 3, ROWS_H], BF16)
        cturned = sb("cturned", [3 * ROWS_H, P], BF16)
        ps_s = ctx.enter_context(nc.psum_tensor(f"{tag}_ps_s", [P, 4, CHUNK], F32))
        ps_m = ctx.enter_context(nc.psum_tensor(f"{tag}_ps_m", [P, MXB, CHUNK], F32))
        ps_o = ctx.enter_context(nc.psum_tensor(f"{tag}_ps_o", [P, CHUNK], F32))

        if late:
            late_loaded = sem("late_loaded")
        if to_split:
            w_high_ready = sem("w_high_ready")
            w_split = sem("w_split")
        rows_set = sem("rows_set")
        qk_loaded = [sem(f"qk_loaded{j}") for j in range(SLOTS)]
        first_loaded = [sem(f"first_loaded{j}") for j in range(1, SLOTS)]
        v_loaded = [sem(f"v_loaded{j}") for j in range(SLOTS)]
        piece_ready = sem("piece_ready")
        piece_taken = sem("piece_taken")
        filled = sem("filled")
        negated = sem("negated")
        chain = sem("chain")
        parts_ready = sem("parts_ready")
        shift_loaded = sem("shift_loaded")
        score_ready = sem("score_ready")
        exp_done = sem("exp_done")
        pv_done = sem("pv_done")
        out_copied = sem("out_copied")

        block = ctx.enter_context(nc.Block())

        @block.gpsimd
        def _(pool):
            pool.memset(zeros[:, :], 0.0).then_inc(chain, 1)
            pool.wait_ge(chain, 1)
            slots[1].load_k(pool, k_d, 1, alibi_d, first_loaded[0])

            def parts_of_maxima(g, qh):
                def link(ins, n):
                    ins.then_inc(chain, 1)
                    pool.wait_ge(chain, (g * 2 + qh) * LINKS + (n + 1))

                pool.wait_ge(negated, g * 2 + (qh + 1))
                if not (isinstance(g, int) and (g, qh) == (0, 0)):
                    before = turned_item(g, 0) if qh else turned_item(g - 1, 1)
                    pool.wait_ge(piece_taken, before + 1)
                link(pool.tensor_tensor(cparts[:, 0, :], negm[:, :], zeros[:, :], ALU.subtract), 1)
                link(pool.tensor_tensor(rest[:, :], negm[:, :], cparts[:, 0, :], ALU.subtract), 2)
                link(pool.tensor_tensor(cparts[:, 1, :], rest[:, :], zeros[:, :], ALU.subtract), 3)
                pool.tensor_tensor(cparts[:, 2, :], rest[:, :], cparts[:, 1, :],
                                   ALU.subtract).then_inc(parts_ready, 1)

            for qh in range(2):
                parts_of_maxima(0, qh)
            slots[2].load_k(pool, k_d, 2, alibi_d, first_loaded[1])
            for to, source in late:
                pool.dma_start(to, source).then_inc(late_loaded, 16)
            with pool.Fori(0, NG - 2) as turn:
                for qh in range(2):
                    parts_of_maxima(turn + 1, qh)
            for qh in range(2):
                parts_of_maxima(NG - 1, qh)
            pool.wait_ge(late_loaded, 16 * len(late))
            for n, (whole, high, low_part) in enumerate(to_split):
                pool.wait_ge(w_high_ready, n + 1)
                pool.tensor_tensor(low_part[:, :, :], whole[:, :, :], high[:, :, :].bitcast(F32),
                                   ALU.subtract).then_inc(w_split, 1)
            if to_split:
                pool.wait_ge(w_split, len(to_split))

        @block.sync
        def _(sp):
            def load(g, j):
                slots[j].load_q(sp, q_d, g, qk_loaded[j])
                slots[j].load_k(sp, k_d, g, alibi_d, qk_loaded[j])
                slots[j].load_v(sp, v_d, g, v_loaded[j])

            def shift_rows(g, j, qh):
                sp.wait_ge(piece_taken, turned_item(g, qh) + 1)
                half = slice(qh * GH * CHUNK, (qh + 1) * GH * CHUNK)
                sp.dma_start(slots[j].q[crow:rows, half].rearrange("w (n t) -> w n t", t=P),
                             cturned[:, :]).then_inc(shift_loaded, 16)

            def store(s, qh):
                sp.wait_ge(out_copied, 2 * s + qh + 1)
                sp.dma_start(z_d[qh, bass.ds(s * GH, GH), :], o_sb[DH:P:VW, qh, :]).then_inc(out_stored[qh], 16)
                half = slice(qh * CHUNK, (qh + 1) * CHUNK)
                for h in range(GH):
                    sp.dma_start(o_d[bass.ds(s * GD + h * DH, DH), half],
                                 o_sb[VW * h:VW * h + DH, qh, :]).then_inc(out_stored[qh], 16)

            def step(s, j, ahead=True, loads=True):
                shift_rows(s, j, 1)
                if isinstance(s, int) and s == NG - 2:
                    for qh in range(2):
                        sp.wait_ge(out_stored[qh], output.STORES * s)
                    output.load_denominators(sp, 0)
                if isinstance(s, int) and s == NG - 1:
                    output.store_reciprocals(sp, 0)
                    output.load(sp, 0)
                if loads:
                    sp.wait_ge(pv_done, s * NU)
                    load(s + (SLOTS - 1), (j + SLOTS - 1) % SLOTS)
                store(s, 0)
                if ahead:
                    shift_rows(s + 1, (j + 1) % SLOTS, 0)
                store(s, 1)

            for g in range(1, SLOTS):
                slots[g].set_rows(sp, ones_d, rows_set)
            for g in range(1, SLOTS):
                slots[g].load_q(sp, q_d, g, qk_loaded[g])
                slots[g].load_v(sp, v_d, g, v_loaded[g])
            shift_rows(0, 0, 0)
            step(0, 0, loads=False)
            with sp.Fori(0, LOOPED // SLOTS) as turn:
                for n in range(SLOTS):
                    step(turn * SLOTS + (n + PEELED_FRONT), (n + PEELED_FRONT) % SLOTS)
            for s in range(PEELED_FRONT + LOOPED, NG):
                step(s, s % SLOTS, ahead=s + 1 < NG, loads=s + SLOTS - 1 < NG)

        @block.tensor
        def _(pe):
            def loads(turn, n):
                more = n // SLOTS + (1 if n % SLOTS else 0)
                return more if turn is None else turn + more

            def maxima(g, j, i, turn, n):
                h, qt, half, keys = pieces[i]
                bank = bank_of(g, j, i)
                if i == 0:
                    if j:
                        pe.wait_ge(rows_set, SETS)
                        pe.wait_ge(first_loaded[j - 1], K_LOAD)
                    wait_past(pe, qk_loaded[j], loads(turn, n) * LOAD - (K_LOAD if j else 0))
                wait_past(pe, piece_taken, item(g, i) + (1 - MXB))
                at = (qt // 4 * GH + h) * CHUNK + qt % 4 * P
                q = slots[j].q[0:crow, at:at + P]
                k = slots[j].k[0:crow, h * S + half * CHUNK:h * S + half * CHUNK + keys]
                diagonal = causal and half == qt // 4
                if diagonal:
                    pe.matmul(ps_m[:, bank, keys - P:keys], consts["ident_bf"][:, :],
                              consts["mask_qk"][:, :], start=True, stop=False, skip_group_check=True)
                pe.matmul(ps_m[:, bank, 0:keys], q, k, start=not diagonal, stop=True,
                          skip_group_check=diagonal).then_inc(piece_ready, 1)

            def turn_maxima(g, j, qh):
                pe.wait_ge(parts_ready, g * 2 + (qh + 1))
                pe.wait_ge(piece_taken, turned_item(g, qh) + (1 - MXB))
                pe.matmul(ps_m[0:3 * ROWS_H, turned_bank(g, j, qh), 0:P], cparts[:, :, :].rearrange("p w n -> p (w n)"),
                          consts["ident_bf"][:, :], start=True, stop=True).then_inc(piece_ready, 1)

            def ahead(s, j, lo, hi, turn, n):
                for x in range(lo, hi):
                    past, i = divmod(x, NPC)
                    g, slot = s + past, (j + past) % SLOTS
                    live = turn is not None or g < NG
                    if live:
                        maxima(g, slot, i, turn, n + past)
                    if i == PPU - 1 and (turn is not None or 0 < g <= NG):
                        turn_maxima(g - 1, (slot - 1) % SLOTS, 1)
                    if i == NPH + PPU - 1 and live:
                        turn_maxima(g, slot, 0)

            def scores(s, j, u, pair):
                qh, kt = units[u]
                off = max(0, P * kt - CHUNK * qh) if causal else 0
                diagonal = causal and P * kt >= CHUNK * qh
                if u == first_of[qh] and pair == 0:
                    pe.wait_ge(shift_loaded, s * (2 * SHIFT) + SHIFT * (qh + 1))
                wait_past(pe, exp_done, s * NT + (2 * u + pair - 1))
                for h in (2 * pair, 2 * pair + 1):
                    k = slots[j].k[0:rows, h * S + kt * P:h * S + (kt + 1) * P]
                    q = slots[j].q[0:rows, (qh * GH + h) * CHUNK + off:(qh * GH + h + 1) * CHUNK]
                    if diagonal:
                        pe.matmul(ps_s[:, h, off:off + P], consts["ident_bf"][:, :],
                                  consts["mask_kq"][:, :], start=True, stop=False, skip_group_check=True)
                    mm = pe.matmul(ps_s[:, h, off:CHUNK], k, q, start=not diagonal, stop=True,
                                   skip_group_check=diagonal)
                mm.then_inc(score_ready, 1)

            def values(s, j, u, turn, n):
                qh, kt = units[u]
                off = max(0, P * kt - CHUNK * qh) if causal else 0
                pe.wait_ge(exp_done, s * NT + (2 * u + 2))
                if u == 0:
                    wait_past(pe, v_loaded[j], loads(turn, n) * 16)
                if u == first_of[qh]:
                    wait_past(pe, out_copied, 2 * s + qh)
                for h in range(GH):
                    mm = pe.matmul(ps_o[VW * h:VW * (h + 1), off:CHUNK], slots[j].v[:, kt, VW * h:VW * (h + 1)],
                                   p_sb[:, (2 * u + h // 2) % NP, h % 2, off:CHUNK],
                                   start=(u == first_of[qh]), stop=(u == last_of[qh]))
                mm.then_inc(pv_done, 1)

            def step(s, j, turn=None, n=0):
                for u in range(NU):
                    lo, hi = AHEAD + before_unit[u], AHEAD + before_unit[u + 1]
                    first_cut = lo + (hi - lo + 2) // 4
                    second_cut = first_cut + (hi - lo + 1) // 4
                    scores(s, j, u, 0)
                    ahead(s, j, lo, first_cut, turn, n)
                    scores(s, j, u, 1)
                    ahead(s, j, first_cut, second_cut, turn, n)
                    if u:
                        values(s, j, u - 1, turn, n)
                    ahead(s, j, second_cut, hi, turn, n)
                values(s, j, NU - 1, turn, n)

            ahead(0, 0, 0, AHEAD, None, 0)
            step(0, 0)
            with pe.Fori(0, LOOPED // SLOTS) as turn:
                for n in range(PEELED_FRONT, PEELED_FRONT + SLOTS):
                    step(turn * SLOTS + n, n % SLOTS, turn, n)
            for s in range(PEELED_FRONT + LOOPED, NG):
                step(s, s % SLOTS, None, s)

        @block.scalar
        def _(act):
            def copy_out(s, qh):
                act.wait_ge(pv_done, s * NU + (last_of[qh] + 1))
                wait_past(act, out_stored[qh], s * output.STORES)
                act.activation(o_sb[:, qh, :], ps_o[:, :], ACT.Copy).then_inc(out_copied, 1)

            def step(s):
                for u, (qh, kt) in enumerate(units):
                    off = max(0, P * kt - CHUNK * qh) if causal else 0
                    wait_past(act, pv_done, s * NU + (u - 1))
                    for pair in range(2):
                        act.wait_ge(score_ready, s * NT + (2 * u + pair + 1))
                        act.activation(p_sb[:, (2 * u + pair) % NP, :, off:CHUNK],
                                       ps_s[:, 2 * pair:2 * pair + 2, off:CHUNK], ACT.Exp,
                                       scale=scale).then_inc(exp_done, 1)
                    if u == last_of[0] + 1:
                        copy_out(s, 0)
                copy_out(s, 1)

            step(0)
            with act.Fori(0, LOOPED) as turn:
                step(turn + PEELED_FRONT)
            for s in range(PEELED_FRONT + LOOPED, NG):
                step(s)
                if s == NG - 3 and to_split:
                    act.wait_ge(late_loaded, 16 * len(late))
                    for whole, high, _ in to_split:
                        act.activation(high[:, :, :], whole[:, :, :], ACT.Copy).then_inc(w_high_ready, 1)

        @block.vector
        def _(dve):
            def reduce_piece(g, j, i):
                h, qt, half, keys = pieces[i]
                dve.wait_ge(piece_ready, item(g, i) + 1)
                dve.tensor_reduce(mxp[:, qt // 4, 4 * h + qt % 4, half:half + 1],
                                  ps_m[:, bank_of(g, j, i), 0:keys], AX.X, ALU.max).then_inc(piece_taken, 1)

            def negated_maxima(g, qh):
                dve.wait_ge(piece_taken, item(g, (NPH, NPC)[qh] - 1) + 1)
                wait_past(dve, parts_ready, g * 2 + qh)
                dve.tensor_reduce(negm[:, :], mxp[:, qh, :, :], AX.X, ALU.max, negate=True).then_inc(negated, 1)

            def copy_turned(g, j, qh):
                dve.wait_ge(piece_ready, turned_item(g, qh) + 1)
                wait_past(dve, shift_loaded, g * (2 * SHIFT) + SHIFT * qh)
                dve.tensor_copy(cturned[:, :], ps_m[0:3 * ROWS_H, turned_bank(g, j, qh), 0:P]).then_inc(piece_taken, 1)

            def ahead(s, j, lo, hi, looped=False):
                for x in range(lo, hi):
                    past, i = divmod(x, NPC)
                    g, slot = s + past, (j + past) % SLOTS
                    live = looped or g < NG
                    if live:
                        reduce_piece(g, slot, i)
                    if i == PPU - 1 and (looped or 0 < g <= NG):
                        copy_turned(g - 1, (slot - 1) % SLOTS, 1)
                    if live:
                        if i == NPH + PPU - 1:
                            copy_turned(g, slot, 0)
                        if i + 1 in (NPH, NPC):
                            negated_maxima(g, int(i + 1 == NPC))

            dve.memset(mxp[:, :, :, :], LOWEST).then_inc(filled, 1)
            dve.wait_ge(filled, 1)
            ahead(0, 0, 0, AHEAD)
            ahead(0, 0, AHEAD, AHEAD + NPC)
            with dve.Fori(0, LOOPED // SLOTS) as turn:
                for n in range(PEELED_FRONT, PEELED_FRONT + SLOTS):
                    ahead(turn * SLOTS + n, n % SLOTS, AHEAD, AHEAD + NPC, True)
            for s in range(PEELED_FRONT + LOOPED, NG):
                ahead(s, s % SLOTS, AHEAD, AHEAD + NPC)
                if s == NG - 2:
                    output.reciprocals(dve, 0)
            output.scale(dve, 0)


def bank_plan(tasks):
    return {task: (n % BANKS, n // BANKS) for n, task in enumerate(tasks)}


class Banks:

    def __init__(self, nc, ctx, tag, tasks):
        self.place = bank_plan(tasks)
        self.done = 0
        assert len(self.place) == len(tasks)
        self.ps = ctx.enter_context(nc.psum_tensor(f"{tag}_ps", [P, BANKS, CHUNK], F32))
        self.filled = ctx.enter_context(nc.semaphore(f"{tag}_filled"))
        self.drained = [ctx.enter_context(nc.semaphore(f"{tag}_drained{b}")) for b in range(BANKS)]

    def out(self, task):
        return self.ps[:, self.place[task][0], :]

    def wait_empty(self, pe, task):
        bank, before = self.place[task]
        if before:
            pe.wait_ge(self.drained[bank], before)

    def wait_full(self, e, task):
        bank, before = self.place[task]
        e.wait_ge(self.filled, before * BANKS + bank + 1)

    def wait_drained(self, e, task):
        bank, before = self.place[task]
        e.wait_ge(self.drained[bank], before + 1)

    def fill(self, task):
        bank, before = self.place[task]
        assert before * BANKS + bank == self.done, task
        self.done += 1
        return self.filled

    def drain(self, task):
        return self.drained[self.place[task][0]]


PARTS = 4


def store_parts(sp, q_d, k_d, c, i, parts, sem):
    b, half = c // 2, c % 2
    if i < KC:
        row = b * D + i * P
        sp.dma_start(k_d[:, row:row + P, half * CHUNK:(half + 1) * CHUNK].rearrange("w d t -> d w t"),
                     parts).then_inc(sem, 16)
    else:
        for n in range(P // GD):
            row = ((b * GPB + (i - KC) * (P // GD) + n) * 2 + half) * GD
            sp.dma_start(q_d[:, row:row + GD, :].rearrange("w d t -> d w t"),
                         parts[n * GD:(n + 1) * GD]).then_inc(sem, 16)


def stored_counts(uses):
    return 16 * (uses + uses // 2)


def wait_first_batch(sp, parts_stored, v_stored):
    for i in range(PARTS):
        sp.wait_ge(parts_stored[i], stored_counts(2 * 2 * KC // PARTS))
    for i in range(2):
        sp.wait_ge(v_stored[i], 16 * TPC)


def split_products(pe, out, lhs, rhs, pieces):
    steps = [(kc, a, b) for kc in range(pieces) for a, b in ((0, 0), (0, 1), (1, 0))]
    for n, (kc, a, b) in enumerate(steps):
        mm = pe.matmul(out, lhs[a](kc), rhs[b](kc), start=(n == 0), stop=(n == len(steps) - 1))
    return mm


class Norm:

    def __init__(self, nc, ctx, tag, x_sb, consts):
        def sb(name, shape):
            return ctx.enter_context(nc.sbuf_tensor(f"{tag}_{name}", shape, F32))

        def sem(name):
            return ctx.enter_context(nc.semaphore(f"{tag}_{name}"))
        self.x_sb, self.minus_half = x_sb, consts["minus_half"]
        self.stats = sb("stats", [P, TPC, 6])
        self.mv = sb("mv", [P, TPC, 2])
        self.var = sb("var", [P, TPC])
        self.rstd = sb("rstd", [P, TPC])
        self.xn = sb("xn", [P, TPC, D])
        self.steps = sem("norm_steps")
        self.var_ready = sem("var_ready")
        self.rstd_ready = sem("rstd_ready")
        self.xn_ready = sem("xn_ready")
        self.PER = 2 * TPC + TPC

    def vector(self, dve, nth, c, turned=None):
        base = nth * 2 * TPC
        for t in range(TPC):
            dve.bn_stats(self.stats[:, t, :], self.x_sb[:, c * TPC + t, :]).then_inc(self.steps, 1)
        for t in range(TPC):
            dve.wait_ge(self.steps, base + t + 1)
            dve.bn_aggr(self.mv[:, t, :], self.stats[:, t, :]).then_inc(self.steps, 1)
        dve.wait_ge(self.steps, base + 2 * TPC)
        dve.tensor_scalar(self.var[:, :], self.mv[:, :, 1], EPS, None, ALU.add).then_inc(self.var_ready, 1)
        dve.wait_ge(self.rstd_ready, nth + 1)
        if turned:
            turned()
        for t in range(TPC):
            dve.tensor_scalar(self.xn[:, t, :], self.x_sb[:, c * TPC + t, :], self.mv[:, t, 0:1],
                              self.rstd[:, t:t + 1], ALU.subtract, ALU.mult).then_inc(self.xn_ready, 1)

    def gpsimd(self, pool, nth):
        pool.wait_ge(self.var_ready, nth + 1)
        pool.tensor_tensor(self.rstd[:, :], self.var[:, :], self.minus_half[:, 0:TPC],
                           ALU.pow).then_inc(self.rstd_ready, 1)

    def transposes(self, pe, banks, nth, tasks, ident):
        for kc, task in enumerate(tasks):
            banks.wait_empty(pe, task)
            for t in range(TPC):
                if kc == 0:
                    pe.wait_ge(self.xn_ready, nth * TPC + t + 1)
                mm = pe.transpose(banks.out(task)[:, t * P:(t + 1) * P],
                                  self.xn[:, t, kc * P:(kc + 1) * P], ident[:, :])
            mm.then_inc(banks.fill(task), 1)


def project_a(nc, env, first):
    x_sb, w, consts = env["x_sb"], env["w"], env["consts"]
    order = ["loraB"] + [("fold", kc) for kc in range(KC)]
    turn_tasks = {c: [("turn", c, kc) for kc in range(KC)] for c in range(NC)}
    order += turn_tasks[0]
    for c in range(NC):
        order += [("latent", c), ("q", c, 0)]
        order += [("k", c, m) for m in range(KC)]
        order += [("v", c, t) for t in range(TPC)]
        order += [("rotated", c, m) for m in range(KC)]
        order += turn_tasks[c + 1] if c + 1 < NC else []
        order += [("q", c, 1), ("q", c, 2), ("rotated", c, KC), ("rotated", c, KC + 1), ("q", c, 3),
                  ("rotated", c, KC + 2), ("rotated", c, KC + 3)]
    MIX = 3
    CONSTS = 16 * 5
    PT = 2 * KC

    def plain(i):
        return (w_raw if i < KC else plain_q)[:, i % KC, :]

    def plain_task(c, i):
        return ("k", c, i) if i < KC else ("q", c, i - KC)

    w_raw = w["proj"]
    with ExitStack() as ctx:
        def sb(name, shape, dt=F32):
            return ctx.enter_context(nc.sbuf_tensor(f"pa_{name}", shape, dt))

        def sem(name):
            return ctx.enter_context(nc.semaphore(f"pa_{name}"))

        banks = Banks(nc, ctx, "pa", order)
        norm = Norm(nc, ctx, "pa", x_sb, consts)
        coef = sb("coef", [RANKS, 1])
        cos = sb("cos", [P, S])
        sin = sb("sin", [P, S])
        rot = sb("rot", [P, P])
        xnt = sb("xnt", [P, 2, KC, CHUNK], F32R)
        xnt_low = sb("xnt_low", [P, 2, KC, CHUNK], F32R)
        wq_high, wq_low = sb("wq_high", [P, KC, D], F32R), sb("wq_low", [P, KC, D], F32R)
        wc_high, wc_low = sb("wc_high", [P, KC, LATENT], F32R), sb("wc_low", [P, KC, LATENT], F32R)
        latent = sb("latent", [LATENT, 2, CHUNK])
        early = env["o_memory"][:, :].rearrange("p (n t) -> p n t", t=CHUNK)
        plain_q, by_cos = early[:, 0:KC], early[:, KC:KC + MIX]
        lora_bt = early[:, KC + MIX, :]
        lora_a, lora_b = early[:, 1, :], early[:, 2, :].rearrange("p (k r) -> p k r", k=KC)
        roped = sb("roped", [P, MIX, CHUNK])
        by_sin = w["q"][:, MIX, :]
        vt = w["o"][:, :, :].rearrange("p k (b c) -> p (k b) c", c=VW).rearrange("p (a h) c -> p a h c", a=2)
        rest = w["q"]
        parts = sb("parts", [P, PARTS, 3, CHUNK], BF16)

        consts_loaded = sem("consts_loaded")
        x_loaded = [sem(f"x_loaded{c}") for c in range(NC)]
        lora_loaded = sem("lora_loaded")
        w_loaded = sem("w_loaded")
        attn_loaded = sem("attn_loaded")
        w_high_ready = sem("w_high_ready")
        w_split = sem("w_split")
        x_high_ready = sem("x_high_ready")
        table_loaded = sem("table_loaded")
        late_loaded = sem("late_loaded")
        ones_set = sem("ones_set")
        cos_ready = sem("cos_ready")
        roped_ready = sem("roped_ready")
        high_ready = sem("high_ready")
        rest_ready = sem("rest_ready")
        middle_ready = sem("middle_ready")
        low_ready = sem("low_ready")
        parts_stored = [sem(f"parts_stored{i}") for i in range(PARTS)]
        v_stored = [sem(f"v_stored{i}") for i in range(2)]

        block = ctx.enter_context(nc.Block())

        @block.sync
        def _(sp):
            for name in ("ident", "minus_half", "ident_bf", "mask_qk", "mask_kq"):
                sp.dma_start(consts[name][:, :], env["ins"][name]).then_inc(consts_loaded, 16)
            for c in range(NC):
                sp.dma_start(x_sb[:, c * TPC:(c + 1) * TPC, :],
                             env["x"][c * CHUNK:(c + 1) * CHUNK, :].rearrange("(t p) d -> p t d", p=P)
                             ).then_inc(x_loaded[c], 16)
                if c == 0:
                    for ot in range(KC):
                        sp.dma_start(lora_b[:, ot, :].rearrange("p (n r) -> p n r", r=DH),
                                     env["lora_B"][:, ot * P:(ot + 1) * P, :].rearrange("n o r -> o n r")
                                     ).then_inc(lora_loaded, 16)
                    sp.dma_start(lora_a[:, :], env["lora_A"].rearrange("n r d -> (n r) d")).then_inc(lora_loaded, 16)
                    sp.dma_start(coef[:, :], env["lora_weights"].rearrange("(n a b) -> n a b", a=1, b=1)
                                 .broadcast_to([RANKS // DH, DH, 1])).then_inc(lora_loaded, 16)
                    sp.dma_start(w_raw[:, :, :], env["W"].rearrange("(o p) d -> p o d", p=P)).then_inc(w_loaded, 16)
                    sp.dma_start(w["q"][:, :, :], env["Wq"].rearrange("(k p) n -> p k n", p=P)).then_inc(attn_loaded, 16)
                    sp.dma_start(w["c"][:, :, :], env["Wc"].rearrange("(k p) n -> p k n", p=P)).then_inc(attn_loaded, 16)
                    sp.dma_start(w["k"][:, :], env["Wk"]).then_inc(attn_loaded, 16)
                    sp.dma_start(w["v"][:, :], env["Wv"]).then_inc(attn_loaded, 16)
                    for t, name in ((cos, "cos"), (sin, "sin"), (rot, "rot")):
                        sp.dma_start(t[:, :], env[name]).then_inc(table_loaded, 16)
            late = [
                (w["bv"][:, :], env["b_attn"][2 * D:3 * D].partition_broadcast(P)),
                (w["bias"][:, :], env["bias"].partition_broadcast(P)),
                (w["bproj"][:, :], env["b_proj"].partition_broadcast(P)),
            ]
            n_v = 0
            for c in range(NC):
                b, half = c // 2, c % 2

                def store_v():
                    for t in range(TPC):
                        n = c * TPC + t
                        banks.wait_drained(sp, ("v", c, t))
                        sp.dma_start(
                            env["va_d"].rearrange("(g p) (k c) -> p g k c", p=P, k=8)[
                                :, b * GPB:(b + 1) * GPB, half * TPC + t, :],
                            vt[:, n % 2, :, :].rearrange("p (g h) c -> p g (h c)", h=GH)).then_inc(v_stored[n % 2], 16)
                store_v()
                for i in range(PT):
                    n = c * PT + i
                    sp.wait_ge(low_ready, n + 1)
                    store_parts(sp, env["qa_d"], env["ka_d"], c, i, parts[:, n % PARTS, :, :],
                                parts_stored[n % PARTS])
                    if c == 2:
                        if i == 0:
                            wait_first_batch(sp, parts_stored, v_stored)
                        first.load_share(sp, i, env["qa_d"], env["ka_d"], env["va_d"], None, env["ones"])
                    if c == 0 and i == 0:
                        for dst, src in late:
                            sp.dma_start(dst, src).then_inc(late_loaded, 16)
                        sp.dma_start(w["bqk"][:, :], env["b_attn"][0:2 * D].rearrange("(m p) -> p m", p=P),
                                     allow_slow_non_contiguous=True).then_inc(late_loaded, 16)
            for i in range(PARTS):
                sp.wait_ge(parts_stored[i], stored_counts(NC * PT // PARTS))
            for i in range(2):
                sp.wait_ge(v_stored[i], 16 * (NC * TPC // 2))
            sp.wait_ge(late_loaded, 16 * (len(late) + 1))
            first.wait_loaded(sp)

        @block.tensor
        def _(pe):
            ident = consts["ident"]
            pe.wait_ge(consts_loaded, CONSTS)
            pe.wait_ge(lora_loaded, 16 * (KC + 2))
            for ot in range(KC):
                mm = pe.transpose(banks.out("loraB")[:, ot * P:(ot + 1) * P], lora_b[:, ot, :], ident[:, :])
            mm.then_inc(banks.fill("loraB"), 1)
            banks.wait_drained(pe, "loraB")
            pe.wait_ge(w_loaded, 16)
            for kc in range(KC):
                out = banks.out(("fold", kc))
                for ot in range(KC):
                    pe.matmul(out[:, ot * P:(ot + 1) * P], w_raw[:, ot, kc * P:(kc + 1) * P], ident[:, :],
                              start=(ot == 0), stop=False, skip_group_check=True)
                mm = pe.matmul(out, lora_a[:, kc * P:(kc + 1) * P], lora_bt[:, :], start=False, stop=True,
                               skip_group_check=True)
                mm.then_inc(banks.fill(("fold", kc)), 1)
            norm.transposes(pe, banks, 0, turn_tasks[0], ident)
            pe.wait_ge(attn_loaded, 64)
            pe.wait_ge(w_split, 2)
            pe.wait_ge(table_loaded, 48)
            for c in range(NC):
                def rotated(i):
                    task = ("rotated", c, i)
                    banks.wait_empty(pe, task)
                    banks.wait_drained(pe, plain_task(c, i))
                    pe.matmul(banks.out(task), rot[:, :], plain(i),
                              start=True, stop=True).then_inc(banks.fill(task), 1)
                x_parts = [lambda kc: xnt[:, c % 2, kc, :], lambda kc: xnt_low[:, c % 2, kc, :]]

                def query(m):
                    task = ("q", c, m)
                    banks.wait_empty(pe, task)
                    cols = slice(m * P, (m + 1) * P)
                    split_products(pe, banks.out(task), [lambda kc: wq_high[:, kc, cols], lambda kc: wq_low[:, kc, cols]],
                                   x_parts, KC).then_inc(banks.fill(task), 1)

                for task in turn_tasks[c]:
                    banks.wait_drained(pe, task)
                task = ("latent", c)
                banks.wait_empty(pe, task)
                split_products(pe, banks.out(task)[0:LATENT, :], [lambda kc: wc_high[:, kc, :], lambda kc: wc_low[:, kc, :]],
                               x_parts, KC).then_inc(banks.fill(task), 1)
                query(0)
                banks.wait_drained(pe, ("latent", c))
                for m in range(KC):
                    task = ("k", c, m)
                    banks.wait_empty(pe, task)
                    pe.matmul(banks.out(task), w["k"][:, m * P:(m + 1) * P], latent[:, c % 2, :],
                              start=True, stop=True).then_inc(banks.fill(task), 1)
                for t in range(TPC):
                    task = ("v", c, t)
                    banks.wait_empty(pe, task)
                    pe.matmul(banks.out(task), latent[:, c % 2, t * P:(t + 1) * P], w["v"][:, :],
                              start=True, stop=True).then_inc(banks.fill(task), 1)
                for i in range(KC):
                    rotated(i)
                if c + 1 < NC:
                    norm.transposes(pe, banks, c + 1, turn_tasks[c + 1], ident)
                query(1)
                query(2)
                rotated(KC)
                rotated(KC + 1)
                query(3)
                rotated(KC + 2)
                rotated(KC + 3)

        @block.scalar
        def _(act):
            def copy(dst, task):
                banks.wait_full(act, task)
                act.activation(dst, banks.out(task), ACT.Copy).then_inc(banks.drain(task), 1)

            def copy_plain(c, i):
                if c:
                    act.wait_ge(roped_ready, (c - 1) * PT + i + 1)
                copy(plain(i), plain_task(c, i))

            def high(c, i):
                n = c * PT + i
                if n >= PARTS:
                    act.wait_ge(parts_stored[n % PARTS], stored_counts(n // PARTS))
                act.wait_ge(roped_ready, n + 1)
                act.activation(parts[:, n % PARTS, 0, :], roped[:, n % MIX, :], ACT.Copy).then_inc(high_ready, 1)

            def middle(c, i):
                n = c * PT + i
                act.wait_ge(rest_ready, n + 1)
                act.activation(parts[:, n % PARTS, 1, :], rest[:, n % MIX, :], ACT.Copy).then_inc(middle_ready, 1)

            def turned(c, pieces):
                if c < NC:
                    for kc in pieces:
                        banks.wait_full(act, turn_tasks[c][kc])
                        act.activation(xnt[:, c % 2, kc, :], banks.out(turn_tasks[c][kc]),
                                       ACT.Copy).then_inc(x_high_ready, 1)

            act.wait_ge(attn_loaded, 64)
            act.activation(wq_high[:, :, :], w["q"][:, :, :], ACT.Copy).then_inc(w_high_ready, 1)
            act.activation(wc_high[:, :, :], w["c"][:, :, :], ACT.Copy).then_inc(w_high_ready, 1)
            def chunk_begun(c):
                banks.wait_full(act, ("latent", c))
                act.activation(latent[:, c % 2, :], banks.out(("latent", c))[0:LATENT, :],
                               ACT.Copy).then_inc(banks.drain(("latent", c)), 1)
                copy_plain(c, KC)

            for kc in range(KC):
                copy(w["eff"][:, kc, :], ("fold", kc))
            turned(0, range(KC))
            act.wait_ge(ones_set, 1)
            chunk_begun(0)
            for c in range(NC):
                for i in range(KC):
                    copy_plain(c, i)
                for t in range(TPC):
                    n = c * TPC + t
                    if n >= 2:
                        act.wait_ge(v_stored[n % 2], 16 * (n // 2))
                    task = ("v", c, t)
                    banks.wait_full(act, task)
                    act.activation(vt[:, n % 2, :, 0:DH], banks.out(task).rearrange("p (h d) -> p h d", d=DH),
                                   ACT.Copy).then_inc(banks.drain(task), 1)
                high(c, 0)
                for i in range(1, KC):
                    high(c, i)
                    middle(c, i - 1)
                    if i == 1:
                        turned(c + 1, (0, 1))
                    if i == 2:
                        turned(c + 1, (2, 3))
                        copy_plain(c, KC + 1)
                copy_plain(c, KC + 2)
                copy_plain(c, KC + 3)
                middle(c, KC - 1)
                high(c, KC)
                for i in range(KC + 1, PT):
                    high(c, i)
                    middle(c, i - 1)
                    if i == KC + 1 and c + 1 < NC:
                        chunk_begun(c + 1)
                middle(c, PT - 1)

        @block.gpsimd
        def _(pool):
            pool.memset(vt[:, :, :, :], 1.0).then_inc(ones_set, 1)

            def times_cos(c, i):
                n = c * PT + i
                if n >= MIX:
                    pool.wait_ge(roped_ready, n - MIX + 1)
                if n == 0:
                    pool.wait_ge(table_loaded, 48)
                banks.wait_drained(pool, plain_task(c, i))
                at = (c % 2) * CHUNK
                pool.tensor_tensor(by_cos[:, n % MIX, :], plain(i), cos[:, at:at + CHUNK],
                                   ALU.mult).then_inc(cos_ready, 1)

            pool.wait_ge(consts_loaded, CONSTS)
            norm.gpsimd(pool, 0)
            for n, (whole, high, low) in enumerate(((w["q"], wq_high, wq_low), (w["c"], wc_high, wc_low))):
                pool.wait_ge(w_high_ready, n + 1)
                pool.tensor_tensor(low[:, :, :], whole[:, :, :], high[:, :, :].bitcast(F32), ALU.subtract).then_inc(w_split, 1)
            norm.gpsimd(pool, 1)
            for c in range(NC):
                for i in range(PT):
                    if i == KC + 2 and c + 2 < NC:
                        norm.gpsimd(pool, c + 2)
                    times_cos(c, i)

        @block.vector
        def _(dve):
            def rope(c, i):
                n = c * PT + i
                task = ("rotated", c, i)
                at = (c % 2) * CHUNK
                banks.wait_full(dve, task)
                if n == 0:
                    dve.wait_ge(table_loaded, 48)
                if n:
                    dve.wait_ge(roped_ready, n)
                dve.tensor_tensor(by_sin[:, :], banks.out(task), sin[:, at:at + CHUNK],
                                  ALU.mult).then_inc(banks.drain(task), 1)
                banks.wait_drained(dve, task)
                dve.wait_ge(cos_ready, n + 1)
                dve.tensor_tensor(roped[:, n % MIX, :], by_cos[:, n % MIX, :], by_sin[:, :],
                                  ALU.add).then_inc(roped_ready, 1)

            def less_high(n):
                dve.wait_ge(high_ready, n + 1)
                dve.tensor_tensor(rest[:, n % MIX, :], roped[:, n % MIX, :], parts[:, n % PARTS, 0, :],
                                  ALU.subtract).then_inc(rest_ready, 1)

            def low(n):
                dve.wait_ge(middle_ready, n + 1)
                dve.tensor_tensor(parts[:, n % PARTS, 2, :], rest[:, n % MIX, :], parts[:, n % PARTS, 1, :],
                                  ALU.subtract).then_inc(low_ready, 1)

            def normalise(c):
                dve.wait_ge(x_loaded[c], 16)
                norm.vector(dve, c, c, c and (lambda: banks.wait_full(dve, turn_tasks[c - 1][-1])))

            def turned_low(c):
                for kc, task in enumerate(turn_tasks[c]):
                    dve.wait_ge(x_high_ready, c * KC + kc + 1)
                    dve.tensor_tensor(xnt_low[:, c % 2, kc, :], banks.out(task), xnt[:, c % 2, kc, :].bitcast(F32),
                                      ALU.subtract).then_inc(banks.drain(task), 1)

            normalise(0)
            dve.wait_ge(lora_loaded, 16 * (KC + 2))
            banks.wait_full(dve, "loraB")
            dve.tensor_scalar(lora_bt[:, :], banks.out("loraB"), coef[:, 0:1], LORA_SCALE,
                              ALU.mult, ALU.mult).then_inc(banks.drain("loraB"), 1)
            turned_low(0)
            normalise(1)
            for c in range(NC):
                for i in range(PT):
                    n = c * PT + i
                    if i == KC + 2 and c + 2 < NC:
                        normalise(c + 2)
                    rope(c, i)
                    if i >= 1:
                        less_high(n - 1)
                    if i >= 2:
                        low(n - 2)
                    if i == KC - 1 and c + 1 < NC:
                        turned_low(c + 1)
                less_high(c * PT + PT - 1)
                low(c * PT + PT - 2)
                low(c * PT + PT - 1)


class Output:

    def __init__(self, nc, ctx, tag, o_d, z_d, rz_d, o_memory=None):
        def sb(name, shape):
            return ctx.enter_context(nc.sbuf_tensor(f"{tag}_{name}", shape, F32))

        def sem(name):
            return ctx.enter_context(nc.semaphore(f"{tag}_{name}"))
        self.o_d, self.z_d, self.rz_d = o_d, z_d, rz_d
        self.z_sb = sb("z", [P, NC, P])
        self.rz_sb = sb("rz", [P, NC, P])
        self.o_sb = (sb("o_t", [P, 2 * KC * CHUNK]) if o_memory is None else o_memory
                     )[:, :].rearrange("p (a k t) -> p a k t", a=2, k=KC)
        self.rzt = sb("rzt", [P, KC, CHUNK])
        self.sums = sb("sums", [P, 2, CHUNK])
        self.sums_stored = [sem(f"sums_stored{qh}") for qh in range(2)]
        self.z_loaded = sem("z_loaded")
        self.rz_ready = sem("rz_ready")
        self.rz_stored = sem("rz_stored")
        self.o_loaded = [sem(f"o_loaded{i}") for i in range(2)]
        self.o_scaled = sem("o_scaled")

    STORES = 16 * (GH + 1)

    @staticmethod
    def heads_of(t, c):
        return t[c % 2, (c // 2) * H:(c // 2 + 1) * H, :].rearrange("h (a t) -> (h a) t", t=P)

    def load_denominators(self, sp, b):
        for c in (2 * b, 2 * b + 1):
            sp.dma_start(self.z_sb[:, c, :], self.heads_of(self.z_d, c)).then_inc(self.z_loaded, 16)

    def reciprocals(self, dve, b):
        dve.wait_ge(self.z_loaded, 32 * (b + 1))
        for c in (2 * b, 2 * b + 1):
            dve.reciprocal(self.rz_sb[:, c, :], self.z_sb[:, c, :]).then_inc(self.rz_ready, 1)

    def store_reciprocals(self, sp, b):
        for c in (2 * b, 2 * b + 1):
            sp.wait_ge(self.rz_ready, c + 1)
            sp.dma_start(self.heads_of(self.rz_d, c), self.rz_sb[:, c, :]).then_inc(self.rz_stored, 16)

    def load(self, sp, c):
        b, half = c // 2, c % 2
        sp.dma_start(self.o_sb[:, c % 2, :, :],
                     self.o_d[b * D:(b + 1) * D, half * CHUNK:(half + 1) * CHUNK].rearrange("(k p) t -> p k t", p=P)
                     ).then_inc(self.o_loaded[c % 2], 16)
        sp.wait_ge(self.rz_stored, 32 * (b + 1))
        if c:
            sp.wait_ge(self.o_scaled, KC * c)
        for kc in range(KC):
            heads = self.rz_d[half, b * H + kc * (P // DH):b * H + (kc + 1) * (P // DH), :]
            sp.dma_start(self.rzt[:, kc, :], heads.unsqueeze(1).broadcast_to([P // DH, DH, CHUNK])
                         ).then_inc(self.o_loaded[c % 2], 16)

    def scale(self, dve, c):
        dve.wait_ge(self.o_loaded[c % 2], 16 * (KC + 1) * (c // 2 + 1))
        for kc in range(KC):
            dve.tensor_tensor(self.o_sb[:, c % 2, kc, :], self.o_sb[:, c % 2, kc, :], self.rzt[:, kc, :],
                              ALU.mult).then_inc(self.o_scaled, 1)


def output_and_ffn(nc, env, tag, output, w_out, out_bias, nxt, w_eff, first=None):
    x_sb, w, consts = env["x_sb"], env["w"], env["consts"]
    fast = len(w_out) > 1
    STEPS = NC + (2 if nxt else 1)
    MIX, PT = 3, 2 * KC
    f_turns = {c: [("f_turn", c, kc) for kc in range(KC)] for c in range(NC)}
    q_turns = {c: [("q_turn", c, kc) for kc in range(KC)] for c in range(NC)}
    order = []
    for k in range(STEPS):
        if 0 <= k - 1 < NC:
            order += f_turns[k - 1]
        if k < NC:
            order += [("o", k, t) for t in range(TPC)]
        if nxt and 0 <= k - 2 < NC:
            order += q_turns[k - 2]
        if 0 <= k - 1 < NC:
            order += [("f", k - 1, t) for t in range(TPC)]
        if nxt and 0 <= k - 2 < NC:
            order += [("qk", k - 2, m) for m in range(PT)] + [("v", k - 2, t) for t in range(TPC)]

    with ExitStack() as ctx:
        def sb(name, shape, dt=F32):
            return ctx.enter_context(nc.sbuf_tensor(f"{tag}_{name}", shape, dt))

        def sem(name):
            return ctx.enter_context(nc.semaphore(f"{tag}_{name}"))

        banks = Banks(nc, ctx, tag, order)
        f_norm = Norm(nc, ctx, tag + "_f", x_sb, consts)
        if fast:
            o_parts = [sb(f"o_part{n}", [P, KC, CHUNK], F32R) for n in range(2)]
            o_high_ready = sem("o_high_ready")
            o_split = sem("o_split")
            f_xnt = [sb(f"f_xnt{n}", [P, KC, CHUNK], F32R) for n in range(2)]
        else:
            f_xnt = [sb("f_xnt", [P, KC, CHUNK])]
        turned_high = sem("turned_high")
        added = sem("added")
        out_stored = sem("out_stored")
        if nxt:
            q_norm = Norm(nc, ctx, tag + "_q", x_sb, consts)
            q_xnt = [sb(f"q_xnt{n}", [P, KC, CHUNK], F32R) for n in range(2)]
            w_qkv = [sb(f"w_qkv{n}", [P, KC, 3 * D], F32R) for n in range(2)]
            memory, words = env["slot_memory"], MIX * CHUNK
            rest = memory[:, 0:words].rearrange("p (m t) -> p m t", m=MIX)
            parts = memory[:, words:3 * words].bitcast(BF16).rearrange("p (a w t) -> p a w t", a=PARTS, w=3)
            w_whole = [memory[:, 3 * D * n:3 * D * (n + 1)] for n in range(3)] + [
                       w["proj"][:, :, :].rearrange("p k n -> p (k n)")[:, 0:3 * D]]
            w_loaded = sem("w_loaded")
            w_high_ready = sem("w_high_ready")
            w_split = sem("w_split")
            vt = w["proj"][:, :, :].rearrange("p k (b c) -> p (k b) c", c=VW).rearrange("p (a h) c -> p a h c", a=2)
            ones_set = sem("ones_set")
            high_ready = sem("high_ready")
            middle_ready = sem("middle_ready")
            low_ready = sem("low_ready")
            parts_stored = [sem(f"parts_stored{i}") for i in range(PARTS)]
            v_stored = [sem(f"v_stored{i}") for i in range(2)]
        o_added, f_added, n = {}, {}, 0
        for k in range(STEPS):
            if k < NC and out_bias is not None:
                n += TPC
                o_added[k] = n
            if 0 <= k - 1 < NC:
                n += TPC
                f_added[k - 1] = n

        def bias_of(i):
            return w["bqk"][:, (i + KC) % PT:(i + KC) % PT + 1]

        block = ctx.enter_context(nc.Block())

        @block.sync
        def _(sp):
            output.load(sp, 1)
            for qh in range(2):
                sp.wait_ge(output.sums_stored[qh], output.STORES * NG)
            output.load_denominators(sp, 1)
            if nxt:
                for kc in range(KC):
                    sp.dma_start(w_whole[kc], env["w_attn"][kc * P:(kc + 1) * P, :]).then_inc(w_loaded, 16)
            output.store_reciprocals(sp, 1)
            for k in range(STEPS):
                if k + 2 < NC:
                    banks.wait_full(sp, ("o", k, TPC - 1))
                    output.load(sp, k + 2)
                c = k - 1
                if not nxt and 0 <= c < NC:
                    for t in range(TPC):
                        sp.wait_ge(added, f_added[c] - TPC + t + 1)
                        row = (c * TPC + t) * P
                        sp.dma_start(env["out"][row:row + P, :], x_sb[:, c * TPC + t, :]).then_inc(out_stored, 16)
                c = k - 2
                if nxt and 0 <= c < NC:
                    b, half = c // 2, c % 2
                    for i in range(PT):
                        n = c * PT + i
                        sp.wait_ge(low_ready, n + 1)
                        store_parts(sp, env["qb_d"], env["kb_d"], c, i, parts[:, n % PARTS, :, :],
                                    parts_stored[n % PARTS])
                        if c == 2:
                            if i == 0:
                                wait_first_batch(sp, parts_stored, v_stored)
                            first.load_share(sp, i, env["qb_d"], env["kb_d"], env["vb_d"],
                                             env["ins"]["alibi"], env["ones"])
                    for t in range(TPC):
                        n = c * TPC + t
                        banks.wait_drained(sp, ("v", c, t))
                        sp.dma_start(
                            env["vb_d"].rearrange("(g p) (k c) -> p g k c", p=P, k=8)[
                                :, b * GPB:(b + 1) * GPB, half * TPC + t, :],
                            vt[:, n % 2, :, :].rearrange("p (g h) c -> p g (h c)", h=GH)).then_inc(v_stored[n % 2], 16)
            if nxt:
                first.wait_loaded(sp)
                for i in range(PARTS):
                    sp.wait_ge(parts_stored[i], stored_counts(NC * PT // PARTS))
                for i in range(2):
                    sp.wait_ge(v_stored[i], 16 * (NC * TPC // 2))
            else:
                sp.wait_ge(out_stored, 16 * TILES)

        @block.tensor
        def _(pe):
            ident = consts["ident"]

            def natural(kind, c, lhs, weights, cols=slice(0, D)):
                for t in range(TPC):
                    task = (kind, c, t)
                    banks.wait_empty(pe, task)
                    tokens = slice(t * P, (t + 1) * P)
                    if len(weights) > 1:
                        mm = split_products(pe, banks.out(task), [lambda kc, x=x: x[:, kc, tokens] for x in lhs],
                                            [lambda kc, x=x: x[:, kc, cols] for x in weights], KC)
                    else:
                        for kc in range(KC):
                            mm = pe.matmul(banks.out(task), lhs[0][:, kc, tokens], weights[0][:, kc, cols],
                                           start=(kc == 0), stop=(kc == KC - 1))
                    mm.then_inc(banks.fill(task), 1)

            for k in range(STEPS):
                if 0 <= k - 1 < NC:
                    f_norm.transposes(pe, banks, k - 1, f_turns[k - 1], ident)
                if k < NC:
                    pe.wait_ge(o_split if fast else output.o_scaled, KC * (k + 1))
                    natural("o", k, o_parts if fast else [output.o_sb[:, k % 2]], w_out)
                if nxt and 0 <= k - 2 < NC:
                    q_norm.transposes(pe, banks, k - 2, q_turns[k - 2], ident)
                c = k - 1
                if 0 <= c < NC:
                    for task in f_turns[c]:
                        banks.wait_drained(pe, task)
                    natural("f", c, f_xnt, w_eff)
                c = k - 2
                if nxt and 0 <= c < NC:
                    if c == 0:
                        pe.wait_ge(w_split, KC)
                    for task in q_turns[c]:
                        banks.wait_drained(pe, task)
                    for m in range(PT):
                        task = ("qk", c, m)
                        banks.wait_empty(pe, task)
                        at = (m + KC) % PT * P
                        split_products(pe, banks.out(task), [lambda kc, x=x: x[:, kc, at:at + P] for x in w_qkv],
                                       [lambda kc, x=x: x[:, kc, :] for x in q_xnt], KC).then_inc(banks.fill(task), 1)
                    natural("v", c, q_xnt, w_qkv, slice(2 * D, 3 * D))

        @block.scalar
        def _(act):
            def turned(xnt, tasks):
                for kc, task in enumerate(tasks):
                    banks.wait_full(act, task)
                    act.activation(xnt[0][:, kc, :], banks.out(task),
                                   ACT.Copy).then_inc(turned_high if len(xnt) > 1 else banks.drain(task), 1)

            def high(c, i):
                n = c * PT + i
                if n >= PARTS:
                    act.wait_ge(parts_stored[n % PARTS], stored_counts(n // PARTS))
                banks.wait_full(act, ("qk", c, i))
                act.activation(parts[:, n % PARTS, 0, :], banks.out(("qk", c, i)), ACT.Identity,
                               bias=bias_of(i)).then_inc(high_ready, 1)

            def middle(c, i):
                n = c * PT + i
                banks.wait_drained(act, ("qk", c, i))
                act.activation(parts[:, n % PARTS, 1, :], rest[:, n % MIX, :], ACT.Copy).then_inc(middle_ready, 1)

            if nxt:
                act.wait_ge(w_loaded, 16 * KC)
                for kc in range(KC):
                    act.activation(w_qkv[0][:, kc, :], w_whole[kc], ACT.Copy).then_inc(w_high_ready, 1)
            def output_high(k):
                for kc in range(KC):
                    act.wait_ge(output.o_scaled, KC * k + kc + 1)
                    if k and kc == 0:
                        banks.wait_full(act, ("o", k - 1, TPC - 1))
                    act.activation(o_parts[0][:, kc, :], output.o_sb[:, k % 2, kc, :],
                                   ACT.Copy).then_inc(o_high_ready, 1)

            if fast:
                output_high(0)
            for k in range(STEPS):
                if 0 <= k - 1 < NC:
                    turned(f_xnt, f_turns[k - 1])
                if fast and k + 1 < NC:
                    output_high(k + 1)
                c = k - 2
                if nxt and 0 <= c < NC:
                    turned(q_xnt, q_turns[c])
                    for i in range(PT):
                        high(c, i)
                        if i:
                            middle(c, i - 1)
                    middle(c, PT - 1)

        @block.gpsimd
        def _(pool):
            for k in range(STEPS):
                if nxt and k == 2:
                    pool.wait_ge(w_split, KC)
                    pool.memset(vt[:, :, :, :], 1.0).then_inc(ones_set, 1)
                if k < NC:
                    f_norm.gpsimd(pool, k)
                if nxt and 0 <= k - 1 < NC:
                    q_norm.gpsimd(pool, k - 1)

        @block.vector
        def _(dve):
            def residual(kind, c, bias, counts):
                for t in range(TPC):
                    task, tile = (kind, c, t), x_sb[:, c * TPC + t, :]
                    banks.wait_full(dve, task)
                    dve.tensor_tensor(tile, banks.out(task), tile, ALU.add).then_inc(banks.drain(task), 1)
                for t in range(TPC):
                    task, tile = (kind, c, t), x_sb[:, c * TPC + t, :]
                    banks.wait_drained(dve, task)
                    if bias is not None:
                        dve.tensor_tensor(tile, tile, bias[:, :], ALU.add).then_inc(added, 1)
                if bias is not None:
                    dve.wait_ge(added, counts[c])

            def less_high(c, i):
                n, task = c * PT + i, ("qk", c, i)
                dve.wait_ge(high_ready, n + 1)
                if n >= MIX:
                    dve.wait_ge(low_ready, n - MIX + 1)
                dve.scalar_tensor_tensor(out=rest[:, n % MIX, :], in0=banks.out(task), scalar=bias_of(i),
                                         in1=parts[:, n % PARTS, 0, :], op0=ALU.add,
                                         op1=ALU.subtract).then_inc(banks.drain(task), 1)

            def low(c, i):
                n = c * PT + i
                dve.wait_ge(middle_ready, n + 1)
                dve.tensor_tensor(parts[:, n % PARTS, 2, :], rest[:, n % MIX, :], parts[:, n % PARTS, 1, :],
                                  ALU.subtract).then_inc(low_ready, 1)

            def value(c, t):
                n, task = c * TPC + t, ("v", c, t)
                if n >= 2:
                    dve.wait_ge(v_stored[n % 2], 16 * (n // 2))
                banks.wait_full(dve, task)
                dve.tensor_tensor(vt[:, n % 2, :, 0:DH], banks.out(task).rearrange("p (h d) -> p h d", d=DH),
                                  w["bv"][:, :].rearrange("p (h d) -> p h d", d=DH),
                                  ALU.add).then_inc(banks.drain(task), 1)

            def turned_low(xnt, nth, tasks):
                for kc, task in enumerate(tasks):
                    dve.wait_ge(turned_high, nth * KC + kc + 1)
                    dve.tensor_tensor(xnt[1][:, kc, :], banks.out(task), xnt[0][:, kc, :].bitcast(F32),
                                      ALU.subtract).then_inc(banks.drain(task), 1)

            def output_low(k):
                for kc in range(KC):
                    dve.wait_ge(o_high_ready, KC * k + kc + 1)
                    dve.tensor_tensor(o_parts[1][:, kc, :], output.o_sb[:, k % 2, kc, :],
                                      o_parts[0][:, kc, :].bitcast(F32), ALU.subtract).then_inc(o_split, 1)

            if fast:
                output_low(0)
            for k in range(STEPS):
                if fast and 0 <= k - 1 < NC:
                    turned_low(f_xnt, k - 1, f_turns[k - 1])
                if k + 1 < NC:
                    output.scale(dve, k + 1)
                if nxt and k == 2:
                    dve.wait_ge(ones_set, 1)
                if k < NC:
                    residual("o", k, out_bias, o_added)
                if nxt and 0 <= k - 2 < NC:
                    turned_low(q_xnt, k - 2, q_turns[k - 2])
                if k < NC:
                    f_norm.vector(dve, k, k, k and (lambda: banks.wait_full(dve, f_turns[k - 1][-1])))
                if k == 0:
                    output.reciprocals(dve, 1)
                if fast and k + 1 < NC:
                    output_low(k + 1)
                if nxt and k == 0:
                    for kc in range(KC):
                        dve.wait_ge(w_high_ready, kc + 1)
                        dve.tensor_tensor(w_qkv[1][:, kc, :], w_whole[kc], w_qkv[0][:, kc, :].bitcast(F32),
                                          ALU.subtract).then_inc(w_split, 1)
                c = k - 1
                if 0 <= c < NC:
                    residual("f", c, w["bias"], f_added)
                    if nxt:
                        q_norm.vector(dve, c, c, c and (lambda: banks.wait_full(dve, q_turns[c - 1][-1])))
                c = k - 2
                if nxt and 0 <= c < NC:
                    for i in range(PT):
                        less_high(c, i)
                        if i:
                            low(c, i - 1)
                    low(c, PT - 1)
                    for t in range(TPC):
                        value(c, t)


def build(nc, ins, out):
    env = {
        "x": ins["L0_attn_a_hidden_states"].rearrange("b s d -> (b s) d"),
        "out": out.rearrange("b s d -> (b s) d"),
        "Wq": ins["L0_attn_a_Wq"], "Wc": ins["L0_attn_a_Wc"], "Wk": ins["L0_attn_a_Wk"],
        "Wv": ins["L0_attn_a_Wv"], "Wo": ins["L0_attn_a_Wo"],
        "w_attn": ins["L0_attn_b_w_attn"], "b_attn": ins["L0_attn_b_b_attn"],
        "w_proj": ins["L0_attn_b_w_proj"], "b_proj": ins["L0_attn_b_b_proj"],
        "lora_A": ins["L0_ffn_lora_A"], "lora_B": ins["L0_ffn_lora_B"], "W": ins["L0_ffn_W"],
        "bias": ins["L0_ffn_bias"], "lora_weights": ins["L0_ffn_lora_weights"],
        "cos": ins["cos"], "sin": ins["sin"], "rot": ins["rot"], "ones": ins["ones"], "ins": ins,
    }
    for a in "ab":
        env[f"q{a}_d"] = nc.dram_tensor(f"q{a}_parts", [3, 2 * B * D, CHUNK], BF16).ap()
        env[f"k{a}_d"] = nc.dram_tensor(f"k{a}_parts", [3, B * D, S], BF16).ap()
        env[f"v{a}_d"] = nc.dram_tensor(f"v{a}_groups", [NG * P, 8 * GH * VW], F32).ap()
        env[f"o{a}_d"] = nc.dram_tensor(f"o{a}_sums", [B * D, S], F32).ap()
        env[f"z{a}_d"] = nc.dram_tensor(f"z{a}_sums", [2, B * H, CHUNK], F32).ap()
        env[f"rz{a}_d"] = nc.dram_tensor(f"z{a}_reciprocals", [2, B * H, CHUNK], F32).ap()

    with ExitStack() as ctx:
        def sb(name, shape, dt=F32):
            return ctx.enter_context(nc.sbuf_tensor(name, shape, dt))

        env["x_sb"] = sb("x_sb", [P, TILES, D])
        env["w"] = {
            "o": sb("w_o", [P, KC, D]), "eff": sb("w_eff", [P, KC, D]), 
            "proj": sb("w_proj", [P, KC, D]), "bqk": sb("b_qk", [P, 2 * KC]), "bv": sb("b_v", [P, D]),
            "bias": sb("b_ffn", [P, D]), "bproj": sb("b_proj", [P, D]),
        }
        consts = env["consts"] = {
            "ident": sb("ident", [P, P]), "minus_half": sb("minus_half", [P, 8]),
            "ident_bf": sb("ident_bf", [P, P], BF16), "mask_qk": sb("mask_qk", [P, P], BF16),
            "mask_kq": sb("mask_kq", [P, P], BF16),
        }
        env["slot_memory"] = sb("slot_memory", [P, Slot.WORDS])
        env["o_memory"] = sb("o_memory", [P, 2 * Slot.QK_WORDS])
        v_memory = sb("v_memory", [P, Slot.V_WORDS])
        first = Slot(env["slot_memory"], SROWS + 3)
        first_b = Slot(env["o_memory"], SROWS + 6, v_memory[:, :])
        first.count_loads(nc, ctx, "first_a")
        first_b.count_loads(nc, ctx, "first_b")
        with ExitStack() as early:
            w = env["w"]
            for name, shape in (("q", [P, KC, D]), ("c", [P, KC, LATENT]), ("k", [LATENT, D]), ("v", [LATENT, D])):
                w[name] = early.enter_context(nc.sbuf_tensor(f"w_{name}", shape, F32))
            project_a(nc, env, first)
        with ExitStack() as both:
            output = Output(nc, both, "out_a", env["oa_d"], env["za_d"], env["rza_d"], env["o_memory"])
            attention(nc, "a", False, DH ** -0.5, consts, env["qa_d"], env["ka_d"], env["va_d"],
                      env["oa_d"], env["za_d"], None, ins["ones"], [], first, output,
                      [(env["w"]["o"][:, :, :], env["Wo"].rearrange("(k p) n -> p k n", p=P))], [])
            output_and_ffn(nc, env, "mid", output, [env["w"]["o"]], None, True, [env["w"]["eff"]], first_b)
        with ExitStack() as both:
            output = Output(nc, both, "out_b", env["ob_d"], env["zb_d"], env["rzb_d"])
            split = {name: [both.enter_context(nc.sbuf_tensor(f"w_{name}_{part}", [P, KC, D], F32R))
                            for part in ("high", "low")] for name in ("proj", "eff")}
            attention(nc, "b", True, 1.0 / DH, consts, env["qb_d"], env["kb_d"], env["vb_d"],
                      env["ob_d"], env["zb_d"], ins["alibi"], ins["ones"], [env["slot_memory"]], first_b, output,
                      [(env["w"]["proj"][:, :, :], env["w_proj"].rearrange("(k p) n -> p k n", p=P))],
                      [(env["w"][name], *split[name]) for name in ("proj", "eff")])
            output_and_ffn(nc, env, "fin", output, split["proj"], env["w"]["bproj"], False, w_eff=split["eff"])


def in_parts(x, dtype):
    high = x.astype(dtype)
    middle = (x - high.astype(np.float32)).astype(dtype)
    low = (x - high.astype(np.float32) - middle.astype(np.float32)).astype(dtype)
    return high, middle, low


def shape_constants():
    bf16 = np.dtype("bfloat16")
    inv_freq = (1.0 / np.float32(10000.0) ** (np.arange(0, DH, 2, dtype=np.float32) / np.float32(DH))).astype(np.float32)
    freqs = np.arange(S, dtype=np.float32)[:, None] * inv_freq
    angle = np.concatenate([freqs, freqs], axis=-1).T
    rot = np.zeros((P, P), np.float32)
    for i in range(P):
        if i % DH < DH // 2:
            rot[i + DH // 2, i] = -1.0
        else:
            rot[i - DH // 2, i] = 1.0
    key, query = np.arange(P)[:, None], np.arange(P)[None, :]
    mask_kq = np.where(key > query, NEG, 0.0).astype(np.float32)
    base = 2 ** (-2 ** (-(np.log2(H) - 3)))
    slopes = (base ** np.arange(1, H + 1, dtype=np.float32)).astype(np.float32)
    ramp = (slopes[:, None] * np.float32(DH) * np.arange(S, dtype=np.float32)[None, :]).astype(np.float32)
    parts = np.stack(in_parts(ramp, bf16), axis=1)
    alibi = parts.reshape(GPB, GH, 3, S).transpose(0, 2, 1, 3).reshape(GPB * 3, GH * S)
    return {
        "cos": np.tile(np.cos(angle), (P // DH, 1)).astype(np.float32),
        "sin": np.tile(np.sin(angle), (P // DH, 1)).astype(np.float32),
        "rot": rot,
        "ident": np.eye(P, dtype=np.float32),
        "minus_half": np.full((P, 8), -0.5, np.float32),
        "ident_bf": np.eye(P, dtype=np.float32).astype(bf16),
        "mask_kq": mask_kq.astype(bf16),
        "mask_qk": mask_kq.T.copy().astype(bf16),
        "ones": np.ones((3, GH * S), bf16),
        "alibi": np.concatenate([alibi, alibi]),
    }


NAMES = ["L0_attn_a_hidden_states", "L0_attn_a_Wq", "L0_attn_a_Wc", "L0_attn_a_Wk", "L0_attn_a_Wv",
         "L0_attn_a_Wo", "L0_attn_b_w_attn", "L0_attn_b_b_attn", "L0_attn_b_w_proj", "L0_attn_b_b_proj",
         "L0_ffn_lora_A", "L0_ffn_lora_B", "L0_ffn_W", "L0_ffn_bias", "L0_ffn_lora_weights"]


def kernel(**inputs):
    import concourse.bacc as bacc
    from concourse.bass_utils import run_bass_kernel_spmd

    nc = bacc.Bacc("TRN2", target_bir_lowering=False, num_devices=1)
    host = {name: np.ascontiguousarray(inputs[name]) for name in NAMES}
    host.update(shape_constants())
    arrays, ins = {}, {}
    for name, a in host.items():
        arrays[f"in_{name}"] = a
        ins[name] = nc.dram_tensor(f"in_{name}", a.shape, mybir.dt.from_np(a.dtype), kind="ExternalInput").ap()
    out = nc.dram_tensor("out", (B, S, D), F32, kind="ExternalOutput").ap()
    build(nc, ins, out)
    r = run_bass_kernel_spmd(nc, [arrays], core_ids=[0])
    return r.results[0]["out"]
```
